# Optimizing a Trainium2 kernel written in Bass

```python
import numpy as np
import jax
import jax.numpy as jnp

def _softmax(x, axis=-1):
    return jax.nn.softmax(x, axis=axis)

def _gelu(x):
    return jax.nn.gelu(x, approximate=True)

def _silu(x):
    return jax.nn.silu(x)

def _sigmoid(x):
    return jax.nn.sigmoid(x)

def _layernorm(x, axis=-1, eps=1e-05):
    m = jnp.mean(x, axis=axis, keepdims=True)
    v = jnp.var(x, axis=axis, keepdims=True)
    return (x - m) / jnp.sqrt(v + eps)

def _scatter_add(tgt, idx, src, axis=0):
    return tgt.at[idx].add(src)

def _segment_sum(src, seg, n):
    return jax.ops.segment_sum(src, seg, n)
kernel_name = 'mk_gnn_ffn_d1_gnn_r8_476c97'

def setup_inputs(seed: int=0):
    np.random.seed(seed)
    _w = jnp.asarray

    def _rec_inputs():
        import jax
        import jax.numpy as jnp
        _gk = jax.random.key(seed)
        x = -0.0002117 + 1 * jax.random.normal(jax.random.fold_in(_gk, 1), (1250, 512), jnp.float32)
        src = jax.random.randint(jax.random.fold_in(_gk, 2), (20000,), 0, 1250, jnp.int32)
        dst = jax.random.randint(jax.random.fold_in(_gk, 3), (20000,), 0, 1250, jnp.int32)
        _o = jnp.argsort(dst, stable=True)
        src = src[_o]
        dst = dst[_o]
        return (x, src, dst)
    x, src, dst = _rec_inputs()

    def _L0_gnn_setup():
        import jax, jax.numpy as jnp
        import numpy as np
        N, E, H, D_IN, D_PRIME = (6250, 100000, 8, 512, 64)

        def _segment_softmax(scores, seg, num_segments):
            smax = jax.ops.segment_max(scores, seg, num_segments=num_segments)
            ex = jnp.exp(scores - smax[seg])
            denom = jax.ops.segment_sum(ex, seg, num_segments=num_segments)
            return ex / denom[seg]
        key = jax.random.key(seed)
        ks = jax.random.split(key, 6)
        x = jax.random.normal(ks[0], (N, D_IN), dtype=jnp.float32)
        edge_index = jax.random.randint(ks[1], (2, E), 0, N)
        Ws = jax.random.normal(ks[2], (H, D_IN, D_PRIME), dtype=jnp.float32) * 0.05
        Wb = jax.random.normal(ks[3], (H, D_PRIME), dtype=jnp.float32) * 0.05
        a_w = jax.random.normal(ks[4], (H, 2 * D_PRIME), dtype=jnp.float32) * 0.05
        a_b = jax.random.normal(ks[5], (H,), dtype=jnp.float32) * 0.05
        return dict(x=x, edge_index=edge_index, Ws=Ws, Wb=Wb, a_w=a_w, a_b=a_b)
    _L0_gnn_all = _L0_gnn_setup()
    _L0_gnn_in = {k: v for k, v in _L0_gnn_all.items() if k in ('Ws', 'Wb', 'a_w', 'a_b')}
    del _L0_gnn_all

    def _L0_ffn_setup():
        import jax, jax.numpy as jnp
        import numpy as np
        B, N, DIM = (1, 256, 512)
        DH, H = (64, 8)
        E, FF = (8, 256)

        def _layernorm(x, g, b, eps=1e-05):
            mu = jnp.mean(x, axis=-1, keepdims=True)
            var = jnp.mean(jnp.square(x - mu), axis=-1, keepdims=True)
            return (x - mu) * jax.lax.rsqrt(var + eps) * g + b

        def _l2norm(x, eps=1e-12):
            return x / jnp.sqrt(jnp.sum(jnp.square(x), axis=-1, keepdims=True) + eps)
        key = jax.random.key(seed)
        ks = jax.random.split(key, 12)
        g = lambda k, shape: jax.random.normal(k, shape, jnp.float32) * 0.02
        return {'x': jax.random.normal(ks[0], (B, N, DIM), jnp.float32), 'ln_g': jnp.ones((DIM,), jnp.float32), 'ln_b': jnp.zeros((DIM,), jnp.float32), 'Wq': g(ks[1], (DIM, DIM)), 'Wk': g(ks[2], (DIM, DIM)), 'Wv': g(ks[3], (DIM, DIM)), 'Wo': g(ks[4], (DIM, DIM)), 'qn_g': jnp.ones((DH,), jnp.float32), 'kn_g': jnp.ones((DH,), jnp.float32), 'gate_W': g(ks[5], (DIM, E)), 'gate_b': jnp.zeros((E,), jnp.float32), 'W1': g(ks[6], (E, DIM, FF)), 'b1': jnp.zeros((E, FF), jnp.float32), 'W2': g(ks[7], (E, FF, DIM)), 'b2': jnp.zeros((E, DIM), jnp.float32)}
    _L0_ffn_all = _L0_ffn_setup()
    _L0_ffn_in = {k: v for k, v in _L0_ffn_all.items() if k in ('ln_g', 'ln_b', 'Wq', 'Wk', 'Wv', 'Wo', 'qn_g', 'kn_g', 'gate_W', 'gate_b', 'W1', 'b1', 'W2', 'b2')}
    del _L0_ffn_all
    return {'x': x, 'src': src, 'dst': dst, 'L0_gnn_Ws': _L0_gnn_in['Ws'], 'L0_gnn_Wb': _L0_gnn_in['Wb'], 'L0_gnn_a_w': _L0_gnn_in['a_w'], 'L0_gnn_a_b': _L0_gnn_in['a_b'], 'L0_ffn_ln_g': _L0_ffn_in['ln_g'], 'L0_ffn_ln_b': _L0_ffn_in['ln_b'], 'L0_ffn_Wq': _L0_ffn_in['Wq'], 'L0_ffn_Wk': _L0_ffn_in['Wk'], 'L0_ffn_Wv': _L0_ffn_in['Wv'], 'L0_ffn_Wo': _L0_ffn_in['Wo'], 'L0_ffn_qn_g': _L0_ffn_in['qn_g'], 'L0_ffn_kn_g': _L0_ffn_in['kn_g'], 'L0_ffn_gate_W': _L0_ffn_in['gate_W'], 'L0_ffn_gate_b': _L0_ffn_in['gate_b'], 'L0_ffn_W1': _L0_ffn_in['W1'], 'L0_ffn_b1': _L0_ffn_in['b1'], 'L0_ffn_W2': _L0_ffn_in['W2'], 'L0_ffn_b2': _L0_ffn_in['b2']}

def reference(x, src, dst, L0_gnn_Ws, L0_gnn_Wb, L0_gnn_a_w, L0_gnn_a_b, L0_ffn_ln_g, L0_ffn_ln_b, L0_ffn_Wq, L0_ffn_Wk, L0_ffn_Wv, L0_ffn_Wo, L0_ffn_qn_g, L0_ffn_kn_g, L0_ffn_gate_W, L0_ffn_gate_b, L0_ffn_W1, L0_ffn_b1, L0_ffn_W2, L0_ffn_b2):
    import jax
    import jax.numpy as jnp

    def _L0_gnn_ref(x, edge_index, Ws, Wb, a_w, a_b):
        import jax, jax.numpy as jnp
        import numpy as np
        N, E, H, D_IN, D_PRIME = (6250, 100000, 8, 512, 64)

        def _segment_softmax(scores, seg, num_segments):
            smax = jax.ops.segment_max(scores, seg, num_segments=num_segments)
            ex = jnp.exp(scores - smax[seg])
            denom = jax.ops.segment_sum(ex, seg, num_segments=num_segments)
            return ex / denom[seg]
        v_src, v_tgt = (edge_index[0], edge_index[1])
        n = x.shape[0]
        outs = []
        for h in range(Ws.shape[0]):
            Wx = x @ Ws[h] + Wb[h]
            d = Wx.shape[-1]
            s = Wx[v_tgt] @ a_w[h, :d] + Wx[v_src] @ a_w[h, d:] + a_b[h]
            s = jax.nn.leaky_relu(s, negative_slope=0.2)
            alpha = _segment_softmax(s, v_tgt, n)
            outs.append(jax.ops.segment_sum(alpha[:, None] * Wx[v_src], v_tgt, num_segments=n))
        return jnp.stack(outs, axis=1).reshape(n, -1)

    def _L0_ffn_ref(x, ln_g, ln_b, Wq, Wk, Wv, Wo, qn_g, kn_g, gate_W, gate_b, W1, b1, W2, b2):
        import jax, jax.numpy as jnp
        import numpy as np
        B, N, DIM = (1, 256, 512)
        DH, H = (64, 8)
        E, FF = (8, 256)

        def _layernorm(x, g, b, eps=1e-05):
            mu = jnp.mean(x, axis=-1, keepdims=True)
            var = jnp.mean(jnp.square(x - mu), axis=-1, keepdims=True)
            return (x - mu) * jax.lax.rsqrt(var + eps) * g + b

        def _l2norm(x, eps=1e-12):
            return x / jnp.sqrt(jnp.sum(jnp.square(x), axis=-1, keepdims=True) + eps)
        b, n, d = x.shape
        dh = qn_g.shape[0]
        h = d // dh
        hx = _layernorm(x, ln_g, ln_b)
        q = (hx @ Wq).reshape(b, n, h, dh).transpose(0, 2, 1, 3)
        k = (hx @ Wk).reshape(b, n, h, dh).transpose(0, 2, 1, 3)
        v = (hx @ Wv).reshape(b, n, h, dh).transpose(0, 2, 1, 3)
        scale = jnp.sqrt(jnp.float32(dh))
        q = _l2norm(q) * scale * qn_g
        k = _l2norm(k) * scale * kn_g
        scores = jnp.einsum('bhqd,bhkd->bhqk', q, k) * dh ** (-0.5)
        causal = jnp.tril(jnp.ones((n, n), bool))
        scores = jnp.where(causal, scores, jnp.finfo(scores.dtype).min)
        attn = jax.nn.softmax(scores, axis=-1)
        o = jnp.einsum('bhqk,bhkd->bhqd', attn, v)
        y = o.transpose(0, 2, 1, 3).reshape(b, n, d) @ Wo
        gate = jax.nn.softmax(y @ gate_W + gate_b, axis=-1)
        hid = jax.nn.gelu(jnp.einsum('bnd,edf->bnef', y, W1) + b1)
        eo = jnp.einsum('bnef,efd->bned', hid, W2) + b2
        out = jnp.einsum('bned,bne->bnd', eo, gate)
        return out
    edge_index = jnp.stack([src, dst])
    x = x + _L0_gnn_ref(_layernorm(x, axis=-1), edge_index, L0_gnn_Ws, L0_gnn_Wb, L0_gnn_a_w, L0_gnn_a_b)
    x = x + _L0_ffn_ref(_layernorm(x, axis=-1)[None], L0_ffn_ln_g, L0_ffn_ln_b, L0_ffn_Wq, L0_ffn_Wk, L0_ffn_Wv, L0_ffn_Wo, L0_ffn_qn_g, L0_ffn_kn_g, L0_ffn_gate_W, L0_ffn_gate_b, L0_ffn_W1, L0_ffn_b1, L0_ffn_W2, L0_ffn_b2)[0]
    return x

_drawn_inputs = setup_inputs


def setup_inputs(seed=0):
    import zlib

    import numpy as np

    out = dict(_drawn_inputs(seed))
    spreads = {'L0_ffn_ln_g': (1.0, 0.6),
     'L0_ffn_ln_b': (0.0, 0.8),
     'L0_ffn_qn_g': (1.0, 0.6),
     'L0_ffn_kn_g': (1.0, 0.6),
     'L0_ffn_gate_b': (0.0, 0.8),
     'L0_ffn_b1': (0.0, 2.0),
     'L0_ffn_b2': (0.0, 0.8)}
    factors = {'L0_gnn_a_b': 8.0,
     'L0_ffn_Wq': 8.0,
     'L0_ffn_Wk': 8.0,
     'L0_ffn_Wv': 8.0,
     'L0_ffn_Wo': 8.0,
     'L0_ffn_gate_W': 8.0,
     'L0_ffn_W1': 8.0,
     'L0_ffn_W2': 8.0}
    for name, (base, spread) in spreads.items():
        noise = np.random.default_rng([zlib.crc32(name.encode()), seed]).standard_normal(out[name].shape)
        drawn = base * np.exp(spread * noise) if base else spread * noise
        out[name] = jnp.asarray(drawn.astype(out[name].dtype))
    for name, factor in factors.items():
        out[name] = (out[name] * factor).astype(out[name].dtype)
    return out
```

```python
import concourse.bass as bass
from concourse import mybir
from contextlib import ExitStack

F32 = mybir.dt.float32
F32R = mybir.dt.float32r
I32 = mybir.dt.int32
BF16 = mybir.dt.bfloat16
ALU = mybir.AluOpType
ACT = mybir.ActivationFunctionType
X_AXIS = mybir.AxisListType.X
XY_AXES = mybir.AxisListType.XY
RMAX = bass.bass_isa.ReduceOp.max

P = 128
N = 1250
NT = -(-N // P)
NP = NT * P
D = 512
KC = D // P
H = 8
DH = D // H
E = 20000
TG = 13
GE = TG * P
NG = E // GE
TAIL = E - NG * GE
ROW = D + H
WR = 24
WROWS = NP + P
TINY = 1e-37
EPS = 1e-5
MASKED = -1e30


def peeled(eng, count, body):
    body(0, True)
    with eng.Fori(1, count) as j:
        body(j, False)


class Chain:

    def __init__(self, eng, sem, base=0):
        self.eng, self.sem, self.base, self.n = eng, sem, base, 0

    def __call__(self, ins):
        self.n += 1
        ins.then_inc(self.sem, 1)
        self.eng.wait_ge(self.sem, self.base + self.n)


def build(nc, x, src, dst, Ws, Wb, a_w, a_b, ln_g, ln_b, Wq, Wk, Wv, Wo, qn_g, kn_g,
          gate_W, gate_b, W1, b1, W2, b2, out):
    ctx = ExitStack()
    with ctx:
        def sb(name, shape, dt=F32):
            return ctx.enter_context(nc.sbuf_tensor(name, shape, dt))

        def sem(name):
            return ctx.enter_context(nc.semaphore(name))

        psum = ctx.enter_context(nc.psum_tensor("psum", [P, 8 * 512], F32))
        bank = [psum[:, i * 512:(i + 1) * 512] for i in range(8)]
        source_table = nc.dram_tensor("source_table", [NP, ROW], F32, kind="Internal").ap()
        window_table = nc.dram_tensor("window_table", [WROWS, WR], F32, kind="Internal").ap()
        node_numbers = nc.dram_tensor("node_numbers", [1, WROWS], F32, kind="Internal").ap()
        sums = nc.dram_tensor("sums", [WROWS, ROW], F32, kind="Internal").ap()

        X = sb("X", [P, NT, D])
        ident = sb("ident", [P, P])
        bases = sb("bases", [1, NT * (NG + 1)], I32)
        passes = sb("passes", [1, 1], I32)
        added = sem("added")

        project_nodes(nc, sem, bank, X, ident, bases, passes, source_table, window_table,
                      node_numbers, sums, added, x, dst, Ws, Wb, a_w, a_b)
        sum_edges(nc, sem, bank, ident, bases, passes, source_table, window_table, node_numbers,
                  sums, added, src, dst)
        S = sb("node_sums", [P, NT, ROW])
        O = S[:, :, 0:D]
        with ExitStack() as heads:
            QT, KT = (heads.enter_context(nc.sbuf_tensor(name, [P, KC, NP], F32)) for name in ("QT", "KT"))
            V = heads.enter_context(nc.sbuf_tensor("V", [P, NT, H, DH + 2], F32))
            project_heads(nc, sem, bank, X, S, ident, sums, QT, KT, V, ln_g, ln_b, Wq, Wk, Wv, qn_g, kn_g)
            attend(nc, sem, psum, ident, QT, KT, V, O)

        F = W1.shape[2]
        yT = [sb(name, [P, KC, NP], F32R) for name in ("yT_hi", "yT_lo")]
        logits = sb("logits", [H, NP])
        raw = [[sb(f"expert_raw{w}{b}", [P, c, n]) for b in range(2)] for w, (c, n) in enumerate(((KC, F), (F // P, D)))]
        parts = [[[sb(f"expert_{part}{w}", [P, c, n], F32R) for part in ("first_hi", "first_lo")]]
                 for w, (c, n) in enumerate(((KC, F), (F // P, D)))]
        weights_loaded = [sem(f"expert_loaded{b}") for b in range(2)]
        weights_hi, weights_lo = sem("expert_weights_hi"), sem("expert_weights_lo")
        combine_heads(nc, sem, bank, ident, O, yT, logits, raw, parts, weights_loaded, weights_hi, weights_lo,
                      Wo, gate_W, gate_b, W1, W2)
        run_experts(nc, sem, bank, ident, X, yT, logits, raw, parts, weights_loaded, weights_hi, weights_lo,
                    W1, b1, W2, b2)
        store_out(nc, sem, X, out)


def split(nc_eng, exact_eng, hi, lo, value, step):
    step(nc_eng.tensor_copy(hi, value))
    step(exact_eng.tensor_tensor(lo, value, hi.bitcast(F32), ALU.subtract))


def project_nodes(nc, sem, bank, X, ident, bases, passes, source_table, window_table, node_numbers,
                  sums, added, x, dst, Ws, Wb, a_w, a_b):
    ctx = ExitStack()
    with ctx:
        def sb(name, shape, dt=F32):
            return ctx.enter_context(nc.sbuf_tensor(name, shape, dt))

        W = sb("W", [P, KC, D])
        W_hi, W_lo = sb("W_hi", [P, KC, D], F32R), sb("W_lo", [P, KC, D], F32R)
        Wa = sb("Wa", [P, KC, 2 * H])
        Wa_hi, Wa_lo = sb("Wa_hi", [P, KC, 2 * H], F32R), sb("Wa_lo", [P, KC, 2 * H], F32R)
        a_row = sb("a_row", [P, H, 2 * DH])
        ab_row = sb("ab_row", [P, H])
        Wb_row = sb("Wb_row", [P, D])
        score_bias = sb("score_bias", [P, 2 * H])
        product = sb("product", [P, KC * D])
        stats = sb("stats", [P, NT, 6])
        mean_var = sb("mean_var", [P, NT, 2])
        rstd = sb("rstd", [P, NT])
        eps = sb("eps", [P, 1])
        Hn = [sb(f"Hn{b}", [P, D]) for b in range(2)]
        HT_hi = [sb(f"HT_hi{b}", [P, KC, P], F32R) for b in range(2)]
        HT_lo = [sb(f"HT_lo{b}", [P, KC, P], F32R) for b in range(2)]
        row = [sb(f"row{b}", [P, ROW]) for b in range(2)]
        scores = sb("scores", [P, NT, 2 * H])
        bound = sb("bound", [P, H])
        bound_all = sb("bound_all", [P, H])
        window = sb("window", [P, NT + 1, WR])
        zeros = sb("zeros", [P, NT * ROW])
        numbers = sb("numbers", [1, WROWS])
        dst_all = sb("dst_all", [P, NG, TG], I32)
        dst_tail = sb("dst_tail", [TAIL, 1], I32)
        first = sb("first", [P, NG + 1], I32)
        off = sb("off", [P, NG, TG])
        off_tail = sb("off_tail", [TAIL, 1])
        outside = sb("outside", [P, 2])
        outside_all = sb("outside_all", [P, 2])
        bad = sb("bad", [1, 4])
        base_f = sb("base_f", [1, NT, NG + 1])
        first_f = sb("first_f", [1, NG + 1])

        x_loaded = sem("x_loaded")
        w_loaded = sem("w_loaded")
        dst_loaded = sem("dst_loaded")
        pad_cleared = sem("pad_cleared")
        ident_zeroed = sem("ident_zeroed")
        ident_ready = sem("ident_ready")
        numbers_ready = sem("numbers_ready")
        zeros_ready = sem("zeros_ready")
        var_ready = sem("var_ready")
        root_ready = sem("root_ready")
        weights_ready = sem("weights_ready")
        normed = sem("normed")
        transposed = sem("transposed")
        hi_ready = sem("hi_ready")
        lo_ready = sem("lo_ready")
        projected = sem("projected")
        row_ready = sem("row_ready")
        row_stored = [sem(f"row_stored{b}") for b in range(2)]
        own = sem("project_vector_own")
        bound_ready = sem("bound_ready")
        bound_reduced = sem("bound_reduced")
        outside_ready = sem("outside_ready")
        outside_reduced = sem("outside_reduced")
        window_ready = sem("window_ready")
        tables_stored = sem("tables_stored")

        LAST = N - (NT - 1) * P
        psT = [bank[0], bank[1]]
        psW = [bank[2], bank[3]]
        psS = [bank[4], bank[5]]
        W_LOADS = H + 3

        def flag_windows(dve, step):
            dve.wait_ge(dst_loaded, 16 * 4)
            step(nc.vector.tensor_tensor(off[:, :, :], dst_all[:, :, :],
                                         first[:, 0:NG].rearrange("p (g o) -> p g o", o=1).broadcast_to([P, NG, TG]),
                                         ALU.subtract))
            step(nc.vector.tensor_tensor(off_tail[:, :], dst_tail[:, :], first[0:TAIL, NG:NG + 1], ALU.subtract))
            step(nc.vector.tensor_reduce(outside[:, 0:1], off[:, :, :], XY_AXES, ALU.max))
            step(nc.vector.tensor_reduce(outside[:, 1:2], off[:, :, :], XY_AXES, ALU.min))
            step(nc.vector.tensor_tensor(outside[0:TAIL, 0:1], outside[0:TAIL, 0:1], off_tail[:, :], ALU.max))
            step(nc.vector.tensor_tensor(outside[0:TAIL, 1:2], outside[0:TAIL, 1:2], off_tail[:, :], ALU.min))
            nc.vector.tensor_scalar(outside[:, 1:2], outside[:, 1:2], -1.0, None, ALU.mult).then_inc(outside_ready, 1)
            dve.wait_ge(outside_reduced, 1)
            step(nc.vector.tensor_scalar(bad[:, 0:1], outside_all[0:1, 0:1], float(P - 1), None, ALU.is_gt))
            step(nc.vector.tensor_scalar(bad[:, 1:2], outside_all[0:1, 1:2], 0.0, None, ALU.is_gt))
            step(nc.vector.tensor_tensor(bad[:, 2:3], bad[:, 0:1], bad[:, 1:2], ALU.max))
            step(nc.vector.tensor_scalar(passes[:, :], bad[:, 2:3], float(NT - 1), 1.0, ALU.mult, ALU.add))
            step(nc.vector.tensor_scalar(bad[:, 3:4], bad[:, 2:3], -1.0, 1.0, ALU.mult, ALU.add))
            step(nc.vector.tensor_scalar(first_f[:, :], first[0:1, :], bad[:, 3:4], None, ALU.mult))
            for t in range(NT):
                step(nc.vector.tensor_scalar(base_f[:, t, :], bad[:, 2:3].broadcast_to([1, NG + 1]), float(t * P), None, ALU.mult))
                step(nc.vector.tensor_tensor(base_f[:, t, :], base_f[:, t, :], first_f[:, :], ALU.add))
            step(nc.vector.tensor_copy(bases[:, :], base_f[:, :, :].rearrange("p t g -> p (t g)")))

        with nc.Block() as block:
            @block.sync
            def _(sp):
                sp.wait_ge(pad_cleared, 1)
                sp.dma_start(X[:, 0:NT - 1, :],
                             x[0:(NT - 1) * P, :].rearrange("(t p) d -> p t d", p=P)).then_inc(x_loaded, 16)
                sp.dma_start(X[0:LAST, NT - 1, :], x[(NT - 1) * P:N, :]).then_inc(x_loaded, 16)
                for h in range(H):
                    sp.dma_start(W[:, :, h * DH:(h + 1) * DH],
                                 Ws[h].rearrange("(c p) d -> p c d", p=P)).then_inc(w_loaded, 16)
                sp.dma_start(a_row[:, :, :], a_w.partition_broadcast(P)).then_inc(w_loaded, 16)
                sp.dma_start(ab_row[:, :], a_b.partition_broadcast(P)).then_inc(w_loaded, 16)
                sp.dma_start(Wb_row[:, :], Wb.rearrange("h d -> (h d)").partition_broadcast(P)).then_inc(w_loaded, 16)
                sp.dma_start(dst_all[:, :, :],
                             dst[0:NG * GE].rearrange("(g p t) -> p g t", p=P, t=TG)).then_inc(dst_loaded, 16)
                sp.dma_start(dst_tail[:, :], dst[NG * GE:E].rearrange("(p o) -> p o", o=1)).then_inc(dst_loaded, 16)
                sp.dma_start(first[:, 0:NG],
                             dst[0:NG * GE].rearrange("(g e) -> g e", e=GE)[:, 0].partition_broadcast(P),
                             allow_slow_non_contiguous=True).then_inc(dst_loaded, 16)
                sp.dma_start(first[:, NG:NG + 1],
                             dst[NG * GE:NG * GE + 1].partition_broadcast(P)).then_inc(dst_loaded, 16)
                sp.wait_ge(numbers_ready, 1)
                sp.dma_start(node_numbers, numbers[:, :]).then_inc(tables_stored, 16)
                with sp.Fori(0, NT // 2) as j:
                    for b in range(2):
                        sp.wait_ge(row_ready, 2 * j + b + 1)
                        sp.dma_start(source_table[bass.ds((2 * j + b) * P, P), :],
                                     row[b][:, :]).then_inc(row_stored[b], 16)
                sp.wait_ge(window_ready, 1)
                sp.dma_start(window_table.rearrange("(t p) r -> p t r", p=P), window[:, :, :]).then_inc(tables_stored, 16)
                sp.wait_ge(tables_stored, 32)
                for b in range(2):
                    sp.wait_ge(row_stored[b], 16 * (NT // 2))

            @block.gpsimd
            def _(pool):
                nc.gpsimd.memset(ident[:, :], 0.0).then_inc(ident_zeroed, 1)
                pool.wait_ge(ident_zeroed, 1)
                nc.gpsimd.affine_select(out=ident[:, :], in_=ident[:, :], compare_op=ALU.not_equal, fill=1.0,
                                        base=0, pattern=[[-1, P]], channel_multiplier=1).then_inc(ident_ready, 1)
                nc.gpsimd.memset(zeros[:, :], 0.0).then_inc(zeros_ready, 1)
                pool.wait_ge(zeros_ready, 1)
                for t0, t1 in ((0, NT), (NT, NT + 1)):
                    nc.gpsimd.dma_start(sums[t0 * P:t1 * P, :].rearrange("(t p) r -> p t r", p=P),
                                        zeros[:, 0:(t1 - t0) * ROW].rearrange("p (t r) -> p t r", r=ROW)).then_inc(added, 16)
                nc.gpsimd.iota(numbers[:, :], [[1, WROWS]], 0, 0,
                               allow_small_or_imprecise_dtypes=True).then_inc(numbers_ready, 1)
                nc.gpsimd.iota(window[:, :, 2 * H:2 * H + 1], [[P, NT + 1]], 0, 1,
                               allow_small_or_imprecise_dtypes=True).then_inc(numbers_ready, 1)
                pool.wait_ge(outside_ready, 1)
                nc.gpsimd.partition_all_reduce(outside_all[:, :], outside[:, :], P, RMAX).then_inc(outside_reduced, 1)
                pool.wait_ge(bound_ready, 1)
                nc.gpsimd.partition_all_reduce(bound_all[:, :], bound[:, :], P, RMAX).then_inc(bound_reduced, 1)
                pool.wait_ge(added, 32)

            @block.scalar
            def _(act):
                act.wait_ge(var_ready, 2)
                nc.scalar.activation(rstd[:, :], mean_var[:, :, 1], ACT.Sqrt, bias=eps[:, 0:1]).then_inc(root_ready, 1)

                def pair(j, first):
                    for b in range(2):
                        t = 2 * j + b
                        if not first:
                            act.wait_ge(projected, t - 1)
                        act.wait_ge(transposed, t + 1)
                        nc.scalar.activation(HT_hi[b][:, :, :], psT[b][:, :].rearrange("p (c n) -> p c n", c=KC),
                                             ACT.Copy).then_inc(hi_ready, 1)

                peeled(act, NT // 2, pair)

            @block.vector
            def _(dve):
                step = Chain(dve, own)
                nc.vector.memset(X[:, NT - 1, :], 0.0).then_inc(pad_cleared, 1)
                nc.vector.memset(eps[:, :], EPS).then_inc(var_ready, 1)
                step(nc.vector.memset(window[:, :, 2 * H + 1:WR], 0.0))
                step(nc.vector.memset(window[:, :, 0:2 * H], 0.0))
                dve.wait_ge(x_loaded, 32)
                for t in range(NT):
                    last = nc.vector.bn_stats(stats[:, t, :], X[:, t, :])
                step(last)
                for t in range(NT):
                    last = nc.vector.bn_aggr(mean_var[:, t, :], stats[:, t, :])
                last.then_inc(var_ready, 1)
                dve.wait_ge(w_loaded, 16 * W_LOADS)
                step(nc.vector.tensor_copy(W_hi[:, :, :], W[:, :, :]))
                step(nc.vector.tensor_tensor(W_lo[:, :, :], W[:, :, :], W_hi[:, :, :].bitcast(F32), ALU.subtract))
                Wv4 = W[:, :, :].rearrange("p c (h d) -> p c h d", h=H)
                pr = product[:, :].rearrange("p (c h d) -> p c h d", c=KC, h=H)
                for half in range(2):
                    part = a_row[:, :, half * DH:(half + 1) * DH]
                    for c in range(KC):
                        last = nc.vector.tensor_tensor(pr[:, c], Wv4[:, c], part, ALU.mult)
                    step(last)
                    step(nc.vector.tensor_reduce(Wa[:, :, half * H:(half + 1) * H], pr, X_AXIS, ALU.add))
                    step(nc.vector.tensor_tensor(pr[:, 0], Wb_row[:, :].rearrange("p (h d) -> p h d", h=H), part, ALU.mult))
                    step(nc.vector.tensor_reduce(score_bias[:, half * H:(half + 1) * H], pr[:, 0], X_AXIS, ALU.add))
                step(nc.vector.tensor_tensor(score_bias[:, 0:H], score_bias[:, 0:H], ab_row[:, :], ALU.add))
                step(nc.vector.tensor_copy(Wa_hi[:, :, :], Wa[:, :, :]))
                nc.vector.tensor_tensor(Wa_lo[:, :, :], Wa[:, :, :], Wa_hi[:, :, :].bitcast(F32),
                                        ALU.subtract).then_inc(weights_ready, 1)
                dve.wait_ge(root_ready, 1)
                step(nc.vector.reciprocal(rstd[:, :], rstd[:, :]))
                flag_windows(dve, step)

                def pair(j, first):
                    for b in range(2):
                        t = 2 * j + b
                        nc.vector.tensor_scalar(Hn[b][:, :], X[:, bass.ds(t, 1), :].rearrange("p o d -> p (o d)"),
                                                mean_var[:, bass.ds(t, 1), 0], rstd[:, bass.ds(t, 1)],
                                                ALU.subtract, ALU.mult).then_inc(normed, 1)
                    for b in range(2):
                        t = 2 * j + b
                        dve.wait_ge(hi_ready, t + 1)
                        nc.vector.tensor_tensor(HT_lo[b][:, :, :], psT[b][:, :].rearrange("p (c n) -> p c n", c=KC),
                                                HT_hi[b][:, :, :].bitcast(F32), ALU.subtract).then_inc(lo_ready, 1)
                    for b in range(2):
                        t = 2 * j + b
                        dve.wait_ge(projected, t + 1)
                        if not first:
                            dve.wait_ge(row_stored[b], 16 * j)
                        nc.vector.tensor_tensor(row[b][:, 0:D], psW[b][:, :], Wb_row[:, :], ALU.add)
                        nc.vector.tensor_tensor(row[b][:, D:ROW], psS[b][:, H:2 * H], score_bias[:, H:2 * H], ALU.add)
                        nc.vector.tensor_tensor(scores[:, bass.ds(t, 1), :].rearrange("p o s -> p (o s)"),
                                                psS[b][:, 0:2 * H], score_bias[:, :], ALU.add).then_inc(row_ready, 1)

                peeled(dve, NT // 2, pair)
                dve.wait_ge(row_ready, NT)
                step(nc.vector.tensor_reduce(bound[:, :], scores[:, :, H:2 * H].rearrange("p t h -> p h t"), X_AXIS, ALU.max))
                nc.vector.tensor_copy(bound[:, :], bound[:, :]).then_inc(bound_ready, 1)
                dve.wait_ge(bound_reduced, 1)
                step(nc.vector.tensor_copy(window[:, 0:NT, 0:H], scores[:, :, 0:H]))
                for t in range(NT):
                    last = nc.vector.tensor_tensor(window[:, t, H:2 * H], scores[:, t, 0:H], bound_all[:, :], ALU.add)
                step(last)
                dve.wait_ge(numbers_ready, 2)
                for t in range(NT):
                    last = nc.vector.scalar_tensor_tensor(window[:, t, H:2 * H], window[:, t, H:2 * H], 0.2,
                                                          window[:, t, H:2 * H], ALU.mult, ALU.max)
                last.then_inc(window_ready, 1)

            @block.tensor
            def _(pe):
                pe.wait_ge(ident_ready, 1)

                def pair(j, first):
                    for b in range(2):
                        t = 2 * j + b
                        pe.wait_ge(normed, t + 1)
                        for c in range(KC):
                            last = nc.tensor.transpose(psT[b][:, c * P:(c + 1) * P], Hn[b][:, c * P:(c + 1) * P], ident[:, :])
                        last.then_inc(transposed, 1)
                    if first:
                        pe.wait_ge(weights_ready, 1)
                    for b in range(2):
                        t = 2 * j + b
                        pe.wait_ge(lo_ready, t + 1)
                        if not first:
                            pe.wait_ge(row_ready, t - 1)
                        pairs = [(HT_hi, W_hi, Wa_hi), (HT_hi, W_lo, Wa_lo), (HT_lo, W_hi, Wa_hi)]
                        for n, (h, w, wa) in enumerate(pairs):
                            for c in range(KC):
                                nc.tensor.matmul(psW[b][:, :], h[b][:, c, :], w[:, c, :],
                                                 start=(n == 0 and c == 0), stop=(n == 2 and c == KC - 1))
                        for n, (h, w, wa) in enumerate(pairs):
                            for c in range(KC):
                                last = nc.tensor.matmul(psS[b][:, 0:2 * H], h[b][:, c, :], wa[:, c, :],
                                                        start=(n == 0 and c == 0), stop=(n == 2 and c == KC - 1))
                        last.then_inc(projected, 1)

                peeled(pe, NT // 2, pair)


def sum_edges(nc, sem, bank, ident, bases, passes, source_table, window_table, node_numbers, sums,
              added, src, dst):
    ctx = ExitStack()
    with ctx:
        def sb(name, shape, dt=F32):
            return ctx.enter_context(nc.sbuf_tensor(name, shape, dt))

        G = [sb(f"G{b}", [P, TG, ROW]) for b in range(2)]
        target = [sb(f"target{b}", [P, TG], I32) for b in range(2)]
        source = [sb(f"source{b}", [P, TG], I32) for b in range(2)]
        target_f = [sb(f"target_f{b}", [P, TG]) for b in range(2)]
        window = [sb(f"window_rows{b}", [P, WR]) for b in range(2)]
        nodes = [sb(f"nodes{b}", [P, P]) for b in range(2)]
        onehot = [sb(f"onehot{b}", [P, TG, P]) for b in range(2)]
        onehot_T = [sb(f"onehot_T{b}", [P, TG * P]) for b in range(2)]
        targets_row = [sb(f"targets_row{b}", [P, GE], I32) for b in range(2)]
        logit = [sb(f"logit{b}", [P, TG, H]) for b in range(2)]
        shifted = [sb(f"shifted{b}", [P, TG, H]) for b in range(2)]
        weight = [sb(f"weight{b}", [P, TG, H]) for b in range(2)]
        flush = [sb(f"flush{b}", [P, ROW]) for b in range(2)]
        psS = [bank[2], bank[3]]
        psN = [bank[4], bank[5]]
        psD = [bank[6], bank[7]]

        loaded = [sem(f"loaded{b}") for b in range(2)]
        gathered = [sem(f"gathered{b}") for b in range(2)]
        onehots_ready = [sem(f"onehots_ready{b}") for b in range(2)]
        gate = sem("gate")
        scored = sem("scored")
        logits_ready = [sem(f"logits_ready{b}") for b in range(2)]
        weights_ready = [sem(f"edge_weights_ready{b}") for b in range(2)]
        weighted = [sem(f"weighted{b}") for b in range(2)]
        summed = [sem(f"summed{b}") for b in range(2)]
        flushed = [sem(f"flushed{b}") for b in range(2)]
        own_early = sem("edges_vector_own_early")
        own_late = sem("edges_vector_own_late")

        PAIRS = NG // 2
        LOADS = 5 * 16
        WEAVE = 4
        WEAVE_PE = 9

        def uses(b, p, g):
            return p * (PAIRS + (b == 0)) + g

        def tiles(b, p, g):
            return p * (PAIRS * TG + (b == 0)) + g * TG

        def groups(b, p, g):
            return p * (NG + 1) + 2 * g + b

        def in_turn(eng, start_pass, early, slot):
            rounds = eng.value_load(passes[0:1, 0:1], min_val=1, max_val=NT)
            with eng.Fori(0, rounds) as p:
                start_pass(p)
                early(p, 0, 0, TG, P)
                with eng.Fori(0, PAIRS - 1) as g:
                    slot((p, 0, g, TG, P), (p, 1, g, TG, P))
                    slot((p, 1, g, TG, P), (p, 0, g + 1, TG, P))
                g = PAIRS - 1
                slot((p, 0, g, TG, P), (p, 1, g, TG, P))
                slot((p, 1, g, TG, P), (p, 0, g + 1, 1, TAIL))
                slot((p, 0, g + 1, 1, TAIL), None)

        with nc.Block() as block:
            @block.sync
            def _(sp):
                def load(p, b, g, nt, ne):
                    base = sp.value_load(bases[0:1, bass.ds(groups(b, p, g), 1)], min_val=0, max_val=NP - 1)
                    sp.wait_ge(logits_ready[b], uses(b, p, g) + 1)
                    at = (2 * g + b) * GE
                    sp.dma_start(target[b][0:ne, 0:nt],
                                 dst[bass.ds(at, ne * nt)].rearrange("(p t) -> p t", t=nt)).then_inc(loaded[b], 16)
                    sp.dma_start(targets_row[b][:, 0:ne * nt],
                                 dst[bass.ds(at, ne * nt)].partition_broadcast(P)).then_inc(loaded[b], 16)
                    sp.dma_start(source[b][0:ne, 0:nt],
                                 src[bass.ds(at, ne * nt)].rearrange("(p t) -> p t", t=nt)).then_inc(loaded[b], 16)
                    sp.dma_start(window[b][:, :], window_table[bass.ds(base, P), :]).then_inc(loaded[b], 16)
                    sp.dma_start(nodes[b][:, :],
                                 node_numbers[0, bass.ds(base, P)].partition_broadcast(P)).then_inc(loaded[b], 16)

                in_turn(sp, lambda p: None, load, lambda late, early: load(*early) if early else None)

            @block.gpsimd
            def _(pool):
                def gather(p, b, g, nt, ne):
                    pool.wait_ge(loaded[b], LOADS * (uses(b, p, g) + 1))
                    for t in range(nt):
                        pool.wait_ge(summed[b], tiles(b, p, g) + t + 1)
                        pool.sem_inc(gate, 1)
                        nc.gpsimd.indirect_dma_start(
                            G[b][0:ne, t, :], None, source_table,
                            bass.IndirectOffsetOnAxis(ap=source[b][0:ne, t:t + 1], axis=0)).then_inc(gathered[b], 16)

                def add(p, b, g):
                    base = pool.value_load(bases[0:1, bass.ds(groups(b, p, g), 1)], min_val=0, max_val=NP - 1)
                    pool.wait_ge(flushed[b], uses(b, p, g) + 2)
                    pool.wait_ge(added, 16 * (groups(b, p, g) + 2))
                    nc.gpsimd.dma_start(sums[bass.ds(base, P), :], flush[b][:, :],
                                        accum_op=ALU.add).then_inc(added, 16)

                rounds = pool.value_load(passes[0:1, 0:1], min_val=1, max_val=NT)
                with pool.Fori(0, rounds) as p:
                    for b in range(2):
                        pool.wait_ge(summed[b], tiles(b, p, 0) + TG)
                        gather(p, b, 0, TG, P)
                    with pool.Fori(1, PAIRS) as g:
                        for b in range(2):
                            gather(p, b, g, TG, P)
                            add(p, b, g - 1)
                    gather(p, 0, PAIRS, 1, TAIL)
                    for b in range(2):
                        add(p, b, PAIRS - 1)
                    add(p, 0, PAIRS)
                pool.wait_ge(added, 16 * (rounds * (NG + 1) + 2))

            @block.vector
            def _(dve):
                for b in range(2):
                    dve.sem_inc(logits_ready[b], 1)

                def early(p, b, g, nt, ne):
                    dve.wait_ge(loaded[b], LOADS * (uses(b, p, g) + 1))
                    dve.wait_ge(summed[b], tiles(b, p, g) + TG)
                    step = Chain(dve, own_early, groups(b, p, g))
                    step(nc.vector.tensor_copy(target_f[b][0:ne, 0:nt], target[b][0:ne, 0:nt]))
                    nc.vector.tensor_tensor(
                        onehot[b][0:ne, 0:nt, :],
                        nodes[b][0:ne, :].rearrange("p (o n) -> p o n", o=1).broadcast_to([ne, nt, P]),
                        target_f[b][0:ne, 0:nt].rearrange("p (t o) -> p t o", o=1).broadcast_to([ne, nt, P]),
                        ALU.is_equal)
                    nc.vector.tensor_scalar(
                        onehot_T[b][:, 0:nt * ne].rearrange("n (t p) -> n t p", t=nt),
                        targets_row[b][:, 0:nt * ne].rearrange("n (p t) -> n t p", t=nt),
                        window[b][:, 2 * H:2 * H + 1], None, ALU.is_equal).then_inc(onehots_ready[b], 1)

                def logits(p, b, g, nt, ne):
                    dve.wait_ge(gathered[b], 16 * (tiles(b, p, g) + nt))
                    dve.wait_ge(scored, groups(b, p, g) + 1)
                    ps = psS[b][0:ne, 0:nt * 2 * H].rearrange("p (t s) -> p t s", s=2 * H)
                    z, z2 = logit[b][0:ne, 0:nt, :], shifted[b][0:ne, 0:nt, :]
                    step = Chain(dve, own_late, 3 * groups(b, p, g))
                    step(nc.vector.tensor_tensor(z, ps[:, :, 0:H], G[b][0:ne, 0:nt, D:ROW], ALU.add))
                    step(nc.vector.scalar_tensor_tensor(z2, z, 0.2, z, ALU.mult, ALU.max))
                    step(nc.vector.tensor_tensor(z, z2, ps[:, :, H:2 * H], ALU.subtract))
                    nc.vector.tensor_scalar(z2, z, 0.0, None, ALU.min).then_inc(logits_ready[b], 1)

                def weigh(p, b, g, t0, t1, ne):
                    for t in range(t0, t1):
                        rows = G[b][0:ne, t, 0:D].rearrange("p (h d) -> p h d", h=H)
                        nc.vector.tensor_tensor(
                            rows, rows,
                            weight[b][0:ne, t, :].rearrange("p (h o) -> p h o", o=1).broadcast_to([ne, H, DH]),
                            ALU.mult).then_inc(weighted[b], 1)

                def slot(late, next_early):
                    p, b, g, nt, ne = late
                    logits(*late)
                    dve.wait_ge(weights_ready[b], uses(b, p, g) + 1)
                    weigh(p, b, g, 0, min(WEAVE, nt), ne)
                    if next_early:
                        early(*next_early)
                    weigh(p, b, g, WEAVE, nt, ne)

                in_turn(dve, lambda p: None, early, slot)

            @block.scalar
            def _(act):
                for b in range(2):
                    act.sem_inc(flushed[b], 1)

                def start_pass(p):
                    act.wait_ge(added, 16 * (groups(0, p, 0) + 2))

                def exponentials(p, b, g, nt, ne):
                    act.wait_ge(logits_ready[b], uses(b, p, g) + 2)
                    nc.scalar.activation(weight[b][0:ne, 0:nt, :], shifted[b][0:ne, 0:nt, :],
                                         ACT.Exp).then_inc(weights_ready[b], 1)

                def slot(late, next_early):
                    if next_early:
                        exponentials(*next_early)
                    p, b, g, nt, ne = late
                    act.wait_ge(summed[b], tiles(b, p, g) + nt + TG)
                    act.wait_ge(added, 16 * (groups(b, p, g) + 1))
                    nc.scalar.activation(flush[b][:, 0:D], psN[b][:, :], ACT.Copy)
                    nc.scalar.activation(flush[b][:, D:ROW], psD[b][:, 0:H], ACT.Copy).then_inc(flushed[b], 1)

                in_turn(act, start_pass, exponentials, slot)

            @block.tensor
            def _(pe):
                for b in range(2):
                    pe.sem_inc(summed[b], TG)

                def early(p, b, g, nt, ne):
                    pe.wait_ge(onehots_ready[b], uses(b, p, g) + 1)
                    for t in range(nt):
                        last = nc.tensor.matmul(psS[b][0:ne, t * 2 * H:(t + 1) * 2 * H],
                                                onehot_T[b][:, t * ne:(t + 1) * ne],
                                                window[b][:, 0:2 * H], start=True, stop=True)
                    last.then_inc(scored, 1)

                def sum_up(p, b, g, t0, t1, nt, ne):
                    for t in range(t0, t1):
                        pe.wait_ge(weighted[b], tiles(b, p, g) + t + 1)
                        nc.tensor.matmul(psN[b][:, :], onehot[b][0:ne, t, :], G[b][0:ne, t, 0:D],
                                         start=(t == 0), stop=(t == nt - 1))
                        nc.tensor.matmul(psD[b][:, 0:H], onehot[b][0:ne, t, :], weight[b][0:ne, t, :],
                                         start=(t == 0), stop=(t == nt - 1)).then_inc(summed[b], 1)

                def slot(late, next_early):
                    p, b, g, nt, ne = late
                    pe.wait_ge(flushed[b], uses(b, p, g) + 1)
                    sum_up(p, b, g, 0, min(WEAVE_PE, nt), nt, ne)
                    if next_early:
                        early(*next_early)
                    sum_up(p, b, g, WEAVE_PE, nt, nt, ne)

                in_turn(pe, lambda p: None, early, slot)


def project_heads(nc, sem, bank, X, S, ident, sums, QT, KT, V, ln_g, ln_b, Wq, Wk, Wv, qn_g, kn_g):
    ctx = ExitStack()
    with ctx:
        def sb(name, shape, dt=F32):
            return ctx.enter_context(nc.sbuf_tensor(name, shape, dt))

        stats = sb("ln_stats", [P, NT, 6])
        mean_var = sb("ln_mean_var", [P, NT, 2])
        rstd = sb("ln_rstd", [P, NT])
        eps = sb("ln_eps", [P, 2])
        g_col, b_col = sb("ln_g_col", [P, KC]), sb("ln_b_col", [P, KC])
        qn_col, kn_col = sb("qn_col", [P, 1]), sb("kn_col", [P, 1])
        stage = [sb(f"w_stage{i}", [P, KC, D]) for i in range(2)]
        W_hi = [sb(f"Wqkv_hi{m}", [P, KC, D], F32R) for m in range(3)]
        W_lo = [sb(f"Wqkv_lo{m}", [P, KC, D], F32R) for m in range(3)]
        Hn = [sb(f"qkv_Hn{b}", [P, D]) for b in range(2)]
        HT = [sb(f"qkv_HT{b}", [P, KC, P]) for b in range(2)]
        HT_hi = [sb(f"qkv_HT_hi{b}", [P, KC, P], F32R) for b in range(2)]
        HT_lo = [sb(f"qkv_HT_lo{b}", [P, KC, P], F32R) for b in range(2)]
        square = [[sb(f"square{b}{m}", [P, D]) for m in range(2)] for b in range(2)]
        length = [sb(f"length{b}", [P, 2, H]) for b in range(2)]
        unit = [[sb(f"qk_unit{b}{m}", [P, D]) for m in range(2)] for b in range(2)]

        sums_loaded, cols_loaded = sem("sums_loaded"), sem("cols_loaded")
        w_loaded = [sem(f"wqkv_loaded{m}") for m in range(3)]
        own = sem("heads_vector_own")
        var_ready, root_ready = sem("ln_var_ready"), sem("ln_root_ready")
        w_hi_ready, w_lo_ready = sem("wqkv_hi_ready"), sem("wqkv_lo_ready")
        normed_ready = sem("ln_normed_ready")
        transposed, affine, hi_ready, lo_ready = (sem("qkv_transposed"), sem("qkv_affine"), sem("qkv_hi_ready"),
                                                  sem("qkv_lo_ready"))
        projected, squared, reduced, rooted = sem("qkv_projected"), sem("squared"), sem("reduced"), sem("rooted")
        scaled, v_read, qk_transposed, stored = sem("qk_scaled"), sem("v_read"), sem("qk_transposed"), sem("qk_stored")
        loop_own = sem("qkv_vector_own")

        psT = bank[0]
        psP = [[bank[1], bank[2], bank[3]], [bank[4], bank[5], bank[6]]]
        psX = [[bank[7], bank[1]], [bank[7], bank[4]]]
        chunks = lambda ps: ps[:, :].rearrange("p (c n) -> p c n", c=KC)

        with nc.Block() as block:
            @block.sync
            def _(sp):
                sp.dma_start(S[:, :, :], sums[0:NP, :].rearrange("(t p) r -> p t r", p=P)).then_inc(sums_loaded, 16)
                for col, vec in ((g_col, ln_g), (b_col, ln_b)):
                    sp.dma_start(col[:, :], vec.rearrange("(c p) -> p c", p=P),
                                 allow_slow_non_contiguous=True).then_inc(cols_loaded, 16)
                for col, vec in ((qn_col, qn_g), (kn_col, kn_g)):
                    for half in range(2):
                        sp.dma_start(col[half * DH:(half + 1) * DH, :],
                                     vec.rearrange("(p o) -> p o", o=1)).then_inc(cols_loaded, 16)
                for m, w in enumerate((Wq, Wk, Wv)):
                    if m == 2:
                        sp.wait_ge(w_lo_ready, 1)
                    sp.dma_start(stage[m % 2][:, :, :], w.rearrange("(c p) n -> p c n", p=P)).then_inc(w_loaded[m], 16)

            @block.gpsimd
            def _(pool):
                for m in range(3):
                    pool.wait_ge(w_hi_ready, m + 1)
                    nc.gpsimd.tensor_tensor(W_lo[m][:, :, :], stage[m % 2][:, :, :], W_hi[m][:, :, :].bitcast(F32),
                                            ALU.subtract).then_inc(w_lo_ready, 1)

            @block.scalar
            def _(act):
                for m in range(3):
                    act.wait_ge(w_loaded[m], 16)
                    nc.scalar.activation(W_hi[m][:, :, :], stage[m % 2][:, :, :], ACT.Copy).then_inc(w_hi_ready, 1)
                    if m < 2:
                        act.wait_ge(var_ready, m + 1)
                        nc.scalar.activation(rstd[:, :], mean_var[:, :, 1], ACT.Sqrt, bias=eps[:, 0:1]).then_inc(root_ready, 1)
                act.wait_ge(cols_loaded, 16 * 6)

                def transposed_parts(t, b):
                    act.wait_ge(transposed, t + 1)
                    for c in range(KC):
                        last = nc.scalar.activation(HT[b][:, c, :], chunks(psT)[:, c, :], ACT.Identity,
                                                    bias=b_col[:, c:c + 1], scale=g_col[:, c:c + 1])
                    last.then_inc(affine, 1)
                    act.wait_ge(affine, t + 1)
                    nc.scalar.activation(HT_hi[b][:, :, :], HT[b][:, :, :], ACT.Copy).then_inc(hi_ready, 1)

                def lengths(t, b):
                    for m in range(2):
                        act.wait_ge(projected, 3 * t + m + 1)
                        nc.scalar.activation(square[b][m][:, :], psP[b][m][:, :], ACT.Square).then_inc(squared, 1)
                    act.wait_ge(reduced, 2 * t + 2)
                    nc.scalar.activation(length[b][:, :, :], length[b][:, :, :], ACT.Sqrt, bias=eps[:, 1:2]).then_inc(rooted, 1)
                    act.wait_ge(projected, 3 * t + 3)
                    nc.scalar.activation(V[:, bass.ds(t, 1), :, 0:DH].rearrange("p o h d -> p (o h) d"),
                                         psP[b][2][:, :].rearrange("p (h d) -> p h d", h=H), ACT.Copy).then_inc(v_read, 1)

                def pair(j, last):
                    for b in range(2):
                        lengths(2 * j + b, b)
                        if not last:
                            transposed_parts(2 * j + b + 2, b)

                for b in range(2):
                    transposed_parts(b, b)
                with act.Fori(0, NT // 2 - 1) as j:
                    pair(j, False)
                pair(NT // 2 - 1, True)

            @block.vector
            def _(dve):
                step = Chain(dve, own)
                nc.vector.memset(eps[:, 0:1], EPS)
                nc.vector.memset(eps[:, 1:2], 1e-12)
                step(nc.vector.memset(V[:, :, :, DH:DH + 2], 1.0))
                dve.wait_ge(sums_loaded, 16)
                step(nc.vector.tensor_scalar(S[:, :, D:ROW], S[:, :, D:ROW], TINY, None, ALU.max))
                step(nc.vector.reciprocal(S[:, :, D:ROW], S[:, :, D:ROW]))
                for t in range(NT):
                    rows = S[:, t, 0:D].rearrange("p (h d) -> p h d", h=H)
                    last = nc.vector.tensor_tensor(
                        rows, rows, S[:, t, D:ROW].rearrange("p (h o) -> p h o", o=1).broadcast_to([P, H, DH]), ALU.mult)
                step(last)
                step(nc.vector.tensor_tensor(X[:, :, :], X[:, :, :], S[:, :, 0:D], ALU.add))
                source = X
                for n in range(2):
                    for t in range(NT):
                        last = nc.vector.bn_stats(stats[:, t, :], source[:, t, 0:D])
                    step(last)
                    for t in range(NT):
                        last = nc.vector.bn_aggr(mean_var[:, t, :], stats[:, t, :])
                    last.then_inc(var_ready, 1)
                    dve.wait_ge(root_ready, n + 1)
                    step(nc.vector.reciprocal(rstd[:, :], rstd[:, :]))
                    if n == 0:
                        for t in range(NT):
                            last = nc.vector.tensor_scalar(S[:, t, 0:D], X[:, t, :], mean_var[:, t, 0:1], rstd[:, t:t + 1],
                                                           ALU.subtract, ALU.mult)
                        step(last)
                    source = S
                dve.wait_ge(cols_loaded, 16 * 6)
                step(nc.vector.tensor_scalar(qn_col[:, :], qn_col[:, :], float(DH) ** 0.5, None, ALU.mult))

                def norm(t, b):
                    nc.vector.tensor_scalar(Hn[b][:, :], S[:, bass.ds(t, 1), 0:D].rearrange("p o d -> p (o d)"),
                                            mean_var[:, bass.ds(t, 1), 0], rstd[:, bass.ds(t, 1)],
                                            ALU.subtract, ALU.mult).then_inc(normed_ready, 1)

                def low_part(t, b):
                    dve.wait_ge(hi_ready, t + 1)
                    nc.vector.tensor_tensor(HT_lo[b][:, :, :], HT[b][:, :, :], HT_hi[b][:, :, :].bitcast(F32),
                                            ALU.subtract).then_inc(lo_ready, 1)

                def scale(t, b):
                    for m in range(2):
                        dve.wait_ge(squared, 2 * t + m + 1)
                        nc.vector.tensor_reduce(length[b][:, m, :], square[b][m][:, :].rearrange("p (h d) -> p h d", h=H),
                                                X_AXIS, ALU.add).then_inc(reduced, 1)
                    dve.wait_ge(rooted, t + 1)
                    nc.vector.reciprocal(length[b][:, :, :], length[b][:, :, :]).then_inc(loop_own, 1)
                    dve.wait_ge(loop_own, t + 1)
                    for m in range(2):
                        nc.vector.tensor_tensor(
                            unit[b][m][:, :].rearrange("p (h d) -> p h d", h=H),
                            psP[b][m][:, :].rearrange("p (h d) -> p h d", h=H),
                            length[b][:, m, :].rearrange("p (h o) -> p h o", o=1).broadcast_to([P, H, DH]),
                            ALU.mult).then_inc(scaled, 1)

                def store(t, b):
                    for m, (out, col) in enumerate(((QT, qn_col), (KT, kn_col))):
                        dve.wait_ge(qk_transposed, 2 * t + m + 1)
                        nc.vector.tensor_scalar(out[:, :, bass.ds(t * P, P)], chunks(psX[b][m]), col[:, 0:1], None,
                                                ALU.mult).then_inc(stored, 1)

                def pair(j, last):
                    for b in range(2):
                        if not last:
                            norm(2 * j + b + 2, b)
                        scale(2 * j + b, b)
                        if not last:
                            low_part(2 * j + b + 2, b)
                    for b in range(2):
                        store(2 * j + b, b)

                for b in range(2):
                    norm(b, b)
                for b in range(2):
                    low_part(b, b)
                with dve.Fori(0, NT // 2 - 1) as j:
                    pair(j, False)
                pair(NT // 2 - 1, True)

            @block.tensor
            def _(pe):
                def transpose(t, b):
                    pe.wait_ge(normed_ready, t + 1)
                    if not (isinstance(t, int) and t == 0):
                        pe.wait_ge(affine, t)
                    for c in range(KC):
                        last = nc.tensor.transpose(psT[:, c * P:(c + 1) * P], Hn[b][:, c * P:(c + 1) * P], ident[:, :])
                    last.then_inc(transposed, 1)

                def project(t, b, first):
                    pe.wait_ge(lo_ready, t + 1)
                    if not first:
                        pe.wait_ge(stored, 2 * t - 2)
                        pe.wait_ge(v_read, t - 1)
                    for m in range(3):
                        if first and b == 0:
                            pe.wait_ge(w_lo_ready, m + 1)
                        for n, (h, w) in enumerate(((HT_hi, W_hi), (HT_hi, W_lo), (HT_lo, W_hi))):
                            for c in range(KC):
                                last = nc.tensor.matmul(psP[b][m][:, :], h[b][:, c, :], w[m][:, c, :],
                                                        start=(n == 0 and c == 0), stop=(n == 2 and c == KC - 1))
                        last.then_inc(projected, 1)

                def transpose_heads(t, b):
                    for m in range(2):
                        pe.wait_ge(scaled, 2 * t + m + 1)
                        if m == 0 and not (isinstance(t, int) and t == 0):
                            pe.wait_ge(stored, 2 * t - 1)
                        for c in range(KC):
                            last = nc.tensor.transpose(psX[b][m][:, c * P:(c + 1) * P], unit[b][m][:, c * P:(c + 1) * P], ident[:, :])
                        last.then_inc(qk_transposed, 1)

                def pair(j, first, last):
                    for b in range(2):
                        project(2 * j + b, b, first)
                        if not last:
                            transpose(2 * j + b + 2, b)
                    for b in range(2):
                        transpose_heads(2 * j + b, b)

                for b in range(2):
                    transpose(b, b)
                pair(0, True, False)
                with pe.Fori(1, NT // 2 - 1) as j:
                    pair(j, False, False)
                pair(NT // 2 - 1, False, True)


def attend(nc, sem, psum, ident, QT, KT, V, O):
    ctx = ExitStack()
    with ctx:
        def sb(name, shape, dt=F32):
            return ctx.enter_context(nc.sbuf_tensor(name, shape, dt))

        CQ = 4
        CHUNKS = [range(c, min(c + CQ, NT)) for c in range(0, NT, CQ)]
        REGION = 1024
        PIECES = [(c, i, k0, min(k0 + REGION, (i + 1) * P))
                  for c, tiles in enumerate(CHUNKS) for i in tiles for k0 in range(0, (i + 1) * P, REGION)]
        KEYS = [tiles[-1] + 1 for tiles in CHUNKS]
        NC, NPC, NK = len(CHUNKS), len(PIECES), sum(KEYS)
        assert NPC % 2 == 0 and NK % 2 == 0
        FREE = 2 * NC

        Q = [sb(f"Qs{b}", [P, NP], F32R) for b in range(2)]
        K_hi = [sb(f"K_hi{b}", [P, NP], F32R) for b in range(2)]
        K_lo = [sb(f"K_lo{b}", [P, NP], F32R) for b in range(2)]
        Vs = [sb(f"Vs{b}", [P, NT, DH + 2]) for b in range(2)]
        PT = [[sb(f"PT{i}_{k}", [P, CQ * P]) for k in range(NT)] for i in range(2)]
        ident_b = sb("ident_b", [P, P], BF16)
        mask_q = sb("mask_q", [P, P], BF16)
        mask_k = sb("mask_k", [P, P], BF16)
        ones = sb("ones8", [2 * CQ, P], F32R)
        blocks = sb("blocks", [2 * CQ, CQ, P])
        part = sb("part_max", [P, 2])
        neg_max = sb("neg_max", [P, CQ])
        max_parts = sb("max_parts", [P, 2 * CQ], F32R)
        M = sb("max_row", [2 * CQ, CQ, P], F32R)
        inverse = sb("inverse", [P, CQ])

        masks_cleared, masks_ready = sem("masks_cleared"), sem("masks_ready")
        hi_staged, lo_staged, staged = sem("hi_staged"), sem("lo_staged"), sem("staged")
        scores_ready, maxed, max_split, max_transposed, max_ready = (
            sem("scores_ready"), sem("maxed"), sem("max_split"), sem("max_transposed"), sem("max_ready"))
        keyed, weighed, attended, o_read, own = (
            sem("keyed"), sem("exp_done"), sem("attended"), sem("o_read"), sem("attend_vector_own"))
        inverted, v_staged = sem("inverted"), sem("v_staged")

        region = [psum[:, n * REGION:(n + 1) * REGION] for n in range(2)]
        psK = [psum[:, (4 + n) * 512:(5 + n) * 512] for n in range(2)]
        psO = psum[:, 6 * 512:7 * 512]
        psM = psum[:, 7 * 512:8 * 512]

        def head(j, b):
            return 2 * j + b

        def chunk(j, b, c):
            return NC * head(j, b) + c

        def slots(j, last):
            for b in range(2):
                for c in range(NC):
                    if c + 1 < NC:
                        after = (j, b, c + 1)
                    elif b == 0:
                        after = (j, 1, 0)
                    else:
                        after = None if last else (j + 1, 0, 0)
                    yield b, c, after

        def in_turn(eng, slot):
            def pair(j, last):
                for b, c, after in slots(j, last):
                    slot(j, b, c, after, last)

            with eng.Fori(0, H // 2 - 1) as j:
                pair(j, False)
            pair(H // 2 - 1, True)

        def next_head(j, b, c, last):
            if c != 1 or (last and b == 1):
                return None
            return (j, 1) if b == 0 else (j + 1, 0)

        def halves(b):
            own_rows, other_rows = slice(b * DH, (b + 1) * DH), slice((1 - b) * DH, (2 - b) * DH)
            return own_rows, other_rows

        with nc.Block() as block:
            @block.gpsimd
            def _(pool):
                nc.gpsimd.memset(mask_q[:, :], 0.0)
                nc.gpsimd.memset(mask_k[:, :], 0.0)
                nc.gpsimd.memset(ones[:, :].bitcast(F32), 1.0)
                nc.gpsimd.memset(max_parts[:, :].bitcast(F32), 0.0)
                nc.gpsimd.tensor_copy(ident_b[:, :], ident[:, :])
                nc.gpsimd.memset(blocks[:, :, :], 0.0).then_inc(masks_cleared, 1)
                pool.wait_ge(masks_cleared, 1)
                nc.gpsimd.affine_select(out=mask_q[:, :], in_=mask_q[:, :], compare_op=ALU.is_ge, fill=MASKED,
                                        base=0, pattern=[[-1, P]], channel_multiplier=1)
                nc.gpsimd.affine_select(out=mask_k[:, :], in_=mask_k[:, :], compare_op=ALU.is_ge, fill=MASKED,
                                        base=0, pattern=[[1, P]], channel_multiplier=-1)
                nc.gpsimd.affine_select(out=blocks[:, :, :], in_=blocks[:, :, :], compare_op=ALU.not_equal, fill=1.0,
                                        base=0, pattern=[[-1, CQ], [0, P]], channel_multiplier=1).then_inc(masks_cleared, 1)
                pool.wait_ge(masks_cleared, 2)
                nc.gpsimd.affine_select(out=blocks[:, :, :], in_=blocks[:, :, :], compare_op=ALU.not_equal, fill=1.0,
                                        base=-CQ, pattern=[[-1, CQ], [0, P]], channel_multiplier=1).then_inc(masks_ready, 1)

                def stage(j, b):
                    rows, _ = halves(b)
                    pool.wait_ge(attended, NC * (head(j, b) - 1) + FREE)
                    if not (isinstance(j, int) and head(j, b) == 0):
                        pool.wait_ge(hi_staged, head(j, b))
                    nc.gpsimd.tensor_copy(Vs[b][:, :, :], V[:, :, bass.ds(head(j, b), 1), :].rearrange("p t o d -> p t (o d)")).then_inc(v_staged, 1)
                    pool.wait_ge(v_staged, head(j, b) + 1)
                    c = bass.ds(j, 1)
                    nc.gpsimd.tensor_copy(Q[b][rows, :], QT[rows, c, :].rearrange("p o n -> p (o n)"))
                    nc.gpsimd.tensor_copy(K_hi[b][rows, :], KT[rows, c, :].rearrange("p o n -> p (o n)")).then_inc(hi_staged, 1)

                pool.wait_ge(masks_ready, 1)
                stage(0, 0)

                def slot(j, b, c, after, last):
                    if nxt := next_head(j, b, c, last):
                        stage(*nxt)

                in_turn(pool, slot)

            @block.scalar
            def _(act):
                act.sem_inc(weighed, 2)

                def stage(j, b):
                    rows, others = halves(b)
                    act.wait_ge(lo_staged, head(j, b) + 1)
                    nc.scalar.activation(K_hi[b][others, :], K_hi[b][rows, :].bitcast(F32), ACT.Copy)
                    nc.scalar.activation(K_lo[b][others, :], K_lo[b][rows, :].bitcast(F32), ACT.Copy).then_inc(staged, 1)

                stage(0, 0)

                def slot(j, b, c, after, last):
                    act.wait_ge(attended, chunk(j, b, c) - 1 + FREE)
                    for kt in range(KEYS[c]):
                        n = NK * head(j, b) + sum(KEYS[:c]) + kt
                        lo = max(kt - CHUNKS[c][0], 0) * P
                        hi = len(CHUNKS[c]) * P
                        act.wait_ge(keyed, n + 1)
                        nc.scalar.activation(PT[(NC * b + c) % 2][kt][:, lo:hi], psK[kt_bank(b, c, kt)][:, lo:hi],
                                             ACT.Exp).then_inc(weighed, 1)
                    if nxt := next_head(j, b, c, last):
                        stage(*nxt)

                def kt_bank(b, c, kt):
                    return (sum(KEYS[:c]) + kt) % 2

                in_turn(act, slot)

            @block.vector
            def _(dve):
                def stage(j, b):
                    rows, others = halves(b)
                    c = bass.ds(j, 1)
                    dve.wait_ge(hi_staged, head(j, b) + 1)
                    nc.vector.tensor_tensor(Q[b][others, :], QT[rows, c, :].rearrange("p o n -> p (o n)"),
                                            Q[b][rows, :].bitcast(F32), ALU.subtract)
                    nc.vector.tensor_tensor(K_lo[b][rows, :], KT[rows, c, :].rearrange("p o n -> p (o n)"),
                                            K_hi[b][rows, :].bitcast(F32), ALU.subtract).then_inc(lo_staged, 1)

                def maxima(j, b, c):
                    step = Chain(dve, own, chunk(j, b, c) + head(j, b))
                    for s, (pc, i, k0, k1) in enumerate(PIECES):
                        if pc != c:
                            continue
                        dve.wait_ge(scores_ready, NPC * head(j, b) + s + 1)
                        whole = (i + 1) * P <= REGION
                        to = neg_max[:, i - CHUNKS[c][0]:i - CHUNKS[c][0] + 1] if whole or k0 == 0 else part[:, (i % 2):(i % 2) + 1]
                        nc.vector.tensor_reduce(to, region[s % 2][:, 0:k1 - k0], X_AXIS, ALU.max,
                                                negate=True).then_inc(maxed, 1)
                    dve.wait_ge(maxed, NPC * head(j, b) + sum(x[0] <= c for x in PIECES) + 2)
                    n = len(CHUNKS[c])
                    if c == NC - 1:
                        step(nc.vector.tensor_tensor(neg_max[:, 0:n], neg_max[:, 0:n], part[:, 0:n], ALU.min))
                    step(nc.vector.tensor_copy(max_parts[:, 0:n], neg_max[:, 0:n]))
                    nc.vector.tensor_tensor(max_parts[:, CQ:CQ + n], neg_max[:, 0:n], max_parts[:, 0:n].bitcast(F32),
                                            ALU.subtract).then_inc(max_split, 1)

                dve.sem_inc(maxed, 2)
                dve.sem_inc(o_read, 1)
                dve.wait_ge(masks_ready, 1)
                stage(0, 0)
                maxima(0, 0, 0)

                def slot(j, b, c, after, last):
                    dve.wait_ge(max_transposed, chunk(j, b, c) + 1)
                    nc.vector.tensor_tensor(M[:, :, :], psM[0:2 * CQ, 0:P].rearrange("p (o n) -> p o n", o=1).broadcast_to([2 * CQ, CQ, P]),
                                            blocks[:, :, :], ALU.mult).then_inc(max_ready, 1)
                    if nxt := next_head(j, b, c, last):
                        stage(*nxt)
                    if after:
                        maxima(*after)
                    n = len(CHUNKS[c])
                    o = psO[:, 0:n * (DH + 2)].rearrange("p (t d) -> p t d", d=DH + 2)
                    dve.wait_ge(attended, chunk(j, b, c) + 1 + FREE)
                    nc.vector.reciprocal(inverse[:, 0:n], o[:, :, DH]).then_inc(inverted, 1)
                    dve.wait_ge(inverted, chunk(j, b, c) + 1)
                    nc.vector.tensor_tensor(
                        O[:, CHUNKS[c][0]:CHUNKS[c][0] + n, bass.ds(head(j, b) * DH, DH)], o[:, :, 0:DH],
                        inverse[:, 0:n].rearrange("p (t o) -> p t o", o=1).broadcast_to([P, n, DH]),
                        ALU.mult).then_inc(o_read, 1)

                in_turn(dve, slot)

            @block.tensor
            def _(pe):
                pe.sem_inc(attended, FREE)
                pe.wait_ge(masks_ready, 1)

                def scores(j, b, c):
                    for s, (pc, i, k0, k1) in enumerate(PIECES):
                        if pc != c:
                            continue
                        if s == 0:
                            pe.wait_ge(staged, head(j, b) + 1)
                        pe.wait_ge(maxed, NPC * head(j, b) + s + 1)
                        q = Q[b][:, i * P:(i + 1) * P]
                        for a in range(k0, k1, 512):
                            e = min(a + 512, k1)
                            out = region[s % 2][:, a - k0:e - k0]
                            diagonal = e == (i + 1) * P
                            nc.tensor.matmul(out, q, K_hi[b][:, a:e], start=True, stop=False)
                            last = nc.tensor.matmul(out, q, K_lo[b][:, a:e], start=False, stop=not diagonal)
                            if diagonal:
                                last = nc.tensor.matmul(region[s % 2][:, e - P - k0:e - k0], ident_b[:, :], mask_q[:, :],
                                                        start=False, stop=True)
                        last.then_inc(scores_ready, 1)

                scores(0, 0, 0)

                def slot(j, b, c, after, last):
                    pe.wait_ge(max_split, chunk(j, b, c) + 1)
                    nc.tensor.transpose(psM[0:2 * CQ, 0:P], max_parts[:, :].bitcast(F32), ident[:, :]).then_inc(max_transposed, 1)
                    if after:
                        scores(*after)
                    pe.wait_ge(max_ready, chunk(j, b, c) + 1)
                    first = CHUNKS[c][0]
                    hi = len(CHUNKS[c]) * P
                    for kt in range(KEYS[c]):
                        n = NK * head(j, b) + sum(KEYS[:c]) + kt
                        lo = max(kt - first, 0) * P
                        pe.wait_ge(weighed, n + 1)
                        out = psK[(sum(KEYS[:c]) + kt) % 2]
                        q = Q[b][:, first * P + lo:first * P + hi]
                        nc.tensor.matmul(out[:, lo:hi], K_hi[b][:, kt * P:(kt + 1) * P], q, start=True, stop=False)
                        nc.tensor.matmul(out[:, lo:hi], K_lo[b][:, kt * P:(kt + 1) * P], q, start=False, stop=False)
                        if kt >= first:
                            nc.tensor.matmul(out[:, lo:lo + P], ident_b[:, :], mask_k[:, :], start=False, stop=False)
                        nc.tensor.matmul(out[:, lo:hi], ones[:, :], M[:, :, :].rearrange("p t n -> p (t n)")[:, lo:hi],
                                         start=False, stop=True).then_inc(keyed, 1)
                    pe.wait_ge(o_read, chunk(j, b, c) + 1)
                    for i in CHUNKS[c]:
                        pe.wait_ge(weighed, NK * head(j, b) + sum(KEYS[:c]) + i + 1 + 2)
                        for kt in range(i + 1):
                            last = nc.tensor.matmul(psO[:, (i - first) * (DH + 2):(i - first + 1) * (DH + 2)],
                                                    PT[(NC * b + c) % 2][kt][:, (i - first) * P:(i - first + 1) * P],
                                                    Vs[b][:, kt, :], start=(kt == 0), stop=(kt == i))
                    last.then_inc(attended, 1)

                in_turn(pe, slot)


def combine_heads(nc, sem, bank, ident, O, yT, logits, raw, parts, weights_loaded, weights_hi, weights_lo,
                  Wo, gate_W, gate_b, W1, W2):
    ctx = ExitStack()
    with ctx:
        def sb(name, shape, dt=F32):
            return ctx.enter_context(nc.sbuf_tensor(name, shape, dt))

        STEP = 2 * P
        NS = NP // STEP
        Wo_raw = sb("Wo_raw", [P, KC, D])
        Wo_hi, Wo_lo = sb("Wo_hi", [P, KC, D], F32R), sb("Wo_lo", [P, KC, D], F32R)
        OT_hi, OT_lo = sb("OT_hi", [P, KC, NP], F32R), sb("OT_lo", [P, KC, NP], F32R)
        O_tile = [sb(f"O_tile{b}", [P, D]) for b in range(2)]
        gW = sb("gate_weights", [P, KC, H])
        gW_hi, gW_lo = sb("gate_hi", [P, KC, H], F32R), sb("gate_lo", [P, KC, H], F32R)
        gb_col = sb("gate_bias", [H, 1])

        tile_ready = sem("o_tile_ready")
        wo_loaded, gate_loaded = sem("wo_loaded"), sem("gate_loaded")
        wo_hi_ready, wo_lo_ready = sem("wo_hi_ready"), sem("wo_lo_ready")
        gate_hi_ready, gate_lo_ready = sem("gate_hi_ready"), sem("gate_lo_ready")
        o_transposed, ot_hi_ready, ot_lo_ready = sem("o_transposed"), sem("ot_hi_ready"), sem("ot_lo_ready")
        y_made, y_hi_ready, y_lo_ready = sem("y_made"), sem("y_hi_ready"), sem("y_lo_ready")
        gate_turn = sem("gate_turn")
        logits_made, logits_read = sem("logits_made"), sem("logits_read")

        psT, psY, psL = bank[0:2], bank[2:6], bank[6]
        chunks = lambda ps: ps[:, :].rearrange("p (c n) -> p c n", c=KC)
        yT_hi, yT_lo = yT

        def in_steps(eng, turn, product, gate):
            turn(0)
            turn(1)
            product(0)
            with eng.Fori(1, NS - 1) as n:
                turn(n + 1)
                product(n)
                gate(n - 1)
            product(NS - 1)
            gate(NS - 2)
            gate(NS - 1)

        with nc.Block() as block:
            @block.sync
            def _(sp):
                sp.dma_start(Wo_raw[:, :, :], Wo.rearrange("(c p) n -> p c n", p=P)).then_inc(wo_loaded, 16)
                sp.dma_start(gW[:, :, :], gate_W.rearrange("(c p) n -> p c n", p=P)).then_inc(gate_loaded, 16)
                sp.dma_start(gb_col[:, :], gate_b.rearrange("(p o) -> p o", o=1)).then_inc(gate_loaded, 16)
                for e in range(2):
                    for w, source in enumerate((W1, W2)):
                        sp.dma_start(raw[w][e][:, :, :], source[e].rearrange("(c p) n -> p c n", p=P)).then_inc(weights_loaded[e], 16)

            @block.gpsimd
            def _(pool):
                def turn(n):
                    for b in range(2):
                        if not (isinstance(n, int) and n == 0):
                            pool.wait_ge(o_transposed, 2 * n + b - 1)
                        nc.gpsimd.tensor_copy(O_tile[b][:, :], O[:, bass.ds(2 * n + b, 1), :].rearrange("p o n -> p (o n)")).then_inc(tile_ready, 1)

                turn(0)
                pool.wait_ge(wo_hi_ready, 1)
                nc.gpsimd.tensor_tensor(Wo_lo[:, :, :], Wo_raw[:, :, :], Wo_hi[:, :, :].bitcast(F32),
                                        ALU.subtract).then_inc(wo_lo_ready, 1)
                with pool.Fori(1, NS) as n:
                    turn(n)
                for w in range(2):
                    pool.wait_ge(weights_hi, w + 1)
                    nc.gpsimd.tensor_tensor(parts[w][0][1][:, :, :], raw[w][0][:, :, :], parts[w][0][0][:, :, :].bitcast(F32),
                                            ALU.subtract).then_inc(weights_lo, 1)

            @block.scalar
            def _(act):
                act.wait_ge(wo_loaded, 16)
                nc.scalar.activation(Wo_hi[:, :, :], Wo_raw[:, :, :], ACT.Copy).then_inc(wo_hi_ready, 1)
                act.wait_ge(gate_loaded, 32)
                nc.scalar.activation(gW_hi[:, :, :], gW[:, :, :], ACT.Copy).then_inc(gate_hi_ready, 1)

                def turn(n):
                    for b in range(2):
                        act.wait_ge(o_transposed, 2 * n + b + 1)
                        nc.scalar.activation(OT_hi[:, :, bass.ds((2 * n + b) * P, P)], chunks(psT[b]), ACT.Copy).then_inc(ot_hi_ready, 1)

                def product(n):
                    for m in range(KC):
                        act.wait_ge(y_made, KC * n + m + 1)
                        nc.scalar.activation(yT_hi[:, m, bass.ds(n * STEP, STEP)], psY[m][:, 0:STEP], ACT.Copy).then_inc(y_hi_ready, 1)

                def gate(n):
                    act.wait_ge(logits_made, n + 1)
                    act.sem_inc(gate_turn, 1)
                    nc.scalar.activation(logits[:, bass.ds(n * STEP, STEP)], psL[0:H, 0:STEP], ACT.Identity,
                                         bias=gb_col[:, 0:1]).then_inc(logits_read, 1)

                in_steps(act, turn, product, gate)
                act.wait_ge(weights_loaded[0], 32)
                for w in range(2):
                    nc.scalar.activation(parts[w][0][0][:, :, :], raw[w][0][:, :, :], ACT.Copy).then_inc(weights_hi, 1)

            @block.vector
            def _(dve):
                dve.wait_ge(gate_hi_ready, 1)
                nc.vector.tensor_tensor(gW_lo[:, :, :], gW[:, :, :], gW_hi[:, :, :].bitcast(F32), ALU.subtract).then_inc(gate_lo_ready, 1)

                def turn(n):
                    for b in range(2):
                        dve.wait_ge(ot_hi_ready, 2 * n + b + 1)
                        cols = bass.ds((2 * n + b) * P, P)
                        nc.vector.tensor_tensor(OT_lo[:, :, cols], chunks(psT[b]), OT_hi[:, :, cols].bitcast(F32),
                                                ALU.subtract).then_inc(ot_lo_ready, 1)

                def product(n):
                    for m in range(KC):
                        dve.wait_ge(y_hi_ready, KC * n + m + 1)
                        cols = bass.ds(n * STEP, STEP)
                        nc.vector.tensor_tensor(yT_lo[:, m, cols], psY[m][:, 0:STEP], yT_hi[:, m, cols].bitcast(F32),
                                                ALU.subtract).then_inc(y_lo_ready, 1)

                in_steps(dve, turn, product, lambda n: None)

            @block.tensor
            def _(pe):
                pe.sem_inc(ot_lo_ready, 2)
                pe.sem_inc(y_lo_ready, KC)
                pe.sem_inc(logits_read, 1)

                def turn(n):
                    for b in range(2):
                        pe.wait_ge(tile_ready, 2 * n + b + 1)
                        pe.wait_ge(ot_lo_ready, 2 * n + b + 1)
                        for c in range(KC):
                            last = nc.tensor.transpose(psT[b][:, c * P:(c + 1) * P],
                                                       O_tile[b][:, c * P:(c + 1) * P], ident[:, :])
                        last.then_inc(o_transposed, 1)

                def product(n):
                    if isinstance(n, int) and n == 0:
                        pe.wait_ge(wo_lo_ready, 1)
                    pe.wait_ge(ot_lo_ready, 2 * n + 4)
                    cols = bass.ds(n * STEP, STEP)
                    for m in range(KC):
                        pe.wait_ge(y_lo_ready, KC * n + m + 1)
                        for i, (w, o) in enumerate(((Wo_hi, OT_hi), (Wo_lo, OT_hi), (Wo_hi, OT_lo))):
                            for c in range(KC):
                                last = nc.tensor.matmul(psY[m][:, 0:STEP], w[:, c, m * P:(m + 1) * P], o[:, c, cols],
                                                        start=(i == 0 and c == 0), stop=(i == 2 and c == KC - 1))
                        last.then_inc(y_made, 1)

                def gate(n):
                    pe.wait_ge(logits_read, n + 1)
                    pe.wait_ge(y_lo_ready, KC * n + 2 * KC)
                    cols = bass.ds(n * STEP, STEP)
                    for i, (w, y) in enumerate(((gW_hi, yT_hi), (gW_lo, yT_hi), (gW_hi, yT_lo))):
                        for c in range(KC):
                            last = nc.tensor.matmul(psL[0:H, 0:STEP], w[:, c, :], y[:, c, cols],
                                                    start=(i == 0 and c == 0), stop=(i == 2 and c == KC - 1))
                    last.then_inc(logits_made, 1)

                pe.wait_ge(gate_lo_ready, 1)
                in_steps(pe, turn, product, gate)


def run_experts(nc, sem, bank, ident, X, yT, logits, raw, parts, weights_loaded, weights_hi, weights_lo,
                W1, b1, W2, b2):
    ctx = ExitStack()
    with ctx:
        def sb(name, shape, dt=F32):
            return ctx.enter_context(nc.sbuf_tensor(name, shape, dt))

        NE, F = W1.shape[0], W1.shape[2]
        FC = F // P
        SPANS = [(a, min(a + 512, NP)) for a in range(0, NP, 512)]
        NSP = len(SPANS)
        NB = 3
        NO = 5
        assert (NSP * FC) % NB == 0 and NT % NO == 0 and NB + NO == 8 and NE == H

        parts = [parts[w] + [[sb(f"expert_hi{w}", [P, c, n], F32R), sb(f"expert_lo{w}", [P, c, n], F32R)]]
                 for w, (c, n) in enumerate(((KC, F), (FC, D)))]
        hid = [sb(f"hid{s}", [P, FC, 512]) for s in range(NSP)]
        hid_hi, hid_lo = sb("hid_hi", [P, FC, NP], F32R), sb("hid_lo", [P, FC, NP], F32R)
        b1_col = sb("b1_col", [P, NE * FC])
        b2_rows = sb("b2_rows", [NE, D])
        gates = sb("gates", [P, NT, NE])
        reduced = sb("gate_reduced", [P, NT])
        gatesT = sb("gatesT", [NE, NP])

        biases_loaded = sem("biases_loaded")
        logits_turned, gates_ready, gates_turned, gatesT_ready = (sem("logits_turned"), sem("gates_ready"),
                                                                  sem("gates_turned"), sem("gatesT_ready"))
        own, shifted, exps_ready = sem("expert_vector_own"), sem("gates_shifted"), sem("gates_exps")
        hid_made, gelu_done, hid_hi_ready, hid_lo_ready = (sem("hid_made"), sem("gelu_done"), sem("hid_hi_ready"),
                                                           sem("hid_lo_ready"))
        gelu_turn = sem("gelu_turn")
        expert_made, mixed = sem("expert_made"), sem("mixed")

        psH, psE, psG = bank[0:NB], bank[NB:], bank[7]
        yT_hi, yT_lo = yT

        def in_pairs(eng, step):
            with eng.Fori(0, NE // 2 - 1) as j:
                for b in range(2):
                    step(2 * j + b, b, True, True)
            step(NE - 2, 0, True, False)
            step(NE - 1, 1, False, False)

        with nc.Block() as block:
            @block.sync
            def _(sp):
                sp.dma_start(b1_col[:, :], b1.rearrange("e (f p) -> p (e f)", p=P),
                             allow_slow_non_contiguous=True).then_inc(biases_loaded, 16)
                sp.dma_start(b2_rows[:, :], b2).then_inc(biases_loaded, 16)

                def step(e, b, more_hidden, more_weights):
                    if more_weights:
                        sp.wait_ge(weights_lo, 2 * e + 2)
                        for w, source in enumerate((W1, W2)):
                            sp.dma_start(raw[w][b][:, :, :],
                                         source[bass.ds(e + 2, 1)].rearrange("o (c p) n -> p (o c) n", p=P)).then_inc(weights_loaded[b], 16)

                in_pairs(sp, step)

            @block.gpsimd
            def _(pool):
                def weights(e, b):
                    for w in range(2):
                        pool.wait_ge(weights_hi, 2 * e + w + 1)
                        nc.gpsimd.tensor_tensor(parts[w][b][1][:, :, :], raw[w][b][:, :, :], parts[w][b][0][:, :, :].bitcast(F32),
                                                ALU.subtract).then_inc(weights_lo, 1)

                def hidden(e):
                    for s, (n0, n1) in enumerate(SPANS):
                        pool.wait_ge(hid_hi_ready, NSP * e + s + 1)
                        nc.gpsimd.tensor_tensor(hid_lo[:, :, n0:n1], hid[s][:, :, 0:n1 - n0], hid_hi[:, :, n0:n1].bitcast(F32),
                                                ALU.subtract).then_inc(hid_lo_ready, 1)

                weights(1, 1)
                hidden(0)

                def step(e, b, more_hidden, more_weights):
                    if more_hidden:
                        hidden(e + 1)
                    if more_weights:
                        weights(e + 2, b)

                in_pairs(pool, step)

            @block.scalar
            def _(act):
                act.sem_inc(hid_lo_ready, NSP)
                act.sem_inc(gelu_done, NB)

                def weights(e, b, j):
                    act.wait_ge(weights_loaded[b], 32 * (j + 1))
                    for w in range(2):
                        nc.scalar.activation(parts[w][b][0][:, :, :], raw[w][b][:, :, :], ACT.Copy).then_inc(weights_hi, 1)

                def hidden(e):
                    for s, (n0, n1) in enumerate(SPANS):
                        act.wait_ge(hid_lo_ready, NSP * e + s + 1)
                        for f in range(FC):
                            act.wait_ge(hid_made, NSP * FC * e + FC * s + f + 1)
                            act.sem_inc(gelu_turn, 1)
                            nc.scalar.activation(hid[s][:, f, 0:n1 - n0], psH[(FC * s + f) % NB][:, 0:n1 - n0], ACT.Gelu_apprx_tanh,
                                                 bias=b1_col[:, bass.ds(FC * e + f, 1)]).then_inc(gelu_done, 1)
                        act.wait_ge(gelu_done, NSP * FC * e + FC * s + FC + NB)
                        nc.scalar.activation(hid_hi[:, :, n0:n1], hid[s][:, :, 0:n1 - n0], ACT.Copy).then_inc(hid_hi_ready, 1)

                weights(1, 1, 0)
                act.wait_ge(shifted, 1)
                nc.scalar.activation(gates[:, :, :], gates[:, :, :], ACT.Exp).then_inc(exps_ready, 1)
                act.wait_ge(biases_loaded, 32)
                hidden(0)

                with act.Fori(0, NE // 2 - 1) as j:
                    for b in range(2):
                        hidden(2 * j + b + 1)
                        weights(2 * j + b + 2, b, j + 1)
                hidden(NE - 1)

            @block.vector
            def _(dve):
                step = Chain(dve, own)
                wide = lambda a: a[:, :].rearrange("p (t o) -> p t o", o=1).broadcast_to([P, NT, NE])
                turned = psG[:, 0:NT * NE].rearrange("p (t e) -> p t e", e=NE)
                dve.wait_ge(logits_turned, 1)
                step(nc.vector.tensor_reduce(reduced[:, :], turned, X_AXIS, ALU.max))
                nc.vector.tensor_tensor(gates[:, :, :], turned, wide(reduced), ALU.subtract).then_inc(shifted, 1)
                dve.wait_ge(exps_ready, 1)
                step(nc.vector.tensor_reduce(reduced[:, :], gates[:, :, :], X_AXIS, ALU.add))
                step(nc.vector.reciprocal(reduced[:, :], reduced[:, :]))
                nc.vector.tensor_tensor(gates[:, :, :], gates[:, :, :], wide(reduced), ALU.mult).then_inc(gates_ready, 1)
                dve.wait_ge(gates_ready, 1)
                for s, (n0, n1) in enumerate(SPANS):
                    dve.wait_ge(gates_turned, s + 1)
                    nc.vector.tensor_copy(gatesT[:, n0:n1], psE[s][0:NE, 0:n1 - n0]).then_inc(gatesT_ready, 1)
                for t in range(NT):
                    dve.wait_ge(expert_made, t + 1)
                    nc.vector.tensor_tensor(X[:, t, :], psE[t % NO][:, :], X[:, t, :], ALU.add).then_inc(mixed, 1)

                def mix(e, b, more_hidden, more_weights):
                    for t in range(NT):
                        dve.wait_ge(expert_made, NT * (e + 1) + t + 1)
                        dve.wait_ge(mixed, NT * e + t + 1)
                        nc.vector.scalar_tensor_tensor(X[:, t, :], psE[t % NO][:, :], gates[:, t, bass.ds(e, 1)], X[:, t, :],
                                                       ALU.mult, ALU.add).then_inc(mixed, 1)

                in_pairs(dve, mix)

            @block.tensor
            def _(pe):
                for t in range(NT):
                    last = nc.tensor.transpose(psG[:, t * NE:(t + 1) * NE], logits[:, t * P:(t + 1) * P], ident[0:NE, 0:NE])
                last.then_inc(logits_turned, 1)

                def hidden(e, b):
                    pe.wait_ge(weights_lo, 2 * e + 1)
                    for s, (n0, n1) in enumerate(SPANS):
                        for f in range(FC):
                            pe.wait_ge(gelu_done, NSP * FC * e + FC * s + f + 1)
                            w_hi, w_lo = parts[0][b]
                            for i, (w, y) in enumerate(((w_hi, yT_hi), (w_lo, yT_hi), (w_hi, yT_lo))):
                                for c in range(KC):
                                    last = nc.tensor.matmul(psH[(FC * s + f) % NB][:, 0:n1 - n0], w[:, c, f * P:(f + 1) * P],
                                                            y[:, c, n0:n1], start=(i == 0 and c == 0), stop=(i == 2 and c == KC - 1))
                            last.then_inc(hid_made, 1)

                def result(e, b):
                    pe.wait_ge(weights_lo, 2 * e + 2)
                    for t in range(NT):
                        pe.wait_ge(hid_lo_ready, NSP * e + t * P // 512 + 1 + NSP)
                        pe.wait_ge(mixed, NT * (e + 1) + t + 1 - NO)
                        w_hi, w_lo = parts[1][b]
                        rows = slice(t * P, (t + 1) * P)
                        for i, (h, w) in enumerate(((hid_hi, w_hi), (hid_hi, w_lo), (hid_lo, w_hi))):
                            for f in range(FC):
                                last = nc.tensor.matmul(psE[t % NO][:, :], h[:, f, rows], w[:, f, :],
                                                        start=(i == 0 and f == 0), stop=(i == 2 and f == FC - 1))
                        last.then_inc(expert_made, 1)

                hidden(0, 0)
                pe.wait_ge(gates_ready, 1)
                for s, (n0, n1) in enumerate(SPANS):
                    for t in range(n0 // P, n1 // P):
                        last = nc.tensor.transpose(psE[s][0:NE, t * P - n0:(t + 1) * P - n0], gates[:, t, :], ident[:, :])
                    last.then_inc(gates_turned, 1)
                pe.wait_ge(biases_loaded, 32)
                pe.wait_ge(gatesT_ready, NSP)
                for t in range(NT):
                    if t >= NO:
                        pe.wait_ge(mixed, t + 1 - NO)
                    nc.tensor.matmul(psE[t % NO][:, :], gatesT[:, t * P:(t + 1) * P], b2_rows[:, :],
                                     start=True, stop=True).then_inc(expert_made, 1)

                def step(e, b, more_hidden, more_weights):
                    result(e, b)
                    if more_hidden:
                        hidden(e + 1, 1 - b)

                in_pairs(pe, step)


def store_out(nc, sem, X, out):
    stored = sem("stored")
    with nc.Block() as block:
        @block.sync
        def _(sp):
            sp.dma_start(out[0:(NT - 1) * P, :].rearrange("(t p) d -> p t d", p=P), X[:, 0:NT - 1, :]).then_inc(stored, 16)
            sp.dma_start(out[(NT - 1) * P:N, :], X[0:N - (NT - 1) * P, NT - 1, :]).then_inc(stored, 16)
            sp.wait_ge(stored, 32)


_INS = ['x', 'src', 'dst', 'L0_gnn_Ws', 'L0_gnn_Wb', 'L0_gnn_a_w', 'L0_gnn_a_b', 'L0_ffn_ln_g', 'L0_ffn_ln_b',
        'L0_ffn_Wq', 'L0_ffn_Wk', 'L0_ffn_Wv', 'L0_ffn_Wo', 'L0_ffn_qn_g', 'L0_ffn_kn_g', 'L0_ffn_gate_W',
        'L0_ffn_gate_b', 'L0_ffn_W1', 'L0_ffn_b1', 'L0_ffn_W2', 'L0_ffn_b2']


def kernel(**inputs):
    import numpy as _np
    import concourse.bacc as _bacc
    from concourse import mybir as _mybir
    from concourse.bass_utils import run_bass_kernel_spmd as _run

    nc = _bacc.Bacc("TRN2", target_bir_lowering=False, num_devices=1)
    arrays, args = {}, []
    for name in _INS:
        a = _np.ascontiguousarray(inputs[name])
        arrays[f"in_{name}_dram"] = a
        args.append(nc.dram_tensor(f"in_{name}_dram", a.shape, _mybir.dt.from_np(a.dtype), kind="ExternalInput").ap())
    args.append(nc.dram_tensor("out_0_dram", (1250, 512), _mybir.dt.float32, kind="ExternalOutput").ap())
    build(nc, *args)
    r = _run(nc, [arrays], core_ids=[0])
    return r.results[0]["out_0_dram"]
```

```python
import concourse.bass as bass
from concourse import mybir
from contextlib import ExitStack

F32 = mybir.dt.float32
F32R = mybir.dt.float32r
I32 = mybir.dt.int32
BF16 = mybir.dt.bfloat16
ALU = mybir.AluOpType
ACT = mybir.ActivationFunctionType
X_AXIS = mybir.AxisListType.X
XY_AXES = mybir.AxisListType.XY
RMAX = bass.bass_isa.ReduceOp.max

P = 128
N = 1250
NT = -(-N // P)
NP = NT * P
D = 512
KC = D // P
H = 8
DH = D // H
E = 20000
TG = 13
GE = TG * P
NG = E // GE
TAIL = E - NG * GE
ROW = D + H
WR = 24
WROWS = NP + P
TINY = 1e-37
RANGE = 50.0
EPS = 1e-5
SPREAD = KC * NP // P
MASKED = -1e30


class Chain:

    def __init__(self, eng, sem, base=0):
        self.eng, self.sem, self.base, self.n = eng, sem, base, 0

    def __call__(self, ins):
        self.n += 1
        ins.then_inc(self.sem, 1)
        self.eng.wait_ge(self.sem, self.base + self.n)


def build(nc, x, src, dst, Ws, Wb, a_w, a_b, ln_g, ln_b, Wq, Wk, Wv, Wo, qn_g, kn_g,
          gate_W, gate_b, W1, b1, W2, b2, out):
    ctx = ExitStack()
    with ctx:
        def sb(name, shape, dt=F32):
            return ctx.enter_context(nc.sbuf_tensor(name, shape, dt))

        def sem(name):
            return ctx.enter_context(nc.semaphore(name))

        psum = ctx.enter_context(nc.psum_tensor("psum", [P, 8 * 512], F32))
        bank = [psum[:, i * 512:(i + 1) * 512] for i in range(8)]
        source_table = nc.dram_tensor("source_table", [NP, ROW], F32, kind="Internal").ap()
        window_table = nc.dram_tensor("window_table", [WROWS, WR], F32, kind="Internal").ap()
        node_numbers = nc.dram_tensor("node_numbers", [1, WROWS], F32, kind="Internal").ap()
        sums = nc.dram_tensor("sums", [WROWS, ROW], F32, kind="Internal").ap()

        sums_row = nc.dram_tensor("sums_row", [2, KC * NP], F32, kind="Internal").ap()
        inverse_row = nc.dram_tensor("inverse_row", [2, KC * NP], F32, kind="Internal").ap()
        X = sb("X", [P, NT, D])
        ident = sb("ident", [P, P])
        bases = sb("bases", [1, NT * (NG + 1)], I32)
        passes = sb("passes", [1, 1], I32)
        wide_range = sb("wide_range", [1, 1], I32)
        scores = sb("scores", [P, NT, 2 * H])
        window = sb("window", [P, NT + 1, WR])
        added = sem("added")

        project_nodes(nc, sem, bank, X, ident, bases, passes, wide_range, scores, window, source_table,
                      window_table, node_numbers, sums, added, x, dst, Ws, Wb, a_w, a_b)
        find_maxima(nc, sem, psum, ident, wide_range, scores, window, source_table, window_table, src, dst)
        sum_edges(nc, sem, bank, ident, bases, passes, source_table, window_table, node_numbers,
                  sums, added, src, dst)
        room = sb("sums_then_results", [P, NT * ROW])
        S = room[:, :].rearrange("p (t r) -> p t r", r=ROW)
        OT = room[:, 0:KC * NP].rearrange("p (c n) -> p c n", c=KC)
        weight_sums = sb("weight_sums", [P, 2, SPREAD])
        with ExitStack() as heads:
            QT, KT = (heads.enter_context(nc.sbuf_tensor(name, [P, KC, NP], F32)) for name in ("QT", "KT"))
            V = heads.enter_context(nc.sbuf_tensor("V", [P, NT, D], F32))
            project_heads(nc, sem, bank, X, S, ident, sums, QT, KT, V, ln_g, ln_b, Wq, Wk, Wv, qn_g, kn_g)
            attend(nc, sem, psum, ident, QT, KT, V, OT, weight_sums, sums_row)

        F = W1.shape[2]
        yT = [sb(name, [P, KC, NP], F32R) for name in ("yT_hi", "yT_lo")]
        logits = sb("logits", [H, NP])
        raw = [[sb(f"expert_raw{w}{b}", [P, c, n]) for b in range(2)] for w, (c, n) in enumerate(((KC, F), (F // P, D)))]
        parts = [[[sb(f"expert_{part}{w}", [P, c, n], F32R) for part in ("first_hi", "first_lo")]]
                 for w, (c, n) in enumerate(((KC, F), (F // P, D)))]
        weights_loaded = [sem(f"expert_loaded{b}") for b in range(2)]
        weights_hi, weights_lo = sem("expert_weights_hi"), sem("expert_weights_lo")
        combine_heads(nc, sem, psum, bank, OT, weight_sums, inverse_row, yT, logits, raw, parts, weights_loaded, weights_hi, weights_lo,
                      Wo, gate_W, gate_b, W1, W2)
        run_experts(nc, sem, bank, ident, X, yT, logits, raw, parts, weights_loaded, weights_hi, weights_lo,
                    W1, b1, W2, b2)
        store_out(nc, sem, X, out)


def project_nodes(nc, sem, bank, X, ident, bases, passes, wide_range, scores, window, source_table,
                  window_table, node_numbers, sums, added, x, dst, Ws, Wb, a_w, a_b):
    ctx = ExitStack()
    with ctx:
        def sb(name, shape, dt=F32):
            return ctx.enter_context(nc.sbuf_tensor(name, shape, dt))

        W = sb("W", [P, KC, D])
        W_hi, W_lo = sb("W_hi", [P, KC, D], F32R), sb("W_lo", [P, KC, D], F32R)
        Wa = sb("Wa", [P, KC, 2 * H])
        Wa_hi, Wa_lo = sb("Wa_hi", [P, KC, 2 * H], F32R), sb("Wa_lo", [P, KC, 2 * H], F32R)
        a_row = sb("a_row", [P, H, 2 * DH])
        ab_row = sb("ab_row", [P, H])
        Wb_row = sb("Wb_row", [P, D])
        score_bias = sb("score_bias", [P, 2 * H])
        product = [sb(f"product{i}", [P, KC * D]) for i in range(2)]
        stats = sb("stats", [P, NT, 6])
        mean_var = sb("mean_var", [P, NT, 2])
        rstd = sb("rstd", [P, NT])
        eps = sb("eps", [P, 1])
        Hn = [sb(f"Hn{b}", [P, D]) for b in range(2)]
        HT_hi = [sb(f"HT_hi{b}", [P, KC, P], F32R) for b in range(2)]
        HT_lo = [sb(f"HT_lo{b}", [P, KC, P], F32R) for b in range(2)]
        row = [sb(f"row{b}", [P, ROW]) for b in range(2)]
        bound = sb("bound", [P, 2 * H])
        bound_all = sb("bound_all", [P, 2 * H])
        zeros = sb("zeros", [P, NT * ROW])
        numbers = sb("numbers", [1, WROWS])
        dst_all = sb("dst_all", [P, NG, TG], I32)
        dst_tail = sb("dst_tail", [TAIL, 1], I32)
        first = sb("first", [P, NG + 1], I32)
        off = sb("off", [P, NG, TG])
        off_tail = sb("off_tail", [TAIL, 1])
        outside = sb("outside", [P, 2])
        outside_all = sb("outside_all", [P, 2])
        bad = sb("bad", [1, 4])
        base_f = sb("base_f", [1, NT, NG + 1])
        tile_base = sb("tile_base", [1, NT, NG + 1])
        first_f = sb("first_f", [1, NG + 1])

        x_loaded = sem("x_loaded")
        w_loaded = sem("w_loaded")
        dst_loaded = sem("dst_loaded")
        pad_cleared = sem("pad_cleared")
        ident_zeroed = sem("ident_zeroed")
        ident_ready = sem("ident_ready")
        numbers_ready = sem("numbers_ready")
        zeros_ready = sem("zeros_ready")
        var_ready = sem("var_ready")
        root_ready = sem("root_ready")
        weights_ready = sem("weights_ready")
        w_hi_ready, w_lo_ready, product_ready = sem("w_hi_ready"), sem("w_lo_ready"), sem("source_product_ready")
        tile_base_ready = sem("tile_base_ready")
        normed = sem("normed")
        transposed = sem("transposed")
        hi_ready = sem("hi_ready")
        lo_ready = sem("lo_ready")
        projected = sem("projected")
        row_ready = sem("row_ready")
        row_stored = [sem(f"row_stored{b}") for b in range(2)]
        own = sem("project_vector_own")
        bound_ready = sem("bound_ready")
        bound_reduced = sem("bound_reduced")
        outside_ready = sem("outside_ready")
        outside_reduced = sem("outside_reduced")
        window_ready = sem("window_ready")
        tables_stored = sem("tables_stored")

        LAST = N - (NT - 1) * P
        psT = [bank[0], bank[1]]
        psW = [bank[2], bank[3]]
        psS = [bank[4], bank[5]]
        W_LOADS = H + 3

        def flag_windows(dve, step):
            dve.wait_ge(dst_loaded, 16 * 4)
            step(nc.vector.tensor_tensor(off[:, :, :], dst_all[:, :, :],
                                         first[:, 0:NG].rearrange("p (g o) -> p g o", o=1).broadcast_to([P, NG, TG]),
                                         ALU.subtract))
            step(nc.vector.tensor_tensor(off_tail[:, :], dst_tail[:, :], first[0:TAIL, NG:NG + 1], ALU.subtract))
            step(nc.vector.tensor_reduce(outside[:, 0:1], off[:, :, :], XY_AXES, ALU.max))
            step(nc.vector.tensor_reduce(outside[:, 1:2], off[:, :, :], XY_AXES, ALU.min))
            step(nc.vector.tensor_tensor(outside[0:TAIL, 0:1], outside[0:TAIL, 0:1], off_tail[:, :], ALU.max))
            step(nc.vector.tensor_tensor(outside[0:TAIL, 1:2], outside[0:TAIL, 1:2], off_tail[:, :], ALU.min))
            nc.vector.tensor_scalar(outside[:, 1:2], outside[:, 1:2], -1.0, None, ALU.mult).then_inc(outside_ready, 1)
            dve.wait_ge(outside_reduced, 1)
            step(nc.vector.tensor_scalar(bad[:, 0:1], outside_all[0:1, 0:1], float(P - 1), None, ALU.is_gt))
            step(nc.vector.tensor_scalar(bad[:, 1:2], outside_all[0:1, 1:2], 0.0, None, ALU.is_gt))
            step(nc.vector.tensor_tensor(bad[:, 2:3], bad[:, 0:1], bad[:, 1:2], ALU.max))
            step(nc.vector.tensor_scalar(passes[:, :], bad[:, 2:3], float(NT - 1), 1.0, ALU.mult, ALU.add))
            step(nc.vector.tensor_scalar(bad[:, 3:4], bad[:, 2:3], -1.0, 1.0, ALU.mult, ALU.add))
            step(nc.vector.tensor_scalar(first_f[:, :], first[0:1, :], bad[:, 3:4], None, ALU.mult))
            dve.wait_ge(tile_base_ready, 1)
            step(nc.vector.scalar_tensor_tensor(base_f[:, :, :], tile_base[:, :, :], bad[:, 2:3],
                                                first_f[:, :].rearrange("p (o g) -> p o g", o=1).broadcast_to([1, NT, NG + 1]),
                                                ALU.mult, ALU.add))
            step(nc.vector.tensor_copy(bases[:, :], base_f[:, :, :].rearrange("p t g -> p (t g)")))

        with nc.Block() as block:
            @block.sync
            def _(sp):
                sp.wait_ge(pad_cleared, 1)
                sp.dma_start(X[:, 0:NT - 1, :],
                             x[0:(NT - 1) * P, :].rearrange("(t p) d -> p t d", p=P)).then_inc(x_loaded, 16)
                sp.dma_start(X[0:LAST, NT - 1, :], x[(NT - 1) * P:N, :]).then_inc(x_loaded, 16)
                sp.dma_start(dst_all[:, :, :],
                             dst[0:NG * GE].rearrange("(g p t) -> p g t", p=P, t=TG)).then_inc(dst_loaded, 16)
                sp.dma_start(dst_tail[:, :], dst[NG * GE:E].rearrange("(p o) -> p o", o=1)).then_inc(dst_loaded, 16)
                sp.dma_start(first[:, 0:NG],
                             dst[0:NG * GE].rearrange("(g e) -> g e", e=GE)[:, 0].partition_broadcast(P),
                             allow_slow_non_contiguous=True).then_inc(dst_loaded, 16)
                sp.dma_start(first[:, NG:NG + 1],
                             dst[NG * GE:NG * GE + 1].partition_broadcast(P)).then_inc(dst_loaded, 16)
                sp.wait_ge(numbers_ready, 1)
                sp.dma_start(node_numbers, numbers[:, :]).then_inc(tables_stored, 16)
                with sp.Fori(0, NT // 2) as j:
                    for b in range(2):
                        sp.wait_ge(row_ready, 2 * j + b + 1)
                        sp.dma_start(source_table[bass.ds((2 * j + b) * P, P), :],
                                     row[b][:, :]).then_inc(row_stored[b], 16)
                sp.wait_ge(window_ready, 1)
                sp.dma_start(window_table.rearrange("(t p) r -> p t r", p=P), window[:, :, :]).then_inc(tables_stored, 16)
                sp.wait_ge(tables_stored, 32)
                for b in range(2):
                    sp.wait_ge(row_stored[b], 16 * (NT // 2))

            @block.gpsimd
            def _(pool):
                nc.gpsimd.memset(ident[:, :], 0.0).then_inc(ident_zeroed, 1)
                pool.wait_ge(ident_zeroed, 1)
                nc.gpsimd.affine_select(out=ident[:, :], in_=ident[:, :], compare_op=ALU.not_equal, fill=1.0,
                                        base=0, pattern=[[-1, P]], channel_multiplier=1).then_inc(ident_ready, 1)
                nc.gpsimd.iota(tile_base[:, :, :], [[P, NT], [0, NG + 1]], 0, 0,
                               allow_small_or_imprecise_dtypes=True).then_inc(tile_base_ready, 1)
                nc.gpsimd.memset(zeros[:, :], 0.0).then_inc(zeros_ready, 1)
                pool.wait_ge(zeros_ready, 1)
                for t0, t1 in ((0, NT), (NT, NT + 1)):
                    nc.gpsimd.dma_start(sums[t0 * P:t1 * P, :].rearrange("(t p) r -> p t r", p=P),
                                        zeros[:, 0:(t1 - t0) * ROW].rearrange("p (t r) -> p t r", r=ROW)).then_inc(added, 16)
                nc.gpsimd.iota(numbers[:, :], [[1, WROWS]], 0, 0,
                               allow_small_or_imprecise_dtypes=True).then_inc(numbers_ready, 1)
                nc.gpsimd.iota(window[:, :, 2 * H:2 * H + 1], [[P, NT + 1]], 0, 1,
                               allow_small_or_imprecise_dtypes=True).then_inc(numbers_ready, 1)
                pool.wait_ge(outside_ready, 1)
                nc.gpsimd.partition_all_reduce(outside_all[:, :], outside[:, :], P, RMAX).then_inc(outside_reduced, 1)
                pool.wait_ge(w_loaded, 16 * W_LOADS)
                for c in range(KC):
                    last = nc.gpsimd.tensor_tensor(product[1][:, c * D:(c + 1) * D].rearrange("p (h d) -> p h d", h=H),
                                                   W[:, c, :].rearrange("p (h d) -> p h d", h=H), a_row[:, :, DH:2 * DH], ALU.mult)
                last.then_inc(product_ready, 1)
                pool.wait_ge(w_hi_ready, 1)
                nc.gpsimd.tensor_tensor(W_lo[:, :, :], W[:, :, :], W_hi[:, :, :].bitcast(F32), ALU.subtract).then_inc(w_lo_ready, 1)
                pool.wait_ge(bound_ready, 1)
                nc.gpsimd.partition_all_reduce(bound_all[:, :], bound[:, :], P, RMAX).then_inc(bound_reduced, 1)
                pool.wait_ge(added, 32)

            @block.scalar
            def _(act):
                for h in range(H):
                    act.dma_start(W[:, :, h * DH:(h + 1) * DH],
                                 Ws[h].rearrange("(c p) d -> p c d", p=P)).then_inc(w_loaded, 16)
                act.dma_start(a_row[:, :, :], a_w.partition_broadcast(P)).then_inc(w_loaded, 16)
                act.dma_start(ab_row[:, :], a_b.partition_broadcast(P)).then_inc(w_loaded, 16)
                act.dma_start(Wb_row[:, :], Wb.rearrange("h d -> (h d)").partition_broadcast(P)).then_inc(w_loaded, 16)
                act.wait_ge(var_ready, 2)
                nc.scalar.activation(rstd[:, :], mean_var[:, :, 1], ACT.Sqrt, bias=eps[:, 0:1]).then_inc(root_ready, 1)

                def high_part(t, b):
                    act.wait_ge(transposed, t + 1)
                    nc.scalar.activation(HT_hi[b][:, :, :], psT[b][:, :].rearrange("p (c n) -> p c n", c=KC),
                                         ACT.Copy).then_inc(hi_ready, 1)

                high_part(0, 0)
                high_part(1, 1)
                act.wait_ge(w_loaded, 16 * W_LOADS)
                nc.scalar.activation(W_hi[:, :, :], W[:, :, :], ACT.Copy).then_inc(w_hi_ready, 1)
                with act.Fori(0, NT // 2 - 1) as j:
                    for b in range(2):
                        high_part(2 * j + b + 2, b)

            @block.vector
            def _(dve):
                step = Chain(dve, own)
                nc.vector.memset(X[:, NT - 1, :], 0.0).then_inc(pad_cleared, 1)
                nc.vector.memset(eps[:, :], EPS).then_inc(var_ready, 1)
                step(nc.vector.memset(window[:, :, 2 * H + 1:WR], 0.0))
                step(nc.vector.memset(window[:, :, 0:2 * H], 0.0))
                dve.wait_ge(x_loaded, 32)
                for t in range(NT):
                    last = nc.vector.bn_stats(stats[:, t, :], X[:, t, :])
                step(last)
                for t in range(NT):
                    last = nc.vector.bn_aggr(mean_var[:, t, :], stats[:, t, :])
                last.then_inc(var_ready, 1)
                dve.wait_ge(root_ready, 1)
                step(nc.vector.reciprocal(rstd[:, :], rstd[:, :]))

                def norm(t, b):
                    nc.vector.tensor_scalar(Hn[b][:, :], X[:, bass.ds(t, 1), :].rearrange("p o d -> p (o d)"),
                                            mean_var[:, bass.ds(t, 1), 0], rstd[:, bass.ds(t, 1)],
                                            ALU.subtract, ALU.mult).then_inc(normed, 1)

                def low_part(t, b):
                    dve.wait_ge(hi_ready, t + 1)
                    nc.vector.tensor_tensor(HT_lo[b][:, :, :], psT[b][:, :].rearrange("p (c n) -> p c n", c=KC),
                                            HT_hi[b][:, :, :].bitcast(F32), ALU.subtract).then_inc(lo_ready, 1)

                def results(t, b, j, first):
                    dve.wait_ge(projected, t + 1)
                    if not first:
                        dve.wait_ge(row_stored[b], 16 * j)
                    nc.vector.tensor_tensor(row[b][:, 0:D], psW[b][:, :], Wb_row[:, :], ALU.add)
                    nc.vector.tensor_tensor(row[b][:, D:ROW], psS[b][:, H:2 * H], score_bias[:, H:2 * H], ALU.add)
                    nc.vector.tensor_tensor(scores[:, bass.ds(t, 1), :].rearrange("p o s -> p (o s)"),
                                            psS[b][:, 0:2 * H], score_bias[:, :], ALU.add).then_inc(row_ready, 1)

                for b in range(2):
                    norm(b, b)
                for b in range(2):
                    low_part(b, b)
                flag_windows(dve, step)
                dve.wait_ge(w_loaded, 16 * W_LOADS)
                Wv4 = W[:, :, :].rearrange("p c (h d) -> p c h d", h=H)
                for half in range(2):
                    part = a_row[:, :, half * DH:(half + 1) * DH]
                    pr = product[half][:, :].rearrange("p (c h d) -> p c h d", c=KC, h=H)
                    if half == 0:
                        for c in range(KC):
                            last = nc.vector.tensor_tensor(pr[:, c], Wv4[:, c], part, ALU.mult)
                        step(last)
                    else:
                        dve.wait_ge(product_ready, 1)
                    step(nc.vector.tensor_reduce(Wa[:, :, half * H:(half + 1) * H], pr, X_AXIS, ALU.add))
                    step(nc.vector.tensor_tensor(pr[:, 0], Wb_row[:, :].rearrange("p (h d) -> p h d", h=H), part, ALU.mult))
                    step(nc.vector.tensor_reduce(score_bias[:, half * H:(half + 1) * H], pr[:, 0], X_AXIS, ALU.add))
                step(nc.vector.tensor_tensor(score_bias[:, 0:H], score_bias[:, 0:H], ab_row[:, :], ALU.add))
                step(nc.vector.tensor_copy(Wa_hi[:, :, :], Wa[:, :, :]))
                nc.vector.tensor_tensor(Wa_lo[:, :, :], Wa[:, :, :], Wa_hi[:, :, :].bitcast(F32),
                                        ALU.subtract).then_inc(weights_ready, 1)

                def pair(j, first, last):
                    if not last:
                        for b in range(2):
                            norm(2 * j + b + 2, b)
                    for b in range(2):
                        results(2 * j + b, b, j, first)
                        if not last:
                            low_part(2 * j + b + 2, b)

                pair(0, True, False)
                with dve.Fori(1, NT // 2 - 1) as j:
                    pair(j, False, False)
                pair(NT // 2 - 1, False, True)
                dve.wait_ge(row_ready, NT)
                of_sources = scores[:, :, H:2 * H].rearrange("p t h -> p h t")
                nc.vector.tensor_reduce(bound[:, 0:H], of_sources, X_AXIS, ALU.max)
                nc.vector.tensor_reduce(bound[:, H:2 * H], of_sources, X_AXIS, ALU.min, negate=True).then_inc(bound_ready, 1)
                dve.wait_ge(bound_reduced, 1)
                step(nc.vector.tensor_copy(window[:, 0:NT, 0:H], scores[:, :, 0:H]))
                for t in range(NT):
                    last = nc.vector.tensor_tensor(window[:, t, H:2 * H], scores[:, t, 0:H], bound_all[:, 0:H], ALU.add)
                step(last)
                step(nc.vector.tensor_tensor(bound_all[:, 0:H], bound_all[:, 0:H], bound_all[:, H:2 * H], ALU.add))
                step(nc.vector.tensor_reduce(bound_all[:, H:H + 1], bound_all[:, 0:H], X_AXIS, ALU.max))
                step(nc.vector.tensor_scalar(wide_range[:, :], bound_all[0:1, H:H + 1], RANGE, None, ALU.is_gt))
                dve.wait_ge(numbers_ready, 2)
                for t in range(NT):
                    last = nc.vector.scalar_tensor_tensor(window[:, t, H:2 * H], window[:, t, H:2 * H], 0.2,
                                                          window[:, t, H:2 * H], ALU.mult, ALU.max)
                last.then_inc(window_ready, 1)

            @block.tensor
            def _(pe):
                pe.wait_ge(ident_ready, 1)

                def transpose(t, b):
                    pe.wait_ge(normed, t + 1)
                    if not (isinstance(t, int) and t < 2):
                        pe.wait_ge(lo_ready, t - 1)
                    for c in range(KC):
                        last = nc.tensor.transpose(psT[b][:, c * P:(c + 1) * P], Hn[b][:, c * P:(c + 1) * P], ident[:, :])
                    last.then_inc(transposed, 1)

                def project(t, b, first):
                    pe.wait_ge(lo_ready, t + 1)
                    if not first:
                        pe.wait_ge(row_ready, t - 1)
                    pairs = [(HT_hi, W_hi, Wa_hi), (HT_hi, W_lo, Wa_lo), (HT_lo, W_hi, Wa_hi)]
                    for n, (h, w, wa) in enumerate(pairs):
                        for c in range(KC):
                            nc.tensor.matmul(psW[b][:, :], h[b][:, c, :], w[:, c, :],
                                             start=(n == 0 and c == 0), stop=(n == 2 and c == KC - 1))
                    for n, (h, w, wa) in enumerate(pairs):
                        for c in range(KC):
                            last = nc.tensor.matmul(psS[b][:, 0:2 * H], h[b][:, c, :], wa[:, c, :],
                                                    start=(n == 0 and c == 0), stop=(n == 2 and c == KC - 1))
                    last.then_inc(projected, 1)

                def pair(j, first, last):
                    for b in range(2):
                        project(2 * j + b, b, first)
                        if not last:
                            transpose(2 * j + b + 2, b)

                for b in range(2):
                    transpose(b, b)
                pe.wait_ge(weights_ready, 1)
                pe.wait_ge(w_lo_ready, 1)
                pair(0, True, False)
                with pe.Fori(1, NT // 2 - 1) as j:
                    pair(j, False, False)
                pair(NT // 2 - 1, False, True)


def find_maxima(nc, sem, psum, ident, wide_range, scores, window, source_table, window_table, src, dst):
    ctx = ExitStack()
    with ctx:
        def sb(name, shape, dt=F32):
            return ctx.enter_context(nc.sbuf_tensor(name, shape, dt))

        CT = 4
        CH = CT * P
        CHUNKS = E // CH
        source = sb("chunk_source", [P, CT], I32)
        targets_row = sb("chunk_targets", [P, CH], I32)
        G = sb("chunk_rows", [P, CT, ROW])
        rows_T = sb("chunk_scores", [H, CH])
        pick = sb("pick_head", [H, H, P])
        mask = sb("chunk_mask", [P, CT, P])
        masked = sb("chunk_masked", [P, H, CH])
        best = sb("chunk_best", [P, H])
        maxima = sb("node_maxima", [P, NT, H])

        loaded, gathered, turned, copied, spread, chunk_done = (
            sem("chunk_loaded"), sem("chunk_gathered"), sem("chunk_turned"), sem("chunk_copied"), sem("chunk_spread"),
            sem("chunk_done"))
        gate, chunk_turn = sem("chunk_gate"), sem("chunk_turn")
        pick_cleared, pick_ready = sem("pick_cleared"), sem("pick_ready")
        own, own_end = sem("maxima_vector_own"), sem("end_vector_own")
        shifts_ready, stored = sem("shifts_ready"), sem("shifts_stored")

        def if_wide(eng, body):
            wide = eng.value_load(wide_range[0:1, 0:1], min_val=0, max_val=1)
            with eng.If(wide > 0):
                body()
            eng.end_ifs()

        def every_chunk(eng, chunk):
            with eng.Fori(0, CHUNKS) as c:
                chunk(c, c * CH)
            chunk(CHUNKS, E - CH)

        with nc.Block() as block:
            @block.sync
            def _(sp):
                def chunk(c, at):
                    sp.wait_ge(chunk_done, c + 1)
                    sp.dma_start(source[:, :], src[bass.ds(at, CH)].rearrange("(p t) -> p t", t=CT)).then_inc(loaded, 16)
                    sp.dma_start(targets_row[:, :], dst[bass.ds(at, CH)].partition_broadcast(P)).then_inc(loaded, 16)

                def body():
                    every_chunk(sp, chunk)
                    sp.wait_ge(shifts_ready, 1)
                    sp.dma_start(window_table.rearrange("(t p) r -> p t r", p=P), window[:, :, :]).then_inc(stored, 16)
                    sp.wait_ge(stored, 16)

                if_wide(sp, body)

            @block.gpsimd
            def _(pool):
                def chunk(c, at):
                    pool.wait_ge(loaded, 32 * (c + 1))
                    pool.sem_inc(gate, 1)
                    for t in range(CT):
                        nc.gpsimd.indirect_dma_start(
                            G[:, t, :], None, source_table,
                            bass.IndirectOffsetOnAxis(ap=source[:, t:t + 1], axis=0)).then_inc(gathered, 16)

                def body():
                    nc.gpsimd.memset(pick[:, :, :], 0.0).then_inc(pick_cleared, 1)
                    pool.wait_ge(pick_cleared, 1)
                    nc.gpsimd.affine_select(out=pick[:, :, :], in_=pick[:, :, :], compare_op=ALU.not_equal, fill=1.0,
                                            base=0, pattern=[[-1, H], [0, P]], channel_multiplier=1).then_inc(pick_ready, 1)
                    every_chunk(pool, chunk)

                if_wide(pool, body)

            @block.vector
            def _(dve):
                def chunk(c, at):
                    dve.wait_ge(turned, c + 1)
                    nc.vector.tensor_copy(rows_T[:, :], psum[0:H, 0:CH]).then_inc(copied, 1)
                    dve.wait_ge(spread, c + 1)
                    dve.sem_inc(chunk_turn, 1)
                    with dve.Fori(0, NT) as t:
                        step = Chain(dve, own, 4 * (NT * c + t))
                        step(nc.vector.tensor_scalar(mask[:, :, :], targets_row[:, :].rearrange("n (p t) -> n t p", t=CT),
                                                     window[:, bass.ds(t, 1), 2 * H], None, ALU.not_equal))
                        step(nc.vector.scalar_tensor_tensor(
                            masked[:, :, :], mask[:, :, :].rearrange("p (o t) n -> p o (t n)", o=1).broadcast_to([P, H, CH]),
                            MASKED, psum[:, :].rearrange("p (h n) -> p h n", h=H), ALU.mult, ALU.add))
                        step(nc.vector.tensor_reduce(best[:, :], masked[:, :, :], X_AXIS, ALU.max))
                        now = maxima[:, bass.ds(t, 1), :].rearrange("p o h -> p (o h)")
                        step(nc.vector.tensor_tensor(now, now, best[:, :], ALU.max))
                    dve.sem_inc(chunk_done, 1)

                def body():
                    step = Chain(dve, own_end)
                    step(nc.vector.memset(maxima[:, :, :], MASKED))
                    dve.sem_inc(chunk_done, 1)
                    every_chunk(dve, chunk)
                    shift = window[:, 0:NT, H:2 * H]
                    step(nc.vector.tensor_tensor(maxima[:, :, :], scores[:, :, 0:H], maxima[:, :, :], ALU.add))
                    nc.vector.scalar_tensor_tensor(shift, maxima[:, :, :], 0.2, maxima[:, :, :], ALU.mult, ALU.max).then_inc(shifts_ready, 1)

                if_wide(dve, body)

            @block.tensor
            def _(pe):
                def chunk(c, at):
                    pe.wait_ge(gathered, 16 * CT * (c + 1))
                    for t in range(CT):
                        last = nc.tensor.transpose(psum[0:H, t * P:(t + 1) * P], G[:, t, D:ROW], ident[:, :])
                    last.then_inc(turned, 1)
                    pe.wait_ge(copied, c + 1)
                    for h in range(H):
                        last = nc.tensor.matmul(psum[:, h * CH:(h + 1) * CH], pick[:, h, :], rows_T[:, :], start=True, stop=True)
                    last.then_inc(spread, 1)

                def body():
                    pe.wait_ge(pick_ready, 1)
                    every_chunk(pe, chunk)

                if_wide(pe, body)


def sum_edges(nc, sem, bank, ident, bases, passes, source_table, window_table, node_numbers, sums,
              added, src, dst):
    ctx = ExitStack()
    with ctx:
        def sb(name, shape, dt=F32):
            return ctx.enter_context(nc.sbuf_tensor(name, shape, dt))

        G = [sb(f"G{b}", [P, TG, ROW]) for b in range(2)]
        target = [sb(f"target{b}", [P, TG], I32) for b in range(2)]
        source = [sb(f"source{b}", [P, TG], I32) for b in range(2)]
        target_f = [sb(f"target_f{b}", [P, TG]) for b in range(2)]
        window = [sb(f"window_rows{b}", [P, WR]) for b in range(2)]
        nodes = [sb(f"nodes{b}", [P, P]) for b in range(2)]
        onehot = [sb(f"onehot{b}", [P, TG, P]) for b in range(2)]
        onehot_T = [sb(f"onehot_T{b}", [P, TG * P]) for b in range(2)]
        targets_row = [sb(f"targets_row{b}", [P, GE], I32) for b in range(2)]
        logit = [sb(f"logit{b}", [P, TG, H]) for b in range(2)]
        shifted = [sb(f"shifted{b}", [P, TG, H]) for b in range(2)]
        weight = [sb(f"weight{b}", [P, TG, H]) for b in range(2)]
        flush = [sb(f"flush{b}", [P, ROW]) for b in range(2)]
        psS = [bank[2], bank[3]]
        psN = [bank[4], bank[5]]
        psD = [bank[6], bank[7]]

        loaded = [sem(f"loaded{b}") for b in range(2)]
        gathered = [sem(f"gathered{b}") for b in range(2)]
        onehots_ready = [sem(f"onehots_ready{b}") for b in range(2)]
        gate = sem("gate")
        scored = sem("scored")
        logits_ready = [sem(f"logits_ready{b}") for b in range(2)]
        weights_ready = [sem(f"edge_weights_ready{b}") for b in range(2)]
        weighted = [sem(f"weighted{b}") for b in range(2)]
        summed = [sem(f"summed{b}") for b in range(2)]
        flushed = [sem(f"flushed{b}") for b in range(2)]
        own_early = sem("edges_vector_own_early")
        own_late = sem("edges_vector_own_late")

        PAIRS = NG // 2
        LOADS = 5 * 16
        WEAVE = 4
        WEAVE_PE = 9

        def uses(b, p, g):
            return p * (PAIRS + (b == 0)) + g

        def tiles(b, p, g):
            return p * (PAIRS * TG + (b == 0)) + g * TG

        def groups(b, p, g):
            return p * (NG + 1) + 2 * g + b

        def in_turn(eng, start_pass, early, slot):
            rounds = eng.value_load(passes[0:1, 0:1], min_val=1, max_val=NT)
            with eng.Fori(0, rounds) as p:
                start_pass(p)
                early(p, 0, 0, TG, P)
                with eng.Fori(0, PAIRS - 1) as g:
                    slot((p, 0, g, TG, P), (p, 1, g, TG, P))
                    slot((p, 1, g, TG, P), (p, 0, g + 1, TG, P))
                g = PAIRS - 1
                slot((p, 0, g, TG, P), (p, 1, g, TG, P))
                slot((p, 1, g, TG, P), (p, 0, g + 1, 1, TAIL))
                slot((p, 0, g + 1, 1, TAIL), None)

        with nc.Block() as block:
            @block.sync
            def _(sp):
                def load(p, b, g, nt, ne):
                    base = sp.value_load(bases[0:1, bass.ds(groups(b, p, g), 1)], min_val=0, max_val=NP - 1)
                    sp.wait_ge(logits_ready[b], uses(b, p, g) + 1)
                    at = (2 * g + b) * GE
                    sp.dma_start(target[b][0:ne, 0:nt],
                                 dst[bass.ds(at, ne * nt)].rearrange("(p t) -> p t", t=nt)).then_inc(loaded[b], 16)
                    sp.dma_start(targets_row[b][:, 0:ne * nt],
                                 dst[bass.ds(at, ne * nt)].partition_broadcast(P)).then_inc(loaded[b], 16)
                    sp.dma_start(source[b][0:ne, 0:nt],
                                 src[bass.ds(at, ne * nt)].rearrange("(p t) -> p t", t=nt)).then_inc(loaded[b], 16)
                    sp.dma_start(window[b][:, :], window_table[bass.ds(base, P), :]).then_inc(loaded[b], 16)
                    sp.dma_start(nodes[b][:, :],
                                 node_numbers[0, bass.ds(base, P)].partition_broadcast(P)).then_inc(loaded[b], 16)

                in_turn(sp, lambda p: None, load, lambda late, early: load(*early) if early else None)

            @block.gpsimd
            def _(pool):
                def gather(p, b, g, nt, ne):
                    pool.wait_ge(loaded[b], LOADS * (uses(b, p, g) + 1))
                    for t in range(nt):
                        pool.wait_ge(summed[b], tiles(b, p, g) + t + 1)
                        pool.sem_inc(gate, 1)
                        nc.gpsimd.indirect_dma_start(
                            G[b][0:ne, t, :], None, source_table,
                            bass.IndirectOffsetOnAxis(ap=source[b][0:ne, t:t + 1], axis=0)).then_inc(gathered[b], 16)

                def add(p, b, g):
                    base = pool.value_load(bases[0:1, bass.ds(groups(b, p, g), 1)], min_val=0, max_val=NP - 1)
                    pool.wait_ge(flushed[b], uses(b, p, g) + 2)
                    pool.wait_ge(added, 16 * (groups(b, p, g) + 2))
                    nc.gpsimd.dma_start(sums[bass.ds(base, P), :], flush[b][:, :],
                                        accum_op=ALU.add).then_inc(added, 16)

                rounds = pool.value_load(passes[0:1, 0:1], min_val=1, max_val=NT)
                with pool.Fori(0, rounds) as p:
                    for b in range(2):
                        pool.wait_ge(summed[b], tiles(b, p, 0) + TG)
                        gather(p, b, 0, TG, P)
                    with pool.Fori(1, PAIRS) as g:
                        for b in range(2):
                            gather(p, b, g, TG, P)
                            add(p, b, g - 1)
                    gather(p, 0, PAIRS, 1, TAIL)
                    for b in range(2):
                        add(p, b, PAIRS - 1)
                    add(p, 0, PAIRS)
                pool.wait_ge(added, 16 * (rounds * (NG + 1) + 2))

            @block.vector
            def _(dve):
                for b in range(2):
                    dve.sem_inc(logits_ready[b], 1)

                def early(p, b, g, nt, ne):
                    dve.wait_ge(loaded[b], LOADS * (uses(b, p, g) + 1))
                    dve.wait_ge(summed[b], tiles(b, p, g) + TG)
                    step = Chain(dve, own_early, groups(b, p, g))
                    step(nc.vector.tensor_copy(target_f[b][0:ne, 0:nt], target[b][0:ne, 0:nt]))
                    nc.vector.tensor_tensor(
                        onehot[b][0:ne, 0:nt, :],
                        nodes[b][0:ne, :].rearrange("p (o n) -> p o n", o=1).broadcast_to([ne, nt, P]),
                        target_f[b][0:ne, 0:nt].rearrange("p (t o) -> p t o", o=1).broadcast_to([ne, nt, P]),
                        ALU.is_equal)
                    nc.vector.tensor_scalar(
                        onehot_T[b][:, 0:nt * ne].rearrange("n (t p) -> n t p", t=nt),
                        targets_row[b][:, 0:nt * ne].rearrange("n (p t) -> n t p", t=nt),
                        window[b][:, 2 * H:2 * H + 1], None, ALU.is_equal).then_inc(onehots_ready[b], 1)

                def logits(p, b, g, nt, ne):
                    dve.wait_ge(gathered[b], 16 * (tiles(b, p, g) + nt))
                    dve.wait_ge(scored, groups(b, p, g) + 1)
                    ps = psS[b][0:ne, 0:nt * 2 * H].rearrange("p (t s) -> p t s", s=2 * H)
                    z, z2 = logit[b][0:ne, 0:nt, :], shifted[b][0:ne, 0:nt, :]
                    step = Chain(dve, own_late, 3 * groups(b, p, g))
                    step(nc.vector.tensor_tensor(z, ps[:, :, 0:H], G[b][0:ne, 0:nt, D:ROW], ALU.add))
                    step(nc.vector.scalar_tensor_tensor(z2, z, 0.2, z, ALU.mult, ALU.max))
                    step(nc.vector.tensor_tensor(z, z2, ps[:, :, H:2 * H], ALU.subtract))
                    nc.vector.tensor_scalar(z2, z, 0.0, None, ALU.min).then_inc(logits_ready[b], 1)

                def weigh(p, b, g, t0, t1, ne):
                    for t in range(t0, t1):
                        rows = G[b][0:ne, t, 0:D].rearrange("p (h d) -> p h d", h=H)
                        nc.vector.tensor_tensor(
                            rows, rows,
                            weight[b][0:ne, t, :].rearrange("p (h o) -> p h o", o=1).broadcast_to([ne, H, DH]),
                            ALU.mult).then_inc(weighted[b], 1)

                def slot(late, next_early):
                    p, b, g, nt, ne = late
                    logits(*late)
                    dve.wait_ge(weights_ready[b], uses(b, p, g) + 1)
                    weigh(p, b, g, 0, min(WEAVE, nt), ne)
                    if next_early:
                        early(*next_early)
                    weigh(p, b, g, WEAVE, nt, ne)

                in_turn(dve, lambda p: None, early, slot)

            @block.scalar
            def _(act):
                for b in range(2):
                    act.sem_inc(flushed[b], 1)

                def start_pass(p):
                    act.wait_ge(added, 16 * (groups(0, p, 0) + 2))

                def exponentials(p, b, g, nt, ne):
                    act.wait_ge(logits_ready[b], uses(b, p, g) + 2)
                    nc.scalar.activation(weight[b][0:ne, 0:nt, :], shifted[b][0:ne, 0:nt, :],
                                         ACT.Exp).then_inc(weights_ready[b], 1)

                def slot(late, next_early):
                    if next_early:
                        exponentials(*next_early)
                    p, b, g, nt, ne = late
                    act.wait_ge(summed[b], tiles(b, p, g) + nt + TG)
                    act.wait_ge(added, 16 * (groups(b, p, g) + 1))
                    nc.scalar.activation(flush[b][:, 0:D], psN[b][:, :], ACT.Copy)
                    nc.scalar.activation(flush[b][:, D:ROW], psD[b][:, 0:H], ACT.Copy).then_inc(flushed[b], 1)

                in_turn(act, start_pass, exponentials, slot)

            @block.tensor
            def _(pe):
                for b in range(2):
                    pe.sem_inc(summed[b], TG)

                def early(p, b, g, nt, ne):
                    pe.wait_ge(onehots_ready[b], uses(b, p, g) + 1)
                    for t in range(nt):
                        last = nc.tensor.matmul(psS[b][0:ne, t * 2 * H:(t + 1) * 2 * H],
                                                onehot_T[b][:, t * ne:(t + 1) * ne],
                                                window[b][:, 0:2 * H], start=True, stop=True)
                    last.then_inc(scored, 1)

                def sum_up(p, b, g, t0, t1, nt, ne):
                    for t in range(t0, t1):
                        pe.wait_ge(weighted[b], tiles(b, p, g) + t + 1)
                        nc.tensor.matmul(psN[b][:, :], onehot[b][0:ne, t, :], G[b][0:ne, t, 0:D],
                                         start=(t == 0), stop=(t == nt - 1))
                        nc.tensor.matmul(psD[b][:, 0:H], onehot[b][0:ne, t, :], weight[b][0:ne, t, :],
                                         start=(t == 0), stop=(t == nt - 1)).then_inc(summed[b], 1)

                def slot(late, next_early):
                    p, b, g, nt, ne = late
                    pe.wait_ge(flushed[b], uses(b, p, g) + 1)
                    sum_up(p, b, g, 0, min(WEAVE_PE, nt), nt, ne)
                    if next_early:
                        early(*next_early)
                    sum_up(p, b, g, WEAVE_PE, nt, nt, ne)

                in_turn(pe, lambda p: None, early, slot)


def project_heads(nc, sem, bank, X, S, ident, sums, QT, KT, V, ln_g, ln_b, Wq, Wk, Wv, qn_g, kn_g):
    ctx = ExitStack()
    with ctx:
        def sb(name, shape, dt=F32):
            return ctx.enter_context(nc.sbuf_tensor(name, shape, dt))

        stats = [sb(f"ln_stats{b}", [P, 6]) for b in range(2)]
        mean_var = [sb(f"ln_mean_var{b}", [P, 2]) for b in range(2)]
        rstd = [sb(f"ln_rstd{b}", [P, 1]) for b in range(2)]
        eps = sb("ln_eps", [P, 2])
        g_col, b_col = sb("ln_g_col", [P, KC]), sb("ln_b_col", [P, KC])
        qn_col, kn_col = sb("qn_col", [P, 1]), sb("kn_col", [P, 1])
        stage = [sb(f"w_stage{i}", [P, KC, D]) for i in range(2)]
        W_hi = [sb(f"Wqkv_hi{m}", [P, KC, D], F32R) for m in range(3)]
        W_lo = [sb(f"Wqkv_lo{m}", [P, KC, D], F32R) for m in range(3)]
        Hn = [sb(f"qkv_Hn{b}", [P, D]) for b in range(2)]
        HT = [sb(f"qkv_HT{b}", [P, KC, P]) for b in range(2)]
        HT_hi = [sb(f"qkv_HT_hi{b}", [P, KC, P], F32R) for b in range(2)]
        HT_lo = [sb(f"qkv_HT_lo{b}", [P, KC, P], F32R) for b in range(2)]
        x1 = [sb(f"x1_{b}", [P, D]) for b in range(2)]
        length = [sb(f"length{b}", [P, 2, H]) for b in range(2)]
        unit = [[sb(f"qk_unit{b}{m}", [P, D]) for m in range(2)] for b in range(2)]
        square = unit

        sums_loaded, cols_loaded = [sem(f"sums_loaded{i}") for i in range(2)], sem("cols_loaded")
        w_loaded = [sem(f"wqkv_loaded{m}") for m in range(3)]
        own = sem("heads_vector_own")
        var_ready, root_ready = sem("ln_var_ready"), sem("ln_root_ready")
        w_hi_ready, w_lo_ready = sem("wqkv_hi_ready"), sem("wqkv_lo_ready")
        normed_ready = sem("ln_normed_ready")
        transposed, affine, hi_ready, lo_ready = (sem("qkv_transposed"), sem("qkv_affine"), sem("qkv_hi_ready"),
                                                  sem("qkv_lo_ready"))
        projected, squared, reduced, rooted = sem("qkv_projected"), sem("squared"), sem("reduced"), sem("rooted")
        scaled, v_read, qk_transposed, stored = sem("qk_scaled"), sem("v_read"), sem("qk_transposed"), sem("qk_stored")
        loop_own, loop_prepare = sem("qkv_vector_own"), sem("prepare_vector_own")
        vector_turn, first_lo_ready = sem("vector_turn"), sem("first_lo_ready")
        x1_ready, x_kept = sem("x1_ready"), sem("x_kept")

        psT = bank[0]
        psP = [[bank[1], bank[2], bank[3]], [bank[4], bank[5], bank[6]]]
        psX = [[bank[7], bank[3]], [bank[7], bank[6]]]
        chunks = lambda ps: ps[:, :].rearrange("p (c n) -> p c n", c=KC)

        with nc.Block() as block:
            @block.sync
            def _(sp):
                for m, w in enumerate((Wv, Wk, Wq)):
                    if m == 2:
                        sp.wait_ge(first_lo_ready, 1)
                    sp.dma_start(stage[m % 2][:, :, :], w.rearrange("(c p) n -> p c n", p=P)).then_inc(w_loaded[m], 16)

            @block.gpsimd
            def _(pool):
                for col, vec in ((g_col, ln_g), (b_col, ln_b)):
                    pool.dma_start(col[:, :], vec.rearrange("(c p) -> p c", p=P),
                                   allow_slow_non_contiguous=True).then_inc(cols_loaded, 16)
                for col, vec in ((qn_col, qn_g), (kn_col, kn_g)):
                    for half in range(2):
                        pool.dma_start(col[half * DH:(half + 1) * DH, :],
                                     vec.rearrange("(p o) -> p o", o=1)).then_inc(cols_loaded, 16)

                def keep(t, b):
                    pool.wait_ge(x1_ready, t + 1)
                    nc.gpsimd.tensor_copy(X[:, bass.ds(t, 1), :].rearrange("p o d -> p (o d)"), x1[b][:, :]).then_inc(x_kept, 1)

                keep(0, 0)
                keep(1, 1)
                for m in range(1, 3):
                    pool.wait_ge(w_hi_ready, m + 1)
                    nc.gpsimd.tensor_tensor(W_lo[m][:, :, :], stage[m % 2][:, :, :], W_hi[m][:, :, :].bitcast(F32),
                                            ALU.subtract).then_inc(w_lo_ready, 1)
                with pool.Fori(1, NT // 2) as j:
                    for b in range(2):
                        keep(2 * j + b, b)

            @block.scalar
            def _(act):
                for part, (t0, t1) in enumerate(((0, 2), (2, NT))):
                    act.dma_start(S[:, t0:t1, :], sums[t0 * P:t1 * P, :].rearrange("(t p) r -> p t r", p=P)).then_inc(sums_loaded[part], 16)

                def high_weights(m):
                    act.wait_ge(w_loaded[m], 16)
                    nc.scalar.activation(W_hi[m][:, :, :], stage[m % 2][:, :, :], ACT.Copy).then_inc(w_hi_ready, 1)

                def root(t, b):
                    act.wait_ge(var_ready, t + 1)
                    nc.scalar.activation(rstd[b][:, :], mean_var[b][:, 1:2], ACT.Sqrt,
                                         bias=eps[:, 0:1], scale=1.0 + EPS).then_inc(root_ready, 1)

                def transposed_parts(t, b):
                    act.wait_ge(transposed, t + 1)
                    for c in range(KC):
                        last = nc.scalar.activation(HT[b][:, c, :], chunks(psT)[:, c, :], ACT.Identity,
                                                    bias=b_col[:, c:c + 1], scale=g_col[:, c:c + 1])
                    last.then_inc(affine, 1)
                    act.wait_ge(affine, t + 1)
                    nc.scalar.activation(HT_hi[b][:, :, :], HT[b][:, :, :], ACT.Copy).then_inc(hi_ready, 1)

                def results(t, b):
                    act.wait_ge(projected, 3 * t + 1)
                    nc.scalar.activation(V[:, bass.ds(t, 1), :].rearrange("p o d -> p (o d)"), psP[b][0][:, :], ACT.Copy).then_inc(v_read, 1)
                    for m in range(2):
                        act.wait_ge(projected, 3 * t + m + 2)
                        nc.scalar.activation(square[b][m][:, :], psP[b][m + 1][:, :], ACT.Square).then_inc(squared, 1)

                def lengths(t, b):
                    act.wait_ge(reduced, 2 * t + 2)
                    nc.scalar.activation(length[b][:, :, :], length[b][:, :, :], ACT.Sqrt, bias=eps[:, 1:2]).then_inc(rooted, 1)

                def pair(j, first, last):
                    for b in range(2):
                        t = 2 * j + b
                        if not last:
                            root(t + 2, b)
                        if not (first and b == 0):
                            lengths(t - 1, 1 - b)
                        results(t, b)
                        if not last:
                            transposed_parts(t + 2, b)

                root(0, 0)
                root(1, 1)
                high_weights(0)
                act.wait_ge(cols_loaded, 16 * 6)
                for b in range(2):
                    transposed_parts(b, b)
                high_weights(1)
                high_weights(2)
                pair(0, True, False)
                with act.Fori(1, NT // 2 - 1) as j:
                    pair(j, False, False)
                pair(NT // 2 - 1, False, True)
                lengths(NT - 1, 1)

            @block.vector
            def _(dve):
                step = Chain(dve, own)
                nc.vector.memset(eps[:, 0:1], EPS * EPS)
                step(nc.vector.memset(eps[:, 1:2], 1e-12))

                def invert_sums(t0, t1):
                    step(nc.vector.tensor_scalar(S[:, t0:t1, D:ROW], S[:, t0:t1, D:ROW], TINY, None, ALU.max))
                    step(nc.vector.reciprocal(S[:, t0:t1, D:ROW], S[:, t0:t1, D:ROW]))

                def prepare(t, b):
                    step = Chain(dve, loop_prepare, 4 * t)
                    rows = S[:, bass.ds(t, 1), 0:D].rearrange("p o d -> p (o d)")
                    tile = X[:, bass.ds(t, 1), :].rearrange("p o d -> p (o d)")
                    by_head = rows.rearrange("p (h d) -> p h d", h=H)
                    inverse = S[:, bass.ds(t, 1), D:ROW].rearrange("p o (h i) -> p (o h) i", i=1)
                    step(nc.vector.tensor_tensor(by_head, by_head, inverse.broadcast_to([P, H, DH]), ALU.mult))
                    if not (isinstance(t, int) and t < 2):
                        dve.wait_ge(x_kept, t - 1)
                    step(nc.vector.tensor_tensor(x1[b][:, :], tile, rows, ALU.add))
                    dve.sem_inc(x1_ready, 1)
                    step(nc.vector.bn_stats(stats[b][:, :], x1[b][:, :]))
                    dve.sem_inc(vector_turn, 1)
                    nc.vector.bn_aggr(mean_var[b][:, :], stats[b][:, :]).then_inc(var_ready, 1)
                    dve.wait_ge(root_ready, t + 1)
                    step(nc.vector.reciprocal(rstd[b][:, :], rstd[b][:, :]))

                def norm(t, b):
                    nc.vector.tensor_scalar(Hn[b][:, :], x1[b][:, :], mean_var[b][:, 0:1], rstd[b][:, 0:1],
                                            ALU.subtract, ALU.mult).then_inc(normed_ready, 1)

                def low_part(t, b):
                    dve.wait_ge(hi_ready, t + 1)
                    nc.vector.tensor_tensor(HT_lo[b][:, :, :], HT[b][:, :, :], HT_hi[b][:, :, :].bitcast(F32),
                                            ALU.subtract).then_inc(lo_ready, 1)

                def scale(t, b):
                    for m in range(2):
                        dve.wait_ge(squared, 2 * t + m + 1)
                        nc.vector.tensor_reduce(length[b][:, m, :], square[b][m][:, :].rearrange("p (h d) -> p h d", h=H),
                                                X_AXIS, ALU.add).then_inc(reduced, 1)
                    dve.wait_ge(rooted, t + 1)
                    nc.vector.reciprocal(length[b][:, :, :], length[b][:, :, :]).then_inc(loop_own, 1)
                    dve.wait_ge(loop_own, t + 1)
                    for m in range(2):
                        nc.vector.tensor_tensor(
                            unit[b][m][:, :].rearrange("p (h d) -> p h d", h=H),
                            psP[b][m + 1][:, :].rearrange("p (h d) -> p h d", h=H),
                            length[b][:, m, :].rearrange("p (h o) -> p h o", o=1).broadcast_to([P, H, DH]),
                            ALU.mult).then_inc(scaled, 1)

                def store(t, b):
                    for m, (out, col) in enumerate(((QT, qn_col), (KT, kn_col))):
                        dve.wait_ge(qk_transposed, 2 * t + m + 1)
                        nc.vector.tensor_scalar(out[:, :, bass.ds(t * P, P)], chunks(psX[b][m]), col[:, 0:1], None,
                                                ALU.mult).then_inc(stored, 1)

                def pair(j, first, last):
                    for b in range(2):
                        t = 2 * j + b
                        if not last:
                            prepare(t + 2, b)
                            norm(t + 2, b)
                        if not (first and b == 0):
                            scale(t - 1, 1 - b)
                        if not last:
                            low_part(t + 2, b)
                        if not (first and b == 0):
                            store(t - 1, 1 - b)

                dve.wait_ge(sums_loaded[0], 16)
                invert_sums(0, 2)
                for b in range(2):
                    prepare(b, b)
                    norm(b, b)
                dve.wait_ge(w_hi_ready, 1)
                nc.vector.tensor_tensor(W_lo[0][:, :, :], stage[0][:, :, :], W_hi[0][:, :, :].bitcast(F32),
                                        ALU.subtract).then_inc(first_lo_ready, 1)
                for b in range(2):
                    low_part(b, b)
                dve.wait_ge(sums_loaded[1], 16)
                invert_sums(2, NT)
                dve.wait_ge(cols_loaded, 16 * 6)
                step(nc.vector.tensor_scalar(qn_col[:, :], qn_col[:, :], float(DH) ** 0.5, None, ALU.mult))
                pair(0, True, False)
                with dve.Fori(1, NT // 2 - 1) as j:
                    pair(j, False, False)
                pair(NT // 2 - 1, False, True)
                scale(NT - 1, 1)
                store(NT - 1, 1)

            @block.tensor
            def _(pe):
                def transpose(t, b):
                    pe.wait_ge(normed_ready, t + 1)
                    if not (isinstance(t, int) and t == 0):
                        pe.wait_ge(affine, t)
                    for c in range(KC):
                        last = nc.tensor.transpose(psT[:, c * P:(c + 1) * P], Hn[b][:, c * P:(c + 1) * P], ident[:, :])
                    last.then_inc(transposed, 1)

                def project(t, b, first):
                    pe.wait_ge(lo_ready, t + 1)
                    if not first:
                        pe.wait_ge(v_read, t - 1)
                    for m in range(3):
                        if first and b == 0 and m == 0:
                            pe.wait_ge(first_lo_ready, 1)
                        elif first and b == 0:
                            pe.wait_ge(w_lo_ready, m)
                        if not first and m == 2:
                            pe.wait_ge(stored, 2 * t - 2)
                        for n, (h, w) in enumerate(((HT_hi, W_hi), (HT_hi, W_lo), (HT_lo, W_hi))):
                            for c in range(KC):
                                last = nc.tensor.matmul(psP[b][m][:, :], h[b][:, c, :], w[m][:, c, :],
                                                        start=(n == 0 and c == 0), stop=(n == 2 and c == KC - 1))
                        last.then_inc(projected, 1)

                def transpose_heads(t, b):
                    for m in range(2):
                        pe.wait_ge(scaled, 2 * t + 2 - m)
                        if m == 0 and not (isinstance(t, int) and t == 0):
                            pe.wait_ge(stored, 2 * t - 1)
                        for c in range(KC):
                            last = nc.tensor.transpose(psX[b][m][:, c * P:(c + 1) * P], unit[b][1 - m][:, c * P:(c + 1) * P], ident[:, :])
                        last.then_inc(qk_transposed, 1)

                def pair(j, first, last):
                    for b in range(2):
                        t = 2 * j + b
                        project(t, b, first)
                        if not last:
                            transpose(t + 2, b)
                        if not (first and b == 0):
                            transpose_heads(t - 1, 1 - b)

                for b in range(2):
                    transpose(b, b)
                pair(0, True, False)
                with pe.Fori(1, NT // 2 - 1) as j:
                    pair(j, False, False)
                pair(NT // 2 - 1, False, True)
                transpose_heads(NT - 1, 1)


def attend(nc, sem, psum, ident, QT, KT, V, OT, weight_sums, sums_row):
    ctx = ExitStack()
    with ctx:
        def sb(name, shape, dt=F32):
            return ctx.enter_context(nc.sbuf_tensor(name, shape, dt))

        CQ = 4
        CHUNKS = [range(c, min(c + CQ, NT)) for c in range(0, NT, CQ)]
        REGION = 1024
        PIECES = [(c, i, k0, min(k0 + REGION, (i + 1) * P))
                  for c, tiles in enumerate(CHUNKS) for i in tiles for k0 in range(0, (i + 1) * P, REGION)]
        KEYS = [tiles[-1] + 1 for tiles in CHUNKS]
        NC, NPC, NK = len(CHUNKS), len(PIECES), sum(KEYS)
        assert NPC % 2 == 0 and NK % 2 == 0
        FREE = 2 * NC

        Q = [sb(f"Qs{b}", [P, NP], F32R) for b in range(2)]
        K_hi = [sb(f"K_hi{b}", [P, NP], F32R) for b in range(2)]
        K_lo = [sb(f"K_lo{b}", [P, NP], F32R) for b in range(2)]
        Vs = [sb(f"Vs{b}", [P, NT, P]) for b in range(2)]
        width = [max(len(tiles) for tiles in CHUNKS if k <= tiles[-1]) * P for k in range(NT)]
        PT = [[sb(f"PT{i}_{k}", [P, width[k]]) for k in range(NT)] for i in range(2)]
        sum_rows = sb("sum_rows", [P, KC, NP])
        ident_b = sb("ident_b", [P, P], BF16)
        mask_q = sb("mask_q", [P, P], BF16)
        mask_k = sb("mask_k", [P, P], BF16)
        ones = sb("ones8", [2 * CQ, P], F32R)
        blocks = sb("blocks", [2 * CQ, CQ, P])
        part = sb("part_max", [P, 2])
        neg_max = sb("neg_max", [P, CQ])
        max_parts = sb("max_parts", [P, 2 * CQ], F32R)
        M = sb("max_row", [2 * CQ, CQ, P], F32R)

        masks_cleared, masks_ready = sem("masks_cleared"), sem("masks_ready")
        hi_staged, lo_staged, staged = sem("hi_staged"), sem("lo_staged"), sem("staged")
        scores_ready, maxed, max_split, max_transposed, max_ready = (
            sem("scores_ready"), sem("maxed"), sem("max_split"), sem("max_transposed"), sem("max_ready"))
        keyed, weighed, attended, o_read, own = (
            sem("keyed"), sem("exp_done"), sem("attended"), sem("o_read"), sem("attend_vector_own"))
        pool_turn = sem("pool_turn")
        v_staged, sums_stored, sums_compact = sem("v_staged"), sem("sums_stored"), sem("sums_compact")

        region = [psum[:, n * REGION:(n + 1) * REGION] for n in range(2)]
        psK = [psum[:, (4 + n) * 512:(5 + n) * 512] for n in range(2)]
        psO = psum[:, 6 * 512:7 * 512]
        psM = psum[:, 7 * 512:8 * 512]

        def head(j, b):
            return 2 * j + b

        def chunk(j, b, c):
            return NC * head(j, b) + c

        def slots(j, last):
            for b in range(2):
                for c in range(NC):
                    if c + 1 < NC:
                        after = (j, b, c + 1)
                    elif b == 0:
                        after = (j, 1, 0)
                    else:
                        after = None if last else (j + 1, 0, 0)
                    yield b, c, after

        def in_turn(eng, slot):
            def pair(j, last):
                for b, c, after in slots(j, last):
                    slot(j, b, c, after, last)

            with eng.Fori(0, H // 2 - 1) as j:
                pair(j, False)
            pair(H // 2 - 1, True)

        def next_head(j, b, c, last, when):
            if c != when or (last and b == 1):
                return None
            return (j, 1) if b == 0 else (j + 1, 0)

        def halves(b):
            own_rows, other_rows = slice(b * DH, (b + 1) * DH), slice((1 - b) * DH, (2 - b) * DH)
            return own_rows, other_rows

        with nc.Block() as block:
            @block.sync
            def _(sp):
                sp.wait_ge(o_read, NC * H + 1)
                for b in range(2):
                    row = (1 - b) * DH
                    sp.dma_start(sums_row[b:b + 1, :], sum_rows[row:row + 1, :, :].rearrange("o j n -> o (j n)")).then_inc(sums_stored, 16)
                sp.wait_ge(sums_stored, 32)
                sp.dma_start(weight_sums[:, :, :], sums_row.rearrange("b (p k) -> p b k", k=SPREAD)).then_inc(sums_compact, 16)
                sp.wait_ge(sums_compact, 16)

            @block.gpsimd
            def _(pool):
                nc.gpsimd.memset(mask_q[:, :], 0.0)
                nc.gpsimd.memset(mask_k[:, :], 0.0)
                nc.gpsimd.memset(ones[:, :].bitcast(F32), 1.0)
                nc.gpsimd.memset(max_parts[:, :].bitcast(F32), 0.0)
                nc.gpsimd.tensor_copy(ident_b[:, :], ident[:, :])
                for b in range(2):
                    nc.gpsimd.memset(Vs[b][:, :, (1 - b) * DH:(2 - b) * DH], 1.0)
                nc.gpsimd.memset(blocks[:, :, :], 0.0).then_inc(masks_cleared, 1)
                pool.wait_ge(masks_cleared, 1)
                nc.gpsimd.affine_select(out=mask_q[:, :], in_=mask_q[:, :], compare_op=ALU.is_ge, fill=MASKED,
                                        base=0, pattern=[[-1, P]], channel_multiplier=1)
                nc.gpsimd.affine_select(out=mask_k[:, :], in_=mask_k[:, :], compare_op=ALU.is_ge, fill=MASKED,
                                        base=0, pattern=[[1, P]], channel_multiplier=-1)
                nc.gpsimd.affine_select(out=blocks[:, :, :], in_=blocks[:, :, :], compare_op=ALU.not_equal, fill=1.0,
                                        base=0, pattern=[[-1, CQ], [0, P]], channel_multiplier=1).then_inc(masks_cleared, 1)
                pool.wait_ge(masks_cleared, 2)
                nc.gpsimd.affine_select(out=blocks[:, :, :], in_=blocks[:, :, :], compare_op=ALU.not_equal, fill=1.0,
                                        base=-CQ, pattern=[[-1, CQ], [0, P]], channel_multiplier=1).then_inc(masks_ready, 1)

                def stage(j, b):
                    rows, others = halves(b)
                    raw = KT[rows, bass.ds(j, 1), :].rearrange("p o n -> p (o n)")
                    pool.wait_ge(attended, NC * (head(j, b) - 1) + FREE)
                    if not (isinstance(j, int) and head(j, b) == 0):
                        pool.wait_ge(staged, head(j, b))
                    nc.gpsimd.tensor_copy(Vs[b][:, :, b * DH:(b + 1) * DH], V[:, :, bass.ds(head(j, b) * DH, DH)]).then_inc(v_staged, 1)
                    pool.wait_ge(v_staged, head(j, b) + 1)
                    nc.gpsimd.tensor_copy(K_hi[b][others, :], raw)
                    pool.wait_ge(hi_staged, head(j, b) + 1)
                    pool.sem_inc(pool_turn, 1)
                    nc.gpsimd.tensor_tensor(K_lo[b][others, :], raw, K_hi[b][rows, :].bitcast(F32), ALU.subtract).then_inc(staged, 1)

                stage(0, 0)

                def slot(j, b, c, after, last):
                    if nxt := next_head(j, b, c, last, 0):
                        stage(*nxt)

                in_turn(pool, slot)

            @block.scalar
            def _(act):
                act.sem_inc(weighed, 2)
                act.sem_inc(o_read, 1)

                def stage(j, b):
                    rows, _ = halves(b)
                    chunk_j = bass.ds(j, 1)
                    act.wait_ge(attended, NC * (head(j, b) - 1) + FREE)
                    nc.scalar.activation(Q[b][rows, :], QT[rows, chunk_j, :].rearrange("p o n -> p (o n)"), ACT.Copy)
                    nc.scalar.activation(K_hi[b][rows, :], KT[rows, chunk_j, :].rearrange("p o n -> p (o n)"), ACT.Copy).then_inc(hi_staged, 1)

                stage(0, 0)

                def slot(j, b, c, after, last):
                    act.wait_ge(attended, chunk(j, b, c) - 1 + FREE)
                    for kt in range(KEYS[c]):
                        n = NK * head(j, b) + sum(KEYS[:c]) + kt
                        lo = max(kt - CHUNKS[c][0], 0) * P
                        hi = len(CHUNKS[c]) * P
                        act.wait_ge(keyed, n + 1)
                        nc.scalar.activation(PT[(NC * b + c) % 2][kt][:, lo:hi], psK[kt_bank(b, c, kt)][:, lo:hi],
                                             ACT.Exp).then_inc(weighed, 1)
                    if nxt := next_head(j, b, c, last, 0):
                        stage(*nxt)
                    n = len(CHUNKS[c]) * P
                    rows, others = halves(b)
                    q0 = CHUNKS[c][0] * P
                    act.wait_ge(attended, chunk(j, b, c) + 1 + FREE)
                    nc.scalar.activation(OT[rows, bass.ds(j, 1), q0:q0 + n].rearrange("p o n -> p (o n)"), psO[rows, 0:n], ACT.Copy)
                    one = slice(others.start, others.start + 1)
                    nc.scalar.activation(sum_rows[one, bass.ds(j, 1), q0:q0 + n].rearrange("p o n -> p (o n)"), psO[one, 0:n],
                                         ACT.Copy).then_inc(o_read, 1)

                def kt_bank(b, c, kt):
                    return (sum(KEYS[:c]) + kt) % 2

                in_turn(act, slot)

            @block.vector
            def _(dve):
                def stage(j, b):
                    rows, others = halves(b)
                    c = bass.ds(j, 1)
                    dve.wait_ge(hi_staged, head(j, b) + 1)
                    nc.vector.tensor_tensor(Q[b][others, :], QT[rows, c, :].rearrange("p o n -> p (o n)"),
                                            Q[b][rows, :].bitcast(F32), ALU.subtract)
                    nc.vector.tensor_tensor(K_lo[b][rows, :], KT[rows, c, :].rearrange("p o n -> p (o n)"),
                                            K_hi[b][rows, :].bitcast(F32), ALU.subtract).then_inc(lo_staged, 1)

                def maxima(j, b, c):
                    step = Chain(dve, own, chunk(j, b, c) + head(j, b))
                    for s, (pc, i, k0, k1) in enumerate(PIECES):
                        if pc != c:
                            continue
                        dve.wait_ge(scores_ready, NPC * head(j, b) + s + 1)
                        whole = (i + 1) * P <= REGION
                        to = neg_max[:, i - CHUNKS[c][0]:i - CHUNKS[c][0] + 1] if whole or k0 == 0 else part[:, (i % 2):(i % 2) + 1]
                        nc.vector.tensor_reduce(to, region[s % 2][:, 0:k1 - k0], X_AXIS, ALU.max,
                                                negate=True).then_inc(maxed, 1)
                    dve.wait_ge(maxed, NPC * head(j, b) + sum(x[0] <= c for x in PIECES) + 2)
                    n = len(CHUNKS[c])
                    if c == NC - 1:
                        step(nc.vector.tensor_tensor(neg_max[:, 0:n], neg_max[:, 0:n], part[:, 0:n], ALU.min))
                    step(nc.vector.tensor_copy(max_parts[:, 0:n], neg_max[:, 0:n]))
                    nc.vector.tensor_tensor(max_parts[:, CQ:CQ + n], neg_max[:, 0:n], max_parts[:, 0:n].bitcast(F32),
                                            ALU.subtract).then_inc(max_split, 1)

                def max_row(j, b, c):
                    dve.wait_ge(max_transposed, chunk(j, b, c) + 1)
                    nc.vector.tensor_tensor(M[:, :, :], psM[0:2 * CQ, 0:P].rearrange("p (o n) -> p o n", o=1).broadcast_to([2 * CQ, CQ, P]),
                                            blocks[:, :, :], ALU.mult).then_inc(max_ready, 1)

                dve.sem_inc(maxed, 2)
                dve.wait_ge(masks_ready, 1)
                stage(0, 0)
                maxima(0, 0, 0)
                max_row(0, 0, 0)

                def slot(j, b, c, after, last):
                    if nxt := next_head(j, b, c, last, 1):
                        stage(*nxt)
                    if after:
                        maxima(*after)
                        max_row(*after)
                in_turn(dve, slot)

            @block.tensor
            def _(pe):
                pe.sem_inc(attended, FREE)
                pe.wait_ge(masks_ready, 1)

                def score(j, b, s):
                    c, i, k0, k1 = PIECES[s]
                    if s == 0:
                        pe.wait_ge(lo_staged, head(j, b) + 1)
                        pe.wait_ge(staged, head(j, b) + 1)
                    pe.wait_ge(maxed, NPC * head(j, b) + s + 1)
                    q = Q[b][:, i * P:(i + 1) * P]
                    for a in range(k0, k1, 512):
                        e = min(a + 512, k1)
                        out = region[s % 2][:, a - k0:e - k0]
                        diagonal = e == (i + 1) * P
                        nc.tensor.matmul(out, q, K_hi[b][:, a:e], start=True, stop=False)
                        last = nc.tensor.matmul(out, q, K_lo[b][:, a:e], start=False, stop=not diagonal)
                        if diagonal:
                            last = nc.tensor.matmul(region[s % 2][:, e - P - k0:e - k0], ident_b[:, :], mask_q[:, :],
                                                    start=False, stop=True)
                    last.then_inc(scores_ready, 1)

                def pieces(c):
                    return [s for s, piece in enumerate(PIECES) if piece[0] == c]

                def turn_maxima(j, b, c):
                    pe.wait_ge(max_split, chunk(j, b, c) + 1)
                    nc.tensor.transpose(psM[0:2 * CQ, 0:P], max_parts[:, :].bitcast(F32), ident[:, :]).then_inc(max_transposed, 1)

                for s in pieces(0):
                    score(0, 0, s)
                turn_maxima(0, 0, 0)

                def slot(j, b, c, after, last):
                    to_do = pieces(after[2]) if after else []
                    pe.wait_ge(max_ready, chunk(j, b, c) + 1)
                    first = CHUNKS[c][0]
                    hi = len(CHUNKS[c]) * P
                    for kt in range(KEYS[c]):
                        n = NK * head(j, b) + sum(KEYS[:c]) + kt
                        lo = max(kt - first, 0) * P
                        pe.wait_ge(weighed, n + 1)
                        out = psK[(sum(KEYS[:c]) + kt) % 2]
                        q = Q[b][:, first * P + lo:first * P + hi]
                        nc.tensor.matmul(out[:, lo:hi], K_hi[b][:, kt * P:(kt + 1) * P], q, start=True, stop=False)
                        nc.tensor.matmul(out[:, lo:hi], K_lo[b][:, kt * P:(kt + 1) * P], q, start=False, stop=False)
                        if kt >= first:
                            nc.tensor.matmul(out[:, lo:lo + P], ident_b[:, :], mask_k[:, :], start=False, stop=False)
                        nc.tensor.matmul(out[:, lo:hi], ones[:, :], M[:, :, :].rearrange("p t n -> p (t n)")[:, lo:hi],
                                         start=False, stop=True).then_inc(keyed, 1)
                        for s in to_do[len(to_do) * kt // (KEYS[c] - 1):len(to_do) * (kt + 1) // (KEYS[c] - 1)]:
                            score(after[0], after[1], s)
                    pe.wait_ge(o_read, chunk(j, b, c) + 1)
                    for kt in range(KEYS[c]):
                        if after and kt == KEYS[c] - 3:
                            turn_maxima(*after)
                        lo = max(kt - first, 0) * P
                        pe.wait_ge(weighed, NK * head(j, b) + sum(KEYS[:c]) + kt + 1 + 2)
                        last = nc.tensor.matmul(psO[:, lo:hi], Vs[b][:, kt, :], PT[(NC * b + c) % 2][kt][:, lo:hi],
                                                start=(kt == 0), stop=(kt == KEYS[c] - 1))
                    last.then_inc(attended, 1)

                in_turn(pe, slot)


def combine_heads(nc, sem, psum, bank, OT, weight_sums, inverse_row, yT, logits, raw, parts, weights_loaded, weights_hi, weights_lo,
                  Wo, gate_W, gate_b, W1, W2):
    ctx = ExitStack()
    with ctx:
        def sb(name, shape, dt=F32):
            return ctx.enter_context(nc.sbuf_tensor(name, shape, dt))

        STEP = 2 * P
        NS = NP // STEP
        Wo_raw = sb("Wo_raw", [P, KC, D])
        Wo_hi, Wo_lo = sb("Wo_hi", [P, KC, D], F32R), sb("Wo_lo", [P, KC, D], F32R)
        OT_hi, OT_lo = sb("OT_hi", [P, KC, NP], F32R), sb("OT_lo", [P, KC, NP], F32R)
        inverse_rows = sb("inverse_rows", [H, NP])
        select = sb("select_head", [H, KC, P])
        gW = sb("gate_weights", [P, KC, H])
        gW_hi, gW_lo = sb("gate_hi", [P, KC, H], F32R), sb("gate_lo", [P, KC, H], F32R)
        gb_col = sb("gate_bias", [H, 1])

        wo_loaded, gate_loaded = sem("wo_loaded"), sem("gate_loaded")
        wo_hi_ready, wo_lo_ready = sem("wo_hi_ready"), sem("wo_lo_ready")
        gate_hi_ready, gate_lo_ready = sem("gate_hi_ready"), sem("gate_lo_ready")
        inverse_ready, rows_ready = sem("inverse_ready"), sem("inverse_rows_ready")
        selecting, select_ready = sem("selecting"), sem("select_ready")
        inverse_stored = sem("inverse_stored")
        spread, divided = sem("inverse_spread"), sem("o_divided")
        ot_hi_ready, ot_lo_ready = sem("ot_hi_ready"), sem("ot_lo_ready")
        y_made, y_hi_ready, y_lo_ready = sem("y_made"), sem("y_hi_ready"), sem("y_lo_ready")
        gate_turn = sem("gate_turn")
        logits_made, logits_read = sem("logits_made"), sem("logits_read")

        psI = psum[:, 0:KC * STEP].rearrange("p (c n) -> p c n", c=KC)
        psY, psL = bank[2:6], bank[6]
        yT_hi, yT_lo = yT

        def in_steps(eng, part, product, gate):
            part(0)
            part(1)
            product(0)
            with eng.Fori(1, NS - 1) as n:
                part(n + 1)
                product(n)
                gate(n - 1)
            product(NS - 1)
            gate(NS - 2)
            gate(NS - 1)

        with nc.Block() as block:
            @block.sync
            def _(sp):
                sp.dma_start(Wo_raw[:, :, :], Wo.rearrange("(c p) n -> p c n", p=P)).then_inc(wo_loaded, 16)
                sp.dma_start(gW[:, :, :], gate_W.rearrange("(c p) n -> p c n", p=P)).then_inc(gate_loaded, 16)
                sp.dma_start(gb_col[:, :], gate_b.rearrange("(p o) -> p o", o=1)).then_inc(gate_loaded, 16)
                sp.wait_ge(inverse_ready, 1)
                sp.dma_start(inverse_row.rearrange("b (p k) -> p b k", k=SPREAD), weight_sums[:, :, :]).then_inc(inverse_stored, 16)
                sp.wait_ge(inverse_stored, 16)
                sp.dma_start(inverse_rows[:, :], inverse_row.rearrange("b (j n) -> (b j) n", n=NP)).then_inc(rows_ready, 16)
                for e in range(2):
                    for w, source in enumerate((W1, W2)):
                        sp.dma_start(raw[w][e][:, :, :], source[e].rearrange("(c p) n -> p c n", p=P)).then_inc(weights_loaded[e], 16)

            @block.gpsimd
            def _(pool):
                step = Chain(pool, selecting)
                step(nc.gpsimd.memset(select[:, :, :], 0.0))
                for b in range(2):
                    half = select[:, :, b * DH:(b + 1) * DH]
                    nc.gpsimd.affine_select(out=half, in_=half, compare_op=ALU.not_equal, fill=1.0, base=-b * KC,
                                            pattern=[[-1, KC], [0, DH]], channel_multiplier=1).then_inc(select_ready, 1)
                pool.wait_ge(wo_hi_ready, 1)
                nc.gpsimd.tensor_tensor(Wo_lo[:, :, :], Wo_raw[:, :, :], Wo_hi[:, :, :].bitcast(F32),
                                        ALU.subtract).then_inc(wo_lo_ready, 1)
                for w in range(2):
                    pool.wait_ge(weights_hi, w + 1)
                    nc.gpsimd.tensor_tensor(parts[w][0][1][:, :, :], raw[w][0][:, :, :], parts[w][0][0][:, :, :].bitcast(F32),
                                            ALU.subtract).then_inc(weights_lo, 1)

            @block.scalar
            def _(act):
                act.wait_ge(wo_loaded, 16)
                nc.scalar.activation(Wo_hi[:, :, :], Wo_raw[:, :, :], ACT.Copy).then_inc(wo_hi_ready, 1)
                act.wait_ge(gate_loaded, 32)
                nc.scalar.activation(gW_hi[:, :, :], gW[:, :, :], ACT.Copy).then_inc(gate_hi_ready, 1)

                def part(n):
                    cols = bass.ds(n * STEP, STEP)
                    act.wait_ge(divided, n + 1)
                    nc.scalar.activation(OT_hi[:, :, cols], OT[:, :, cols], ACT.Copy).then_inc(ot_hi_ready, 1)

                def product(n):
                    for m in range(KC):
                        act.wait_ge(y_made, KC * n + m + 1)
                        nc.scalar.activation(yT_hi[:, m, bass.ds(n * STEP, STEP)], psY[m][:, 0:STEP], ACT.Copy).then_inc(y_hi_ready, 1)

                def gate(n):
                    act.wait_ge(logits_made, n + 1)
                    act.sem_inc(gate_turn, 1)
                    nc.scalar.activation(logits[:, bass.ds(n * STEP, STEP)], psL[0:H, 0:STEP], ACT.Identity,
                                         bias=gb_col[:, 0:1]).then_inc(logits_read, 1)

                in_steps(act, part, product, gate)
                act.wait_ge(weights_loaded[0], 32)
                for w in range(2):
                    nc.scalar.activation(parts[w][0][0][:, :, :], raw[w][0][:, :, :], ACT.Copy).then_inc(weights_hi, 1)

            @block.vector
            def _(dve):
                nc.vector.reciprocal(weight_sums[:, :, :], weight_sums[:, :, :]).then_inc(inverse_ready, 1)
                dve.wait_ge(gate_hi_ready, 1)
                nc.vector.tensor_tensor(gW_lo[:, :, :], gW[:, :, :], gW_hi[:, :, :].bitcast(F32), ALU.subtract).then_inc(gate_lo_ready, 1)

                def part(n):
                    cols = bass.ds(n * STEP, STEP)
                    dve.wait_ge(spread, n + 1)
                    nc.vector.tensor_tensor(OT[:, :, cols], psI, OT[:, :, cols], ALU.mult).then_inc(divided, 1)
                    dve.wait_ge(ot_hi_ready, n + 1)
                    nc.vector.tensor_tensor(OT_lo[:, :, cols], OT[:, :, cols], OT_hi[:, :, cols].bitcast(F32),
                                            ALU.subtract).then_inc(ot_lo_ready, 1)

                def product(n):
                    for m in range(KC):
                        dve.wait_ge(y_hi_ready, KC * n + m + 1)
                        cols = bass.ds(n * STEP, STEP)
                        nc.vector.tensor_tensor(yT_lo[:, m, cols], psY[m][:, 0:STEP], yT_hi[:, m, cols].bitcast(F32),
                                                ALU.subtract).then_inc(y_lo_ready, 1)

                in_steps(dve, part, product, lambda n: None)

            @block.tensor
            def _(pe):
                pe.sem_inc(y_lo_ready, KC)
                pe.sem_inc(logits_read, 1)

                def part(n):
                    if not (isinstance(n, int) and n == 0):
                        pe.wait_ge(divided, n)
                    for c in range(KC):
                        last = nc.tensor.matmul(psI[:, c, :], select[:, c, :], inverse_rows[:, bass.ds(n * STEP, STEP)],
                                                start=True, stop=True)
                    last.then_inc(spread, 1)

                def product(n):
                    if isinstance(n, int) and n == 0:
                        pe.wait_ge(wo_lo_ready, 1)
                    pe.wait_ge(ot_lo_ready, n + 1)
                    cols = bass.ds(n * STEP, STEP)
                    for m in range(KC):
                        pe.wait_ge(y_lo_ready, KC * n + m + 1)
                        for i, (w, o) in enumerate(((Wo_hi, OT_hi), (Wo_lo, OT_hi), (Wo_hi, OT_lo))):
                            for c in range(KC):
                                last = nc.tensor.matmul(psY[m][:, 0:STEP], w[:, c, m * P:(m + 1) * P], o[:, c, cols],
                                                        start=(i == 0 and c == 0), stop=(i == 2 and c == KC - 1))
                        last.then_inc(y_made, 1)

                def gate(n):
                    pe.wait_ge(logits_read, n + 1)
                    pe.wait_ge(y_lo_ready, KC * n + 2 * KC)
                    cols = bass.ds(n * STEP, STEP)
                    for i, (w, y) in enumerate(((gW_hi, yT_hi), (gW_lo, yT_hi), (gW_hi, yT_lo))):
                        for c in range(KC):
                            last = nc.tensor.matmul(psL[0:H, 0:STEP], w[:, c, :], y[:, c, cols],
                                                    start=(i == 0 and c == 0), stop=(i == 2 and c == KC - 1))
                    last.then_inc(logits_made, 1)

                pe.wait_ge(gate_lo_ready, 1)
                pe.wait_ge(select_ready, 2)
                pe.wait_ge(rows_ready, 16)
                in_steps(pe, part, product, gate)


def run_experts(nc, sem, bank, ident, X, yT, logits, raw, parts, weights_loaded, weights_hi, weights_lo,
                W1, b1, W2, b2):
    ctx = ExitStack()
    with ctx:
        def sb(name, shape, dt=F32):
            return ctx.enter_context(nc.sbuf_tensor(name, shape, dt))

        NE, F = W1.shape[0], W1.shape[2]
        FC = F // P
        SPANS = [(a, min(a + 512, NP)) for a in range(0, NP, 512)]
        NSP = len(SPANS)
        NB = 3
        NO = 5
        assert (NSP * FC) % NB == 0 and NT % NO == 0 and NB + NO == 8 and NE == H

        parts = [parts[w] + [[sb(f"expert_hi{w}", [P, c, n], F32R), sb(f"expert_lo{w}", [P, c, n], F32R)]]
                 for w, (c, n) in enumerate(((KC, F), (FC, D)))]
        hid = [sb(f"hid{s}", [P, FC, 512]) for s in range(NSP)]
        hid_hi, hid_lo = sb("hid_hi", [P, FC, NP], F32R), sb("hid_lo", [P, FC, NP], F32R)
        b1_col = sb("b1_col", [P, NE * FC])
        b2_rows = sb("b2_rows", [NE, D])
        gates = sb("gates", [P, NT, NE])
        reduced = sb("gate_reduced", [P, NT])
        gatesT = sb("gatesT", [NE, NP])

        biases_loaded = sem("biases_loaded")
        logits_turned, gates_ready, gates_turned, gatesT_ready = (sem("logits_turned"), sem("gates_ready"),
                                                                  sem("gates_turned"), sem("gatesT_ready"))
        own, shifted, exps_ready = sem("expert_vector_own"), sem("gates_shifted"), sem("gates_exps")
        hid_made, gelu_done, hid_hi_ready, hid_lo_ready = (sem("hid_made"), sem("gelu_done"), sem("hid_hi_ready"),
                                                           sem("hid_lo_ready"))
        gelu_turn = sem("gelu_turn")
        expert_made, mixed = sem("expert_made"), sem("mixed")

        psH, psE, psG = bank[0:NB], bank[NB:], bank[7]
        yT_hi, yT_lo = yT

        def in_pairs(eng, step):
            with eng.Fori(0, NE // 2 - 1) as j:
                for b in range(2):
                    step(2 * j + b, b, True, True)
            step(NE - 2, 0, True, False)
            step(NE - 1, 1, False, False)

        with nc.Block() as block:
            @block.sync
            def _(sp):
                sp.dma_start(b1_col[:, :], b1.rearrange("e (f p) -> p (e f)", p=P),
                             allow_slow_non_contiguous=True).then_inc(biases_loaded, 16)
                sp.dma_start(b2_rows[:, :], b2).then_inc(biases_loaded, 16)

                def step(e, b, more_hidden, more_weights):
                    if more_weights:
                        sp.wait_ge(weights_lo, 2 * e + 2)
                        for w, source in enumerate((W1, W2)):
                            sp.dma_start(raw[w][b][:, :, :],
                                         source[bass.ds(e + 2, 1)].rearrange("o (c p) n -> p (o c) n", p=P)).then_inc(weights_loaded[b], 16)

                in_pairs(sp, step)

            @block.gpsimd
            def _(pool):
                def weights(e, b):
                    for w in range(2):
                        pool.wait_ge(weights_hi, 2 * e + w + 1)
                        nc.gpsimd.tensor_tensor(parts[w][b][1][:, :, :], raw[w][b][:, :, :], parts[w][b][0][:, :, :].bitcast(F32),
                                                ALU.subtract).then_inc(weights_lo, 1)

                def hidden(e):
                    for s, (n0, n1) in enumerate(SPANS):
                        pool.wait_ge(hid_hi_ready, NSP * e + s + 1)
                        nc.gpsimd.tensor_tensor(hid_lo[:, :, n0:n1], hid[s][:, :, 0:n1 - n0], hid_hi[:, :, n0:n1].bitcast(F32),
                                                ALU.subtract).then_inc(hid_lo_ready, 1)

                weights(1, 1)
                hidden(0)

                def step(e, b, more_hidden, more_weights):
                    if more_hidden:
                        hidden(e + 1)
                    if more_weights:
                        weights(e + 2, b)

                in_pairs(pool, step)

            @block.scalar
            def _(act):
                act.sem_inc(hid_lo_ready, NSP)
                act.sem_inc(gelu_done, NB)

                def weights(e, b, j):
                    act.wait_ge(weights_loaded[b], 32 * (j + 1))
                    for w in range(2):
                        nc.scalar.activation(parts[w][b][0][:, :, :], raw[w][b][:, :, :], ACT.Copy).then_inc(weights_hi, 1)

                def hidden(e):
                    for s, (n0, n1) in enumerate(SPANS):
                        act.wait_ge(hid_lo_ready, NSP * e + s + 1)
                        for f in range(FC):
                            act.wait_ge(hid_made, NSP * FC * e + FC * s + f + 1)
                            act.sem_inc(gelu_turn, 1)
                            nc.scalar.activation(hid[s][:, f, 0:n1 - n0], psH[(FC * s + f) % NB][:, 0:n1 - n0], ACT.Gelu_apprx_tanh,
                                                 bias=b1_col[:, bass.ds(FC * e + f, 1)]).then_inc(gelu_done, 1)
                        act.wait_ge(gelu_done, NSP * FC * e + FC * s + FC + NB)
                        nc.scalar.activation(hid_hi[:, :, n0:n1], hid[s][:, :, 0:n1 - n0], ACT.Copy).then_inc(hid_hi_ready, 1)

                weights(1, 1, 0)
                act.wait_ge(shifted, 1)
                nc.scalar.activation(gates[:, :, :], gates[:, :, :], ACT.Exp).then_inc(exps_ready, 1)
                act.wait_ge(biases_loaded, 32)
                hidden(0)

                with act.Fori(0, NE // 2 - 1) as j:
                    for b in range(2):
                        hidden(2 * j + b + 1)
                        weights(2 * j + b + 2, b, j + 1)
                hidden(NE - 1)

            @block.vector
            def _(dve):
                step = Chain(dve, own)
                wide = lambda a: a[:, :].rearrange("p (t o) -> p t o", o=1).broadcast_to([P, NT, NE])
                turned = psG[:, 0:NT * NE].rearrange("p (t e) -> p t e", e=NE)
                dve.wait_ge(logits_turned, 1)
                step(nc.vector.tensor_reduce(reduced[:, :], turned, X_AXIS, ALU.max))
                nc.vector.tensor_tensor(gates[:, :, :], turned, wide(reduced), ALU.subtract).then_inc(shifted, 1)
                dve.wait_ge(exps_ready, 1)
                step(nc.vector.tensor_reduce(reduced[:, :], gates[:, :, :], X_AXIS, ALU.add))
                step(nc.vector.reciprocal(reduced[:, :], reduced[:, :]))
                nc.vector.tensor_tensor(gates[:, :, :], gates[:, :, :], wide(reduced), ALU.mult).then_inc(gates_ready, 1)
                dve.wait_ge(gates_ready, 1)
                for s, (n0, n1) in enumerate(SPANS):
                    dve.wait_ge(gates_turned, s + 1)
                    nc.vector.tensor_copy(gatesT[:, n0:n1], psE[s][0:NE, 0:n1 - n0]).then_inc(gatesT_ready, 1)
                for t in range(NT):
                    dve.wait_ge(expert_made, t + 1)
                    nc.vector.tensor_tensor(X[:, t, :], psE[t % NO][:, :], X[:, t, :], ALU.add).then_inc(mixed, 1)

                def mix(e, b, more_hidden, more_weights):
                    for t in range(NT):
                        dve.wait_ge(expert_made, NT * (e + 1) + t + 1)
                        dve.wait_ge(mixed, NT * e + t + 1)
                        nc.vector.scalar_tensor_tensor(X[:, t, :], psE[t % NO][:, :], gates[:, t, bass.ds(e, 1)], X[:, t, :],
                                                       ALU.mult, ALU.add).then_inc(mixed, 1)

                in_pairs(dve, mix)

            @block.tensor
            def _(pe):
                for t in range(NT):
                    last = nc.tensor.transpose(psG[:, t * NE:(t + 1) * NE], logits[:, t * P:(t + 1) * P], ident[0:NE, 0:NE])
                last.then_inc(logits_turned, 1)

                def hidden(e, b):
                    pe.wait_ge(weights_lo, 2 * e + 1)
                    for s, (n0, n1) in enumerate(SPANS):
                        for f in range(FC):
                            pe.wait_ge(gelu_done, NSP * FC * e + FC * s + f + 1)
                            w_hi, w_lo = parts[0][b]
                            for i, (w, y) in enumerate(((w_hi, yT_hi), (w_lo, yT_hi), (w_hi, yT_lo))):
                                for c in range(KC):
                                    last = nc.tensor.matmul(psH[(FC * s + f) % NB][:, 0:n1 - n0], w[:, c, f * P:(f + 1) * P],
                                                            y[:, c, n0:n1], start=(i == 0 and c == 0), stop=(i == 2 and c == KC - 1))
                            last.then_inc(hid_made, 1)

                def result(e, b):
                    pe.wait_ge(weights_lo, 2 * e + 2)
                    for t in range(NT):
                        pe.wait_ge(hid_lo_ready, NSP * e + t * P // 512 + 1 + NSP)
                        pe.wait_ge(mixed, NT * (e + 1) + t + 1 - NO)
                        w_hi, w_lo = parts[1][b]
                        rows = slice(t * P, (t + 1) * P)
                        for i, (h, w) in enumerate(((hid_hi, w_hi), (hid_hi, w_lo), (hid_lo, w_hi))):
                            for f in range(FC):
                                last = nc.tensor.matmul(psE[t % NO][:, :], h[:, f, rows], w[:, f, :],
                                                        start=(i == 0 and f == 0), stop=(i == 2 and f == FC - 1))
                        last.then_inc(expert_made, 1)

                hidden(0, 0)
                pe.wait_ge(gates_ready, 1)
                for s, (n0, n1) in enumerate(SPANS):
                    for t in range(n0 // P, n1 // P):
                        last = nc.tensor.transpose(psE[s][0:NE, t * P - n0:(t + 1) * P - n0], gates[:, t, :], ident[:, :])
                    last.then_inc(gates_turned, 1)
                pe.wait_ge(biases_loaded, 32)
                pe.wait_ge(gatesT_ready, NSP)
                for t in range(NT):
                    if t >= NO:
                        pe.wait_ge(mixed, t + 1 - NO)
                    nc.tensor.matmul(psE[t % NO][:, :], gatesT[:, t * P:(t + 1) * P], b2_rows[:, :],
                                     start=True, stop=True).then_inc(expert_made, 1)

                def step(e, b, more_hidden, more_weights):
                    result(e, b)
                    if more_hidden:
                        hidden(e + 1, 1 - b)

                in_pairs(pe, step)


def store_out(nc, sem, X, out):
    stored = sem("stored")
    with nc.Block() as block:
        @block.sync
        def _(sp):
            sp.dma_start(out[0:(NT - 1) * P, :].rearrange("(t p) d -> p t d", p=P), X[:, 0:NT - 1, :]).then_inc(stored, 16)
            sp.dma_start(out[(NT - 1) * P:N, :], X[0:N - (NT - 1) * P, NT - 1, :]).then_inc(stored, 16)
            sp.wait_ge(stored, 32)


_INS = ['x', 'src', 'dst', 'L0_gnn_Ws', 'L0_gnn_Wb', 'L0_gnn_a_w', 'L0_gnn_a_b', 'L0_ffn_ln_g', 'L0_ffn_ln_b',
        'L0_ffn_Wq', 'L0_ffn_Wk', 'L0_ffn_Wv', 'L0_ffn_Wo', 'L0_ffn_qn_g', 'L0_ffn_kn_g', 'L0_ffn_gate_W',
        'L0_ffn_gate_b', 'L0_ffn_W1', 'L0_ffn_b1', 'L0_ffn_W2', 'L0_ffn_b2']


def kernel(**inputs):
    import numpy as _np
    import concourse.bacc as _bacc
    from concourse import mybir as _mybir
    from concourse.bass_utils import run_bass_kernel_spmd as _run

    nc = _bacc.Bacc("TRN2", target_bir_lowering=False, num_devices=1)
    arrays, args = {}, []
    for name in _INS:
        a = _np.ascontiguousarray(inputs[name])
        arrays[f"in_{name}_dram"] = a
        args.append(nc.dram_tensor(f"in_{name}_dram", a.shape, _mybir.dt.from_np(a.dtype), kind="ExternalInput").ap())
    args.append(nc.dram_tensor("out_0_dram", (1250, 512), _mybir.dt.float32, kind="ExternalOutput").ap())
    build(nc, *args)
    r = _run(nc, [arrays], core_ids=[0])
    return r.results[0]["out_0_dram"]
```

```python
import concourse.bass as bass
from concourse import mybir
from contextlib import ExitStack

F32 = mybir.dt.float32
F32R = mybir.dt.float32r
I32 = mybir.dt.int32
BF16 = mybir.dt.bfloat16
ALU = mybir.AluOpType
ACT = mybir.ActivationFunctionType
X_AXIS = mybir.AxisListType.X
XY_AXES = mybir.AxisListType.XY
RMAX = bass.bass_isa.ReduceOp.max

P = 128
N = 1250
NT = -(-N // P)
NP = NT * P
D = 512
KC = D // P
H = 8
DH = D // H
E = 20000
TG = 13
GE = TG * P
NG = E // GE
TAIL = E - NG * GE
ROW = D + H
SROW = D + 2 * H
WR = 24
WROWS = NP + P
TINY = 1e-37
RANGE = 50.0
EPS = 1e-5
SPREAD = KC * NP // P
MASKED = -1e30


class Chain:

    def __init__(self, eng, sem, base=0):
        self.eng, self.sem, self.base, self.n = eng, sem, base, 0

    def __call__(self, ins):
        self.n += 1
        ins.then_inc(self.sem, 1)
        self.eng.wait_ge(self.sem, self.base + self.n)


def build(nc, x, src, dst, Ws, Wb, a_w, a_b, ln_g, ln_b, Wq, Wk, Wv, Wo, qn_g, kn_g,
          gate_W, gate_b, W1, b1, W2, b2, out):
    ctx = ExitStack()
    with ctx:
        def sb(name, shape, dt=F32):
            return ctx.enter_context(nc.sbuf_tensor(name, shape, dt))

        def sem(name):
            return ctx.enter_context(nc.semaphore(name))

        psum = ctx.enter_context(nc.psum_tensor("psum", [P, 8 * 512], F32))
        bank = [psum[:, i * 512:(i + 1) * 512] for i in range(8)]
        source_table = nc.dram_tensor("source_table", [NP, ROW], F32, kind="Internal").ap()
        window_table = nc.dram_tensor("window_table", [WROWS, WR], F32, kind="Internal").ap()
        node_numbers = nc.dram_tensor("node_numbers", [1, WROWS], F32, kind="Internal").ap()
        sums = nc.dram_tensor("sums", [WROWS, SROW], F32, kind="Internal").ap()

        sums_row = nc.dram_tensor("sums_row", [2, KC * NP], F32, kind="Internal").ap()
        inverse_row = nc.dram_tensor("inverse_row", [2, KC * NP], F32, kind="Internal").ap()
        X = sb("X", [P, NT, D])
        ident = sb("ident", [P, P])
        bases = sb("bases", [1, NT * (NG + 1)], I32)
        passes = sb("passes", [1, 1], I32)
        wide_range = sb("wide_range", [1, 1], I32)
        scores = sb("scores", [P, NT, 2 * H])
        window = sb("window", [P, NT + 1, WR])
        added = sem("added")
        carrier = sem("carrier")
        weights_ahead = sb("weights_ahead", [P, KC, D])
        columns = [sb(name, [P, n]) for name, n in (("ln_g_col", KC), ("ln_b_col", KC), ("qn_col", 1), ("kn_col", 1))]
        cols_loaded = sem("cols_loaded")
        wv_loaded, wo_loaded = sem("wv_loaded"), sem("wo_loaded")

        project_nodes(nc, sem, bank, X, ident, bases, passes, wide_range, scores, window, source_table,
                      window_table, node_numbers, sums, added, x, dst, Ws, Wb, a_w, a_b)
        find_maxima(nc, sem, carrier, psum, ident, wide_range, scores, window, source_table, window_table, src, dst)
        sum_edges(nc, sem, bank, bases, passes, source_table, window_table, node_numbers,
                  sums, added, carrier, weights_ahead, wv_loaded, Wv, columns, cols_loaded,
                  (ln_g, ln_b, qn_g, kn_g), src, dst)
        room = sb("sums_then_results", [P, NT * SROW])
        S = room[:, :].rearrange("p (t r) -> p t r", r=SROW)
        OT = room[:, 0:KC * NP].rearrange("p (c n) -> p c n", c=KC)
        weight_sums = sb("weight_sums", [P, 2, SPREAD])
        with ExitStack() as heads:
            QT, KT = (heads.enter_context(nc.sbuf_tensor(name, [P, KC, NP], F32)) for name in ("QT", "KT"))
            V = heads.enter_context(nc.sbuf_tensor("V", [P, NT, D], F32))
            project_heads(nc, sem, carrier, bank, X, S, ident, sums, QT, KT, V, weights_ahead,
                          wv_loaded, columns, cols_loaded, Wq, Wk)
            attend(nc, sem, psum, ident, QT, KT, V, OT, weight_sums, sums_row, weights_ahead, wo_loaded, Wo)

        F = W1.shape[2]
        yT = [sb(name, [P, KC, NP], F32R) for name in ("yT_hi", "yT_lo")]
        logits = sb("logits", [H, NP])
        raw = [[sb(f"expert_raw{w}{b}", [P, c, n]) for b in range(2)] for w, (c, n) in enumerate(((KC, F), (F // P, D)))]
        parts = [[[sb(f"expert_{part}{w}", [P, c, n], F32R) for part in ("first_hi", "first_lo")]]
                 for w, (c, n) in enumerate(((KC, F), (F // P, D)))]
        weights_loaded = [sem(f"expert_loaded{b}") for b in range(2)]
        weights_hi, weights_lo = sem("expert_weights_hi"), sem("expert_weights_lo")
        combine_heads(nc, sem, carrier, psum, bank, OT, weight_sums, inverse_row, yT, logits, raw, parts, weights_loaded, weights_hi, weights_lo,
                      weights_ahead, wo_loaded, gate_W, gate_b, W1, W2)
        run_experts(nc, sem, carrier, bank, ident, X, yT, logits, raw, parts, weights_loaded, weights_hi, weights_lo,
                    W1, b1, W2, b2, out)


def project_nodes(nc, sem, bank, X, ident, bases, passes, wide_range, scores, window, source_table,
                  window_table, node_numbers, sums, added, x, dst, Ws, Wb, a_w, a_b):
    ctx = ExitStack()
    with ctx:
        def sb(name, shape, dt=F32):
            return ctx.enter_context(nc.sbuf_tensor(name, shape, dt))

        W = sb("W", [P, KC, D])
        W_hi, W_lo = sb("W_hi", [P, KC, D], F32R), sb("W_lo", [P, KC, D], F32R)
        Wa = sb("Wa", [P, KC, 2 * H])
        Wa_hi, Wa_lo = sb("Wa_hi", [P, KC, 2 * H], F32R), sb("Wa_lo", [P, KC, 2 * H], F32R)
        a_row = sb("a_row", [P, H, 2 * DH])
        ab_row = sb("ab_row", [P, H])
        Wb_row = sb("Wb_row", [P, D])
        score_bias = sb("score_bias", [P, 2 * H])
        product = [sb(f"product{i}", [P, KC * D]) for i in range(2)]
        stats = sb("stats", [P, NT, 6])
        mean_var = sb("mean_var", [P, NT, 2])
        rstd = sb("rstd", [P, NT])
        eps = sb("eps", [P, 1])
        Hn = [sb(f"Hn{b}", [P, D]) for b in range(2)]
        HT_hi = [sb(f"HT_hi{b}", [P, KC, P], F32R) for b in range(2)]
        HT_lo = [sb(f"HT_lo{b}", [P, KC, P], F32R) for b in range(2)]
        row = [sb(f"row{b}", [P, ROW]) for b in range(2)]
        bound = sb("bound", [P, 2 * H])
        bound_all = sb("bound_all", [P, 2 * H])
        zeros = sb("zeros", [P, NT * SROW])
        numbers = sb("numbers", [1, WROWS])
        dst_all = sb("dst_all", [P, NG, TG], I32)
        dst_tail = sb("dst_tail", [TAIL, 1], I32)
        first = sb("first", [P, NG + 1], I32)
        off = sb("off", [P, NG, TG])
        off_tail = sb("off_tail", [TAIL, 1])
        outside = sb("outside", [P, 2])
        outside_all = sb("outside_all", [P, 2])
        bad = sb("bad", [1, 4])
        base_f = sb("base_f", [1, NT, NG + 1])
        tile_base = sb("tile_base", [1, NT, NG + 1])
        first_f = sb("first_f", [1, NG + 1])

        x_loaded = [sem(f"x_loaded{i}") for i in range(2)]
        w_loaded = sem("w_loaded")
        dst_loaded = sem("dst_loaded")
        pad_cleared = sem("pad_cleared")
        ident_ready = sem("ident_ready")
        numbers_ready = sem("numbers_ready")
        zeros_ready = sem("zeros_ready")
        var_ready = sem("var_ready")
        root_ready = sem("root_ready")
        weights_ready = sem("weights_ready")
        w_hi_ready, w_lo_ready, product_ready = sem("w_hi_ready"), sem("w_lo_ready"), sem("source_product_ready")
        tile_base_ready = sem("tile_base_ready")
        normed = sem("normed")
        transposed = sem("transposed")
        hi_ready = sem("hi_ready")
        lo_ready = sem("lo_ready")
        projected = sem("projected")
        row_ready = sem("row_ready")
        row_stored = [sem(f"row_stored{b}") for b in range(2)]
        own = sem("project_vector_own")
        bound_ready = sem("bound_ready")
        bound_reduced = sem("bound_reduced")
        outside_ready = sem("outside_ready")
        outside_reduced = sem("outside_reduced")
        window_ready = sem("window_ready")
        tables_stored = sem("tables_stored")

        LAST = N - (NT - 1) * P
        psT = [bank[0], bank[1]]
        psW = [bank[2], bank[3]]
        psS = [bank[4], bank[5]]
        W_LOADS = H + 3

        def flag_windows(dve, step):
            dve.wait_ge(dst_loaded, 16 * 4)
            step(nc.vector.tensor_tensor(off[:, :, :], dst_all[:, :, :],
                                         first[:, 0:NG].rearrange("p (g o) -> p g o", o=1).broadcast_to([P, NG, TG]),
                                         ALU.subtract))
            step(nc.vector.tensor_tensor(off_tail[:, :], dst_tail[:, :], first[0:TAIL, NG:NG + 1], ALU.subtract))
            step(nc.vector.tensor_reduce(outside[:, 0:1], off[:, :, :], XY_AXES, ALU.max))
            step(nc.vector.tensor_reduce(outside[:, 1:2], off[:, :, :], XY_AXES, ALU.min))
            step(nc.vector.tensor_tensor(outside[0:TAIL, 0:1], outside[0:TAIL, 0:1], off_tail[:, :], ALU.max))
            step(nc.vector.tensor_tensor(outside[0:TAIL, 1:2], outside[0:TAIL, 1:2], off_tail[:, :], ALU.min))
            nc.vector.tensor_scalar(outside[:, 1:2], outside[:, 1:2], -1.0, None, ALU.mult).then_inc(outside_ready, 1)
            dve.wait_ge(outside_reduced, 1)
            step(nc.vector.tensor_scalar(bad[:, 0:1], outside_all[0:1, 0:1], float(P - 1), None, ALU.is_gt))
            step(nc.vector.tensor_scalar(bad[:, 1:2], outside_all[0:1, 1:2], 0.0, None, ALU.is_gt))
            step(nc.vector.tensor_tensor(bad[:, 2:3], bad[:, 0:1], bad[:, 1:2], ALU.max))
            step(nc.vector.tensor_scalar(passes[:, :], bad[:, 2:3], float(NT - 1), 1.0, ALU.mult, ALU.add))
            step(nc.vector.tensor_scalar(bad[:, 3:4], bad[:, 2:3], -1.0, 1.0, ALU.mult, ALU.add))
            step(nc.vector.tensor_scalar(first_f[:, :], first[0:1, :], bad[:, 3:4], None, ALU.mult))
            dve.wait_ge(tile_base_ready, 1)
            step(nc.vector.scalar_tensor_tensor(base_f[:, :, :], tile_base[:, :, :], bad[:, 2:3],
                                                first_f[:, :].rearrange("p (o g) -> p o g", o=1).broadcast_to([1, NT, NG + 1]),
                                                ALU.mult, ALU.add))
            step(nc.vector.tensor_copy(bases[:, :], base_f[:, :, :].rearrange("p t g -> p (t g)")))

        with nc.Block() as block:
            @block.sync
            def _(sp):
                sp.dma_start(X[:, 0:4, :], x[0:4 * P, :].rearrange("(t p) d -> p t d", p=P)).then_inc(x_loaded[0], 16)
                for h in range(H // 2):
                    sp.dma_start(W[:, :, h * DH:(h + 1) * DH],
                                 Ws[h].rearrange("(p c) d -> p c d", c=KC)).then_inc(w_loaded, 16)
                sp.wait_ge(w_loaded, 16 * W_LOADS)
                sp.dma_start(X[:, 4:NT - 1, :],
                             x[4 * P:(NT - 1) * P, :].rearrange("(t p) d -> p t d", p=P)).then_inc(x_loaded[1], 16)
                sp.wait_ge(pad_cleared, 1)
                sp.dma_start(X[0:LAST, NT - 1, :], x[(NT - 1) * P:N, :]).then_inc(x_loaded[1], 16)
                sp.dma_start(dst_all[:, :, :],
                             dst[0:NG * GE].rearrange("(g p t) -> p g t", p=P, t=TG)).then_inc(dst_loaded, 16)
                sp.dma_start(dst_tail[:, :], dst[NG * GE:E].rearrange("(p o) -> p o", o=1)).then_inc(dst_loaded, 16)
                sp.dma_start(first[:, 0:NG],
                             dst[0:NG * GE].rearrange("(g e) -> g e", e=GE)[:, 0].partition_broadcast(P),
                             allow_slow_non_contiguous=True).then_inc(dst_loaded, 16)
                sp.dma_start(first[:, NG:NG + 1],
                             dst[NG * GE:NG * GE + 1].partition_broadcast(P)).then_inc(dst_loaded, 16)
                sp.wait_ge(numbers_ready, 1)
                sp.dma_start(node_numbers, numbers[:, :]).then_inc(tables_stored, 16)
                with sp.Fori(0, NT // 2) as j:
                    for b in range(2):
                        sp.wait_ge(row_ready, 2 * j + b + 1)
                        sp.dma_start(source_table[bass.ds((2 * j + b) * P, P), :],
                                     row[b][:, :]).then_inc(row_stored[b], 16)
                sp.wait_ge(window_ready, 1)
                sp.dma_start(window_table.rearrange("(t p) r -> p t r", p=P), window[:, :, :]).then_inc(tables_stored, 16)
                sp.wait_ge(tables_stored, 32)
                for b in range(2):
                    sp.wait_ge(row_stored[b], 16 * (NT // 2))

            @block.gpsimd
            def _(pool):
                nc.gpsimd.memset(ident[:, :], 0.0).then_inc(ident_ready, 1)
                pool.wait_ge(ident_ready, 1)
                nc.gpsimd.affine_select(out=ident[:, :], in_=ident[:, :], compare_op=ALU.not_equal, fill=1.0,
                                        base=0, pattern=[[-1, P]], channel_multiplier=1).then_inc(ident_ready, 1)
                nc.gpsimd.iota(tile_base[:, :, :], [[P, NT], [0, NG + 1]], 0, 0,
                               allow_small_or_imprecise_dtypes=True).then_inc(tile_base_ready, 1)
                nc.gpsimd.iota(numbers[:, :], [[1, WROWS]], 0, 0,
                               allow_small_or_imprecise_dtypes=True).then_inc(numbers_ready, 1)
                nc.gpsimd.iota(window[:, :, 2 * H:2 * H + 1], [[P, NT + 1]], 0, 1,
                               allow_small_or_imprecise_dtypes=True).then_inc(numbers_ready, 1)
                pool.wait_ge(w_loaded, 16 * W_LOADS)
                for c in range(KC):
                    last = nc.gpsimd.tensor_tensor(product[1][:, c * D:(c + 1) * D].rearrange("p (h d) -> p h d", h=H),
                                                   W[:, c, :].rearrange("p (h d) -> p h d", h=H), a_row[:, :, DH:2 * DH], ALU.mult)
                last.then_inc(product_ready, 1)
                pool.wait_ge(w_hi_ready, 1)
                nc.gpsimd.tensor_tensor(W_lo[:, :, :], W[:, :, :], W_hi[:, :, :].bitcast(F32), ALU.subtract).then_inc(w_lo_ready, 1)
                nc.gpsimd.memset(zeros[:, :], 0.0).then_inc(zeros_ready, 1)
                pool.wait_ge(zeros_ready, 1)
                for t0, t1 in ((0, NT), (NT, NT + 1)):
                    nc.gpsimd.dma_start(sums[t0 * P:t1 * P, :].rearrange("(t p) r -> p t r", p=P),
                                        zeros[:, 0:(t1 - t0) * SROW].rearrange("p (t r) -> p t r", r=SROW)).then_inc(added, 16)
                pool.wait_ge(outside_ready, 1)
                nc.gpsimd.partition_all_reduce(outside_all[:, :], outside[:, :], P, RMAX).then_inc(outside_reduced, 1)
                pool.wait_ge(bound_ready, 1)
                nc.gpsimd.partition_all_reduce(bound_all[:, :], bound[:, :], P, RMAX).then_inc(bound_reduced, 1)
                pool.wait_ge(added, 32)

            @block.scalar
            def _(act):
                for h in range(H // 2, H):
                    act.dma_start(W[:, :, h * DH:(h + 1) * DH],
                                 Ws[h].rearrange("(p c) d -> p c d", c=KC)).then_inc(w_loaded, 16)
                act.dma_start(a_row[:, :, :], a_w.partition_broadcast(P)).then_inc(w_loaded, 16)
                act.dma_start(ab_row[:, :], a_b.partition_broadcast(P)).then_inc(w_loaded, 16)
                act.dma_start(Wb_row[:, :], Wb.rearrange("h d -> (h d)").partition_broadcast(P)).then_inc(w_loaded, 16)
                def roots(count, t0, t1):
                    act.wait_ge(var_ready, count)
                    nc.scalar.activation(rstd[:, t0:t1], mean_var[:, t0:t1, 1], ACT.Sqrt, bias=eps[:, 0:1]).then_inc(root_ready, 1)

                def high_part(t, b):
                    act.wait_ge(transposed, t + 1)
                    nc.scalar.activation(HT_hi[b][:, :, :], psT[b][:, :].rearrange("p (c n) -> p c n", c=KC),
                                         ACT.Copy).then_inc(hi_ready, 1)

                roots(2, 0, 4)
                high_part(0, 0)
                high_part(1, 1)
                act.wait_ge(w_loaded, 16 * W_LOADS)
                nc.scalar.activation(W_hi[:, :, :], W[:, :, :], ACT.Copy).then_inc(w_hi_ready, 1)
                for t in range(2, 4):
                    high_part(t, t % 2)
                roots(3, 4, NT)
                with act.Fori(1, NT // 2 - 1) as j:
                    for b in range(2):
                        high_part(2 * j + b + 2, b)

            @block.vector
            def _(dve):
                step = Chain(dve, own)
                nc.vector.memset(X[:, NT - 1, :], 0.0).then_inc(pad_cleared, 1)
                nc.vector.memset(eps[:, :], EPS).then_inc(var_ready, 1)
                step(nc.vector.memset(window[:, :, 2 * H + 1:WR], 0.0))
                step(nc.vector.memset(window[:, :, 0:2 * H], 0.0))

                def stats_of(part, t0, t1):
                    dve.wait_ge(x_loaded[part], 16 * (part + 1))
                    for t in range(t0, t1):
                        last = nc.vector.bn_stats(stats[:, t, :], X[:, t, :])
                    step(last)
                    for t in range(t0, t1):
                        last = nc.vector.bn_aggr(mean_var[:, t, :], stats[:, t, :])
                    last.then_inc(var_ready, 1)
                    dve.wait_ge(root_ready, part + 1)
                    step(nc.vector.reciprocal(rstd[:, t0:t1], rstd[:, t0:t1]))

                def norm(t, b):
                    nc.vector.tensor_scalar(Hn[b][:, :], X[:, bass.ds(t, 1), :].rearrange("p o d -> p (o d)"),
                                            mean_var[:, bass.ds(t, 1), 0], rstd[:, bass.ds(t, 1)],
                                            ALU.subtract, ALU.mult).then_inc(normed, 1)

                def low_part(t, b):
                    dve.wait_ge(hi_ready, t + 1)
                    nc.vector.tensor_tensor(HT_lo[b][:, :, :], psT[b][:, :].rearrange("p (c n) -> p c n", c=KC),
                                            HT_hi[b][:, :, :].bitcast(F32), ALU.subtract).then_inc(lo_ready, 1)

                def results(t, b, j, first):
                    dve.wait_ge(projected, t + 1)
                    if not first:
                        dve.wait_ge(row_stored[b], 16 * j)
                    nc.vector.tensor_tensor(row[b][:, 0:D], psW[b][:, :], Wb_row[:, :], ALU.add)
                    nc.vector.tensor_tensor(row[b][:, D:ROW], psS[b][:, H:2 * H], score_bias[:, H:2 * H], ALU.add)
                    nc.vector.tensor_tensor(scores[:, bass.ds(t, 1), :].rearrange("p o s -> p (o s)"),
                                            psS[b][:, 0:2 * H], score_bias[:, :], ALU.add).then_inc(row_ready, 1)

                stats_of(0, 0, 4)
                for b in range(2):
                    norm(b, b)
                for b in range(2):
                    low_part(b, b)
                dve.wait_ge(w_loaded, 16 * W_LOADS)
                Wv4 = W[:, :, :].rearrange("p c (h d) -> p c h d", h=H)
                for half in range(2):
                    part = a_row[:, :, half * DH:(half + 1) * DH]
                    pr = product[half][:, :].rearrange("p (c h d) -> p c h d", c=KC, h=H)
                    if half == 0:
                        for c in range(KC):
                            last = nc.vector.tensor_tensor(pr[:, c], Wv4[:, c], part, ALU.mult)
                        step(last)
                    else:
                        dve.wait_ge(product_ready, 1)
                    step(nc.vector.tensor_reduce(Wa[:, :, half * H:(half + 1) * H], pr, X_AXIS, ALU.add))
                    step(nc.vector.tensor_tensor(pr[:, 0], Wb_row[:, :].rearrange("p (h d) -> p h d", h=H), part, ALU.mult))
                    step(nc.vector.tensor_reduce(score_bias[:, half * H:(half + 1) * H], pr[:, 0], X_AXIS, ALU.add))
                step(nc.vector.tensor_tensor(score_bias[:, 0:H], score_bias[:, 0:H], ab_row[:, :], ALU.add))
                step(nc.vector.tensor_copy(Wa_hi[:, :, :], Wa[:, :, :]))
                nc.vector.tensor_tensor(Wa_lo[:, :, :], Wa[:, :, :], Wa_hi[:, :, :].bitcast(F32),
                                        ALU.subtract).then_inc(weights_ready, 1)

                def pair(j, first, last):
                    if not last:
                        for b in range(2):
                            norm(2 * j + b + 2, b)
                    for b in range(2):
                        results(2 * j + b, b, j, first)
                        if not last:
                            low_part(2 * j + b + 2, b)

                pair(0, True, False)
                stats_of(1, 4, NT)
                with dve.Fori(1, NT // 2 - 1) as j:
                    pair(j, False, False)
                flag_windows(dve, step)
                pair(NT // 2 - 1, False, True)
                dve.wait_ge(row_ready, NT)
                of_sources = scores[:, :, H:2 * H].rearrange("p t h -> p h t")
                nc.vector.tensor_reduce(bound[:, 0:H], of_sources, X_AXIS, ALU.max)
                nc.vector.tensor_reduce(bound[:, H:2 * H], of_sources, X_AXIS, ALU.min, negate=True).then_inc(bound_ready, 1)
                dve.wait_ge(bound_reduced, 1)
                step(nc.vector.tensor_copy(window[:, 0:NT, 0:H], scores[:, :, 0:H]))
                for t in range(NT):
                    last = nc.vector.tensor_tensor(window[:, t, H:2 * H], scores[:, t, 0:H], bound_all[:, 0:H], ALU.add)
                step(last)
                step(nc.vector.tensor_tensor(bound_all[:, 0:H], bound_all[:, 0:H], bound_all[:, H:2 * H], ALU.add))
                step(nc.vector.tensor_reduce(bound_all[:, H:H + 1], bound_all[:, 0:H], X_AXIS, ALU.max))
                step(nc.vector.tensor_scalar(wide_range[:, :], bound_all[0:1, H:H + 1], RANGE, None, ALU.is_gt))
                dve.wait_ge(numbers_ready, 2)
                for t in range(NT):
                    last = nc.vector.scalar_tensor_tensor(window[:, t, H:2 * H], window[:, t, H:2 * H], 0.2,
                                                          window[:, t, H:2 * H], ALU.mult, ALU.max)
                last.then_inc(window_ready, 1)

            @block.tensor
            def _(pe):
                pe.wait_ge(ident_ready, 2)

                def transpose(t, b):
                    pe.wait_ge(normed, t + 1)
                    if not (isinstance(t, int) and t < 2):
                        pe.wait_ge(lo_ready, t - 1)
                    for c in range(KC):
                        last = nc.tensor.transpose(psT[b][:, c * P:(c + 1) * P],
                                                   Hn[b][:, :].rearrange("n (p c) -> n c p", c=KC)[:, c, :], ident[:, :])
                    last.then_inc(transposed, 1)

                def project(t, b, first):
                    pe.wait_ge(lo_ready, t + 1)
                    if not first:
                        pe.wait_ge(row_ready, t - 1)
                    pairs = [(HT_hi, W_hi, Wa_hi), (HT_hi, W_lo, Wa_lo), (HT_lo, W_hi, Wa_hi)]
                    for n, (h, w, wa) in enumerate(pairs):
                        for c in range(KC):
                            nc.tensor.matmul(psW[b][:, :], h[b][:, c, :], w[:, c, :],
                                             start=(n == 0 and c == 0), stop=(n == 2 and c == KC - 1))
                    for n, (h, w, wa) in enumerate(pairs):
                        for c in range(KC):
                            last = nc.tensor.matmul(psS[b][:, 0:2 * H], h[b][:, c, :], wa[:, c, :],
                                                    start=(n == 0 and c == 0), stop=(n == 2 and c == KC - 1))
                    last.then_inc(projected, 1)

                def pair(j, first, last):
                    for b in range(2):
                        project(2 * j + b, b, first)
                        if not last:
                            transpose(2 * j + b + 2, b)

                for b in range(2):
                    transpose(b, b)
                pe.wait_ge(weights_ready, 1)
                pe.wait_ge(w_lo_ready, 1)
                pair(0, True, False)
                with pe.Fori(1, NT // 2 - 1) as j:
                    pair(j, False, False)
                pair(NT // 2 - 1, False, True)


def find_maxima(nc, sem, carrier, psum, ident, wide_range, scores, window, source_table, window_table, src, dst):
    ctx = ExitStack()
    with ctx:
        def sb(name, shape, dt=F32):
            return ctx.enter_context(nc.sbuf_tensor(name, shape, dt))

        CT = 4
        CH = CT * P
        CHUNKS = E // CH
        source = sb("chunk_source", [P, CT], I32)
        targets_row = sb("chunk_targets", [P, CH], I32)
        G = sb("chunk_rows", [P, CT, ROW])
        rows_T = sb("chunk_scores", [H, CH])
        pick = sb("pick_head", [H, H, P])
        mask = sb("chunk_mask", [P, CT, P])
        masked = sb("chunk_masked", [P, H, CH])
        best = sb("chunk_best", [P, H])
        maxima = sb("node_maxima", [P, NT, H])

        loaded, gathered, turned, copied, spread, chunk_done = (
            sem("chunk_loaded"), sem("chunk_gathered"), sem("chunk_turned"), sem("chunk_copied"), sem("chunk_spread"),
            sem("chunk_done"))
        pick_ready = sem("pick_ready")
        own, own_end = sem("maxima_vector_own"), sem("end_vector_own")
        shifts_ready, stored = sem("shifts_ready"), sem("shifts_stored")

        def if_wide(eng, body):
            wide = eng.value_load(wide_range[0:1, 0:1], min_val=0, max_val=1)
            with eng.If(wide > 0):
                body()
            eng.end_ifs()

        def every_chunk(eng, chunk):
            with eng.Fori(0, CHUNKS) as c:
                chunk(c, c * CH)
            chunk(CHUNKS, E - CH)

        with nc.Block() as block:
            @block.sync
            def _(sp):
                def chunk(c, at):
                    sp.wait_ge(chunk_done, c + 1)
                    sp.dma_start(source[:, :], src[bass.ds(at, CH)].rearrange("(p t) -> p t", t=CT)).then_inc(loaded, 16)
                    sp.dma_start(targets_row[:, :], dst[bass.ds(at, CH)].partition_broadcast(P)).then_inc(loaded, 16)

                def body():
                    every_chunk(sp, chunk)
                    sp.wait_ge(shifts_ready, 1)
                    sp.dma_start(window_table.rearrange("(t p) r -> p t r", p=P), window[:, :, :]).then_inc(stored, 16)
                    sp.wait_ge(stored, 16)

                if_wide(sp, body)

            @block.gpsimd
            def _(pool):
                def chunk(c, at):
                    pool.wait_ge(loaded, 32 * (c + 1))
                    pool.sem_inc(carrier, 1)
                    for t in range(CT):
                        nc.gpsimd.indirect_dma_start(
                            G[:, t, :], None, source_table,
                            bass.IndirectOffsetOnAxis(ap=source[:, t:t + 1], axis=0)).then_inc(gathered, 16)

                def body():
                    nc.gpsimd.memset(pick[:, :, :], 0.0).then_inc(pick_ready, 1)
                    pool.wait_ge(pick_ready, 1)
                    nc.gpsimd.affine_select(out=pick[:, :, :], in_=pick[:, :, :], compare_op=ALU.not_equal, fill=1.0,
                                            base=0, pattern=[[-1, H], [0, P]], channel_multiplier=1).then_inc(pick_ready, 1)
                    every_chunk(pool, chunk)

                if_wide(pool, body)

            @block.vector
            def _(dve):
                def chunk(c, at):
                    dve.wait_ge(turned, c + 1)
                    nc.vector.tensor_copy(rows_T[:, :], psum[0:H, 0:CH]).then_inc(copied, 1)
                    dve.wait_ge(spread, c + 1)
                    dve.sem_inc(carrier, 1)
                    with dve.Fori(0, NT) as t:
                        step = Chain(dve, own, 4 * (NT * c + t))
                        step(nc.vector.tensor_scalar(mask[:, :, :], targets_row[:, :].rearrange("n (p t) -> n t p", t=CT),
                                                     window[:, bass.ds(t, 1), 2 * H], None, ALU.not_equal))
                        step(nc.vector.scalar_tensor_tensor(
                            masked[:, :, :], mask[:, :, :].rearrange("p (o t) n -> p o (t n)", o=1).broadcast_to([P, H, CH]),
                            MASKED, psum[:, :].rearrange("p (h n) -> p h n", h=H), ALU.mult, ALU.add))
                        step(nc.vector.tensor_reduce(best[:, :], masked[:, :, :], X_AXIS, ALU.max))
                        now = maxima[:, bass.ds(t, 1), :].rearrange("p o h -> p (o h)")
                        step(nc.vector.tensor_tensor(now, now, best[:, :], ALU.max))
                    dve.sem_inc(chunk_done, 1)

                def body():
                    step = Chain(dve, own_end)
                    step(nc.vector.memset(maxima[:, :, :], MASKED))
                    dve.sem_inc(chunk_done, 1)
                    every_chunk(dve, chunk)
                    shift = window[:, 0:NT, H:2 * H]
                    step(nc.vector.tensor_tensor(maxima[:, :, :], scores[:, :, 0:H], maxima[:, :, :], ALU.add))
                    nc.vector.scalar_tensor_tensor(shift, maxima[:, :, :], 0.2, maxima[:, :, :], ALU.mult, ALU.max).then_inc(shifts_ready, 1)

                if_wide(dve, body)

            @block.tensor
            def _(pe):
                def chunk(c, at):
                    pe.wait_ge(gathered, 16 * CT * (c + 1))
                    for t in range(CT):
                        last = nc.tensor.transpose(psum[0:H, t * P:(t + 1) * P], G[:, t, D:ROW], ident[:, :])
                    last.then_inc(turned, 1)
                    pe.wait_ge(copied, c + 1)
                    for h in range(H):
                        last = nc.tensor.matmul(psum[:, h * CH:(h + 1) * CH], pick[:, h, :], rows_T[:, :], start=True, stop=True)
                    last.then_inc(spread, 1)

                def body():
                    pe.wait_ge(pick_ready, 2)
                    every_chunk(pe, chunk)

                if_wide(pe, body)


def sum_edges(nc, sem, bank, bases, passes, source_table, window_table, node_numbers, sums,
              added, carrier, weights_ahead, wv_loaded, Wv, columns, cols_loaded,
              vectors, src, dst):
    ctx = ExitStack()
    with ctx:
        def sb(name, shape, dt=F32):
            return ctx.enter_context(nc.sbuf_tensor(name, shape, dt))

        SETS = 3
        G = [sb(f"G{b}", [P, TG, ROW]) for b in range(SETS)]
        target = [sb(f"target{b}", [P, TG], I32) for b in range(SETS)]
        source = [sb(f"source{b}", [P, TG], I32) for b in range(SETS)]
        target_f = [sb(f"target_f{b}", [P, TG]) for b in range(SETS)]
        window = [sb(f"window_rows{b}", [P, WR]) for b in range(SETS)]
        nodes = [sb(f"nodes{b}", [P, P]) for b in range(SETS)]
        onehot = [sb(f"onehot{b}", [P, TG, P], F32R) for b in range(SETS)]
        onehot_T = [sb(f"onehot_T{b}", [P, TG * P], F32R) for b in range(SETS)]
        targets_row = [sb(f"targets_row{b}", [P, GE], I32) for b in range(SETS)]
        logit = [sb(f"logit{b}", [P, TG, H]) for b in range(SETS)]
        shifted = [sb(f"shifted{b}", [P, TG, H]) for b in range(SETS)]
        weight = [sb(f"weight{b}", [P, TG, H]) for b in range(SETS)]
        window_parts = [sb(f"window_parts{b}", [P, 2, 2 * H], F32R) for b in range(SETS)]
        weight_parts = [sb(f"weight_parts{b}", [P, TG, 2, H], F32R) for b in range(SETS)]
        flush = [sb(f"flush{b}", [P, SROW]) for b in range(SETS)]
        psS = bank[0]
        psN = bank[1:1 + SETS]
        psD = [bank[1 + SETS + b][:, 0:2 * H] for b in range(SETS)]

        loaded = [sem(f"loaded{b}") for b in range(SETS)]
        gathered = [sem(f"gathered{b}") for b in range(SETS)]
        onehots_ready = sem("onehots_ready")
        scored = sem("scored")
        logits_ready = [sem(f"logits_ready{b}") for b in range(SETS)]
        weights_ready = sem("edge_weights_ready")
        weights_hi = sem("edge_weights_hi")
        weighted = [sem(f"weighted{b}") for b in range(SETS)]
        summed = [sem(f"summed{b}") for b in range(SETS)]
        flushed = [sem(f"flushed{b}") for b in range(SETS)]
        own_early = sem("edges_vector_own_early")
        own_late = sem("edges_vector_own_late")

        ROUNDS = NG // SETS
        LOADS = 5 * 16
        WEAVE = 4
        WEAVE_PE = 9

        def uses(b, p, g):
            return p * (ROUNDS + (b == 0)) + g

        def tiles(b, p, g):
            return p * (ROUNDS * TG + (b == 0)) + g * TG

        def groups(b, p, g):
            return p * (NG + 1) + SETS * g + b

        def in_turn(eng, start_pass, early, slot):
            rounds = eng.value_load(passes[0:1, 0:1], min_val=1, max_val=NT)
            with eng.Fori(0, rounds) as p:
                start_pass(p)
                early(p, 0, 0, TG, P)
                with eng.Fori(0, ROUNDS - 1) as g:
                    for b in range(SETS - 1):
                        slot((p, b, g, TG, P), (p, b + 1, g, TG, P))
                    slot((p, SETS - 1, g, TG, P), (p, 0, g + 1, TG, P))
                g = ROUNDS - 1
                for b in range(SETS - 1):
                    slot((p, b, g, TG, P), (p, b + 1, g, TG, P))
                slot((p, SETS - 1, g, TG, P), (p, 0, g + 1, 1, TAIL))
                slot((p, 0, g + 1, 1, TAIL), None)

        with nc.Block() as block:
            @block.sync
            def _(sp):
                def load(p, b, g, nt, ne):
                    base = sp.value_load(bases[0:1, bass.ds(groups(b, p, g), 1)], min_val=0, max_val=NP - 1)
                    sp.wait_ge(logits_ready[b], uses(b, p, g) + 1)
                    at = (SETS * g + b) * GE
                    sp.dma_start(target[b][0:ne, 0:nt],
                                 dst[bass.ds(at, ne * nt)].rearrange("(p t) -> p t", t=nt)).then_inc(loaded[b], 16)
                    sp.dma_start(targets_row[b][:, 0:ne * nt],
                                 dst[bass.ds(at, ne * nt)].partition_broadcast(P)).then_inc(loaded[b], 16)
                    sp.dma_start(source[b][0:ne, 0:nt],
                                 src[bass.ds(at, ne * nt)].rearrange("(p t) -> p t", t=nt)).then_inc(loaded[b], 16)
                    sp.dma_start(window[b][:, :], window_table[bass.ds(base, P), :]).then_inc(loaded[b], 16)
                    sp.dma_start(nodes[b][:, :],
                                 node_numbers[0, bass.ds(base, P)].partition_broadcast(P)).then_inc(loaded[b], 16)

                in_turn(sp, lambda p: None, load, lambda late, early: load(*early) if early else None)
                g_col, b_col, qn_col, kn_col = columns
                ln_g, ln_b, qn_g, kn_g = vectors
                for col, vec in ((g_col, ln_g), (b_col, ln_b)):
                    sp.dma_start(col[:, :], vec.rearrange("(c p) -> p c", p=P),
                                   allow_slow_non_contiguous=True).then_inc(cols_loaded, 16)
                for col, vec in ((qn_col, qn_g), (kn_col, kn_g)):
                    for half in range(2):
                        sp.dma_start(col[half * DH:(half + 1) * DH, :],
                                     vec.rearrange("(p o) -> p o", o=1)).then_inc(cols_loaded, 16)
                sp.dma_start(weights_ahead[:, :, :], Wv.rearrange("(c p) n -> p c n", p=P)).then_inc(wv_loaded, 16)
                sp.wait_ge(wv_loaded, 16)
                sp.wait_ge(cols_loaded, 16 * 6)

            @block.gpsimd
            def _(pool):
                def gather(p, b, g, nt, ne):
                    pool.wait_ge(loaded[b], LOADS * (uses(b, p, g) + 1))
                    for t in range(nt):
                        pool.wait_ge(summed[b], tiles(b, p, g) + t + 1)
                        pool.sem_inc(carrier, 1)
                        nc.gpsimd.indirect_dma_start(
                            G[b][0:ne, t, :], None, source_table,
                            bass.IndirectOffsetOnAxis(ap=source[b][0:ne, t:t + 1], axis=0)).then_inc(gathered[b], 16)

                def add(p, b, g):
                    base = pool.value_load(bases[0:1, bass.ds(groups(b, p, g), 1)], min_val=0, max_val=NP - 1)
                    pool.wait_ge(flushed[b], uses(b, p, g) + 2)
                    pool.wait_ge(added, 16 * (groups(b, p, g) + 2))
                    nc.gpsimd.dma_start(sums[bass.ds(base, P), :], flush[b][:, :],
                                        accum_op=ALU.add).then_inc(added, 16)

                rounds = pool.value_load(passes[0:1, 0:1], min_val=1, max_val=NT)
                with pool.Fori(0, rounds) as p:
                    for b in range(SETS):
                        pool.wait_ge(summed[b], tiles(b, p, 0) + TG)
                        gather(p, b, 0, TG, P)
                    with pool.Fori(1, ROUNDS) as g:
                        for b in range(SETS):
                            gather(p, b, g, TG, P)
                            add(p, b, g - 1)
                    gather(p, 0, ROUNDS, 1, TAIL)
                    for b in range(SETS):
                        add(p, b, ROUNDS - 1)
                    add(p, 0, ROUNDS)
                pool.wait_ge(added, 16 * (rounds * (NG + 1) + 2))

            @block.vector
            def _(dve):
                for b in range(SETS):
                    dve.sem_inc(logits_ready[b], 1)

                def early(p, b, g, nt, ne):
                    dve.wait_ge(loaded[b], LOADS * (uses(b, p, g) + 1))
                    dve.wait_ge(summed[b], tiles(b, p, g) + TG)
                    step = Chain(dve, own_early, 2 * groups(b, p, g))
                    step(nc.vector.tensor_copy(window_parts[b][:, 0, :], window[b][:, 0:2 * H]))
                    nc.vector.tensor_tensor(window_parts[b][:, 1, :], window[b][:, 0:2 * H],
                                            window_parts[b][:, 0, :].bitcast(F32), ALU.subtract)
                    step(nc.vector.tensor_copy(target_f[b][0:ne, 0:nt], target[b][0:ne, 0:nt]))
                    nc.vector.tensor_tensor(
                        onehot[b][0:ne, 0:nt, :],
                        nodes[b][0:ne, :].rearrange("p (o n) -> p o n", o=1).broadcast_to([ne, nt, P]),
                        target_f[b][0:ne, 0:nt].rearrange("p (t o) -> p t o", o=1).broadcast_to([ne, nt, P]),
                        ALU.is_equal)
                    nc.vector.tensor_scalar(
                        onehot_T[b][:, 0:nt * ne].rearrange("n (t p) -> n t p", t=nt),
                        targets_row[b][:, 0:nt * ne].rearrange("n (p t) -> n t p", t=nt),
                        window[b][:, 2 * H:2 * H + 1], None, ALU.is_equal).then_inc(onehots_ready, 1)

                def logits(p, b, g, nt, ne):
                    dve.wait_ge(gathered[b], 16 * (tiles(b, p, g) + nt))
                    dve.wait_ge(scored, groups(b, p, g) + 1)
                    ps = psS[0:ne, 0:nt * 4 * H].rearrange("p (t s) -> p t s", s=4 * H)
                    z, z2 = logit[b][0:ne, 0:nt, :], shifted[b][0:ne, 0:nt, :]
                    step = Chain(dve, own_late, 5 * groups(b, p, g))
                    step(nc.vector.tensor_tensor(z, ps[:, :, 0:H], G[b][0:ne, 0:nt, D:ROW], ALU.add))
                    step(nc.vector.tensor_tensor(z, z, ps[:, :, 2 * H:3 * H], ALU.add))
                    step(nc.vector.scalar_tensor_tensor(z2, z, 0.2, z, ALU.mult, ALU.max))
                    step(nc.vector.tensor_tensor(z, z2, ps[:, :, H:2 * H], ALU.subtract))
                    step(nc.vector.tensor_tensor(z, z, ps[:, :, 3 * H:4 * H], ALU.subtract))
                    nc.vector.tensor_scalar(z2, z, 0.0, None, ALU.min).then_inc(logits_ready[b], 1)

                def weigh(p, b, g, t0, t1, ne):
                    for t in range(t0, t1):
                        rows = G[b][0:ne, t, 0:D].rearrange("p (h d) -> p h d", h=H)
                        nc.vector.tensor_tensor(
                            rows, rows,
                            weight[b][0:ne, t, :].rearrange("p (h o) -> p h o", o=1).broadcast_to([ne, H, DH]),
                            ALU.mult).then_inc(weighted[b], 1)

                def slot(late, next_early):
                    p, b, g, nt, ne = late
                    logits(*late)
                    dve.wait_ge(weights_hi, groups(b, p, g) + 1)
                    nc.vector.tensor_tensor(weight_parts[b][0:ne, 0:nt, 1, :], weight[b][0:ne, 0:nt, :],
                                            weight_parts[b][0:ne, 0:nt, 0, :].bitcast(F32), ALU.subtract)
                    weigh(p, b, g, 0, min(WEAVE, nt), ne)
                    if next_early:
                        early(*next_early)
                    weigh(p, b, g, WEAVE, nt, ne)

                in_turn(dve, lambda p: None, early, slot)

            @block.scalar
            def _(act):
                for b in range(SETS):
                    act.sem_inc(flushed[b], 1)

                def start_pass(p):
                    act.wait_ge(added, 16 * (groups(0, p, 0) + 2))

                def exponentials(p, b, g, nt, ne):
                    act.wait_ge(logits_ready[b], uses(b, p, g) + 2)
                    nc.scalar.activation(weight[b][0:ne, 0:nt, :], shifted[b][0:ne, 0:nt, :],
                                         ACT.Exp).then_inc(weights_ready, 1)
                    act.wait_ge(weights_ready, groups(b, p, g) + 1)
                    nc.scalar.activation(weight_parts[b][0:ne, 0:nt, 0, :], weight[b][0:ne, 0:nt, :],
                                         ACT.Copy).then_inc(weights_hi, 1)

                def slot(late, next_early):
                    if next_early:
                        exponentials(*next_early)
                    p, b, g, nt, ne = late
                    act.wait_ge(summed[b], tiles(b, p, g) + nt + TG)
                    act.wait_ge(added, 16 * (groups(b, p, g) + 1))
                    nc.scalar.activation(flush[b][:, 0:D], psN[b][:, :], ACT.Copy)
                    nc.scalar.activation(flush[b][:, D:SROW], psD[b], ACT.Copy).then_inc(flushed[b], 1)

                in_turn(act, start_pass, exponentials, slot)

            @block.tensor
            def _(pe):
                for b in range(SETS):
                    pe.sem_inc(summed[b], TG)

                def early(p, b, g, nt, ne):
                    pe.wait_ge(onehots_ready, groups(b, p, g) + 1)
                    for t in range(nt):
                        last = nc.tensor.matmul(psS[0:ne, t * 4 * H:(t + 1) * 4 * H],
                                                onehot_T[b][:, t * ne:(t + 1) * ne],
                                                window_parts[b][:, :, :].rearrange("p i s -> p (i s)"), start=True, stop=True)
                    last.then_inc(scored, 1)

                def sum_up(p, b, g, t0, t1, nt, ne):
                    for t in range(t0, t1):
                        pe.wait_ge(weighted[b], tiles(b, p, g) + t + 1)
                        nc.tensor.matmul(psN[b][:, :], onehot[b][0:ne, t, :].bitcast(F32), G[b][0:ne, t, 0:D],
                                         start=(t == 0), stop=(t == nt - 1))
                        nc.tensor.matmul(psD[b], onehot[b][0:ne, t, :],
                                         weight_parts[b][0:ne, t, :, :].rearrange("p i h -> p (i h)"),
                                         start=(t == 0), stop=(t == nt - 1)).then_inc(summed[b], 1)

                def slot(late, next_early):
                    p, b, g, nt, ne = late
                    pe.wait_ge(flushed[b], uses(b, p, g) + 1)
                    sum_up(p, b, g, 0, min(WEAVE_PE, nt), nt, ne)
                    if next_early:
                        early(*next_early)
                    sum_up(p, b, g, WEAVE_PE, nt, nt, ne)

                in_turn(pe, lambda p: None, early, slot)


def project_heads(nc, sem, carrier, bank, X, S, ident, sums, QT, KT, V, weights_ahead, wv_loaded,
                  columns, cols_loaded, Wq, Wk):
    ctx = ExitStack()
    with ctx:
        def sb(name, shape, dt=F32):
            return ctx.enter_context(nc.sbuf_tensor(name, shape, dt))

        stats = [sb(f"ln_stats{b}", [P, 6]) for b in range(2)]
        mean_var = [sb(f"ln_mean_var{b}", [P, 2]) for b in range(2)]
        rstd = [sb(f"ln_rstd{b}", [P, 1]) for b in range(2)]
        eps = sb("ln_eps", [P, 2])
        g_col, b_col, qn_col, kn_col = columns
        stage = [weights_ahead] + [sb(f"w_stage{m}", [P, KC, D]) for m in range(1, 3)]
        W_hi = [sb(f"Wqkv_hi{m}", [P, KC, D], F32R) for m in range(3)]
        W_lo = [sb(f"Wqkv_lo{m}", [P, KC, D], F32R) for m in range(3)]
        Hn = [sb(f"qkv_Hn{b}", [P, D]) for b in range(2)]
        HT = [sb(f"qkv_HT{b}", [P, KC, P]) for b in range(2)]
        HT_hi = [sb(f"qkv_HT_hi{b}", [P, KC, P], F32R) for b in range(2)]
        HT_lo = [sb(f"qkv_HT_lo{b}", [P, KC, P], F32R) for b in range(2)]
        x1 = [sb(f"x1_{b}", [P, D]) for b in range(2)]
        length = [sb(f"length{b}", [P, 2, H]) for b in range(2)]
        unit = [[sb(f"qk_unit{b}{m}", [P, D]) for m in range(2)] for b in range(2)]
        square = unit

        sums_loaded = [sem(f"sums_loaded{i}") for i in range(2)]
        w_loaded = [wv_loaded] + [sem(f"wqkv_loaded{m}") for m in range(1, 3)]
        own = sem("heads_vector_own")
        var_ready, root_ready = sem("ln_var_ready"), sem("ln_root_ready")
        w_hi_ready, w_lo_ready = sem("wqkv_hi_ready"), sem("wqkv_lo_ready")
        normed_ready = sem("ln_normed_ready")
        transposed, affine, hi_ready, lo_ready = (sem("qkv_transposed"), sem("qkv_affine"), sem("qkv_hi_ready"),
                                                  sem("qkv_lo_ready"))
        projected, squared, reduced, rooted = sem("qkv_projected"), sem("squared"), sem("reduced"), sem("rooted")
        scaled, v_read, qk_transposed, stored = sem("qk_scaled"), sem("v_read"), sem("qk_transposed"), sem("qk_stored")
        loop_own, loop_prepare = sem("qkv_vector_own"), sem("prepare_vector_own")
        first_lo_ready = sem("first_lo_ready")
        sums_inverted, rows_scaled = sem("sums_inverted"), sem("rows_scaled")
        x1_ready, x_kept = sem("x1_ready"), sem("x_kept")

        psT = bank[0]
        psP = [[bank[1], bank[2], bank[3]], [bank[4], bank[5], bank[6]]]
        psX = [[bank[7], bank[3]], [bank[7], bank[6]]]
        chunks = lambda ps: ps[:, :].rearrange("p (c n) -> p c n", c=KC)

        with nc.Block() as block:
            @block.sync
            def _(sp):
                for m, w in ((1, Wk), (2, Wq)):
                    sp.dma_start(stage[m][:, :, :], w.rearrange("(c p) n -> p c n", p=P)).then_inc(w_loaded[m], 16)

            @block.gpsimd
            def _(pool):
                def scale_rows(t):
                    by_head = S[:, bass.ds(t, 1), 0:D].rearrange("p o (h d) -> p (o h) d", h=H)
                    inverse = S[:, bass.ds(t, 1), D:ROW].rearrange("p o (h i) -> p (o h) i", i=1)
                    nc.gpsimd.tensor_tensor(by_head, by_head, inverse.broadcast_to([P, H, DH]), ALU.mult).then_inc(rows_scaled, 1)

                def keep(t, b):
                    pool.wait_ge(x1_ready, t + 1)
                    nc.gpsimd.tensor_copy(X[:, bass.ds(t, 1), :].rearrange("p o d -> p (o d)"), x1[b][:, :]).then_inc(x_kept, 1)

                pool.wait_ge(sums_inverted, 1)
                scale_rows(0)
                scale_rows(1)
                keep(0, 0)
                keep(1, 1)
                pool.wait_ge(sums_inverted, 2)
                scale_rows(2)
                scale_rows(3)
                for m in range(1, 3):
                    pool.wait_ge(w_hi_ready, m + 1)
                    nc.gpsimd.tensor_tensor(W_lo[m][:, :, :], stage[m][:, :, :], W_hi[m][:, :, :].bitcast(F32),
                                            ALU.subtract).then_inc(w_lo_ready, 1)
                with pool.Fori(1, NT // 2 - 1) as j:
                    for b in range(2):
                        keep(2 * j + b, b)
                        scale_rows(2 * j + b + 2)
                for b in range(2):
                    keep(NT - 2 + b, b)

            @block.scalar
            def _(act):
                for part, (t0, t1) in enumerate(((0, 2), (2, NT))):
                    act.dma_start(S[:, t0:t1, :], sums[t0 * P:t1 * P, :].rearrange("(t p) r -> p t r", p=P)).then_inc(sums_loaded[part], 16)

                def high_weights(m):
                    act.wait_ge(w_loaded[m], 16)
                    nc.scalar.activation(W_hi[m][:, :, :], stage[m][:, :, :], ACT.Copy).then_inc(w_hi_ready, 1)

                def root(t, b):
                    act.wait_ge(var_ready, t + 1)
                    nc.scalar.activation(rstd[b][:, :], mean_var[b][:, 1:2], ACT.Sqrt,
                                         bias=eps[:, 0:1], scale=1.0 + EPS).then_inc(root_ready, 1)

                def transposed_parts(t, b):
                    act.wait_ge(transposed, t + 1)
                    for c in range(KC):
                        last = nc.scalar.activation(HT[b][:, c, :], chunks(psT)[:, c, :], ACT.Identity,
                                                    bias=b_col[:, c:c + 1], scale=g_col[:, c:c + 1])
                    last.then_inc(affine, 1)
                    act.wait_ge(affine, t + 1)
                    nc.scalar.activation(HT_hi[b][:, :, :], HT[b][:, :, :], ACT.Copy).then_inc(hi_ready, 1)

                def results(t, b):
                    act.wait_ge(projected, 3 * t + 1)
                    nc.scalar.activation(V[:, bass.ds(t, 1), :].rearrange("p o d -> p (o d)"), psP[b][0][:, :], ACT.Copy).then_inc(v_read, 1)
                    for m in range(2):
                        act.wait_ge(projected, 3 * t + m + 2)
                        nc.scalar.activation(square[b][m][:, :], psP[b][m + 1][:, :], ACT.Square).then_inc(squared, 1)

                def lengths(t, b):
                    act.wait_ge(reduced, 2 * t + 2)
                    nc.scalar.activation(length[b][:, :, :], length[b][:, :, :], ACT.Sqrt, bias=eps[:, 1:2]).then_inc(rooted, 1)

                def pair(j, first, last):
                    for b in range(2):
                        t = 2 * j + b
                        if not last:
                            root(t + 2, b)
                        if not (first and b == 0):
                            lengths(t - 1, 1 - b)
                        results(t, b)
                        if not last:
                            transposed_parts(t + 2, b)

                high_weights(0)
                root(0, 0)
                high_weights(1)
                root(1, 1)
                act.wait_ge(cols_loaded, 16 * 6)
                for b in range(2):
                    transposed_parts(b, b)
                high_weights(2)
                pair(0, True, False)
                with act.Fori(1, NT // 2 - 1) as j:
                    pair(j, False, False)
                pair(NT // 2 - 1, False, True)
                lengths(NT - 1, 1)

            @block.vector
            def _(dve):
                step = Chain(dve, own)
                nc.vector.memset(eps[:, 0:1], EPS * EPS)
                step(nc.vector.memset(eps[:, 1:2], 1e-12))

                def invert_sums(t0, t1):
                    step(nc.vector.tensor_tensor(S[:, t0:t1, D:ROW], S[:, t0:t1, D:ROW], S[:, t0:t1, ROW:SROW], ALU.add))
                    step(nc.vector.tensor_scalar(S[:, t0:t1, D:ROW], S[:, t0:t1, D:ROW], TINY, None, ALU.max))
                    nc.vector.reciprocal(S[:, t0:t1, D:ROW], S[:, t0:t1, D:ROW]).then_inc(sums_inverted, 1)

                def prepare(t, b):
                    step = Chain(dve, loop_prepare, 3 * t)
                    rows = S[:, bass.ds(t, 1), 0:D].rearrange("p o d -> p (o d)")
                    tile = X[:, bass.ds(t, 1), :].rearrange("p o d -> p (o d)")
                    dve.wait_ge(rows_scaled, t + 1)
                    if not (isinstance(t, int) and t < 2):
                        dve.wait_ge(x_kept, t - 1)
                    step(nc.vector.tensor_tensor(x1[b][:, :], tile, rows, ALU.add))
                    dve.sem_inc(x1_ready, 1)
                    step(nc.vector.bn_stats(stats[b][:, :], x1[b][:, :]))
                    dve.sem_inc(carrier, 1)
                    nc.vector.bn_aggr(mean_var[b][:, :], stats[b][:, :]).then_inc(var_ready, 1)
                    dve.wait_ge(root_ready, t + 1)
                    step(nc.vector.reciprocal(rstd[b][:, :], rstd[b][:, :]))

                def norm(t, b):
                    nc.vector.tensor_scalar(Hn[b][:, :], x1[b][:, :], mean_var[b][:, 0:1], rstd[b][:, 0:1],
                                            ALU.subtract, ALU.mult).then_inc(normed_ready, 1)

                def low_part(t, b):
                    dve.wait_ge(hi_ready, t + 1)
                    nc.vector.tensor_tensor(HT_lo[b][:, :, :], HT[b][:, :, :], HT_hi[b][:, :, :].bitcast(F32),
                                            ALU.subtract).then_inc(lo_ready, 1)

                def scale(t, b):
                    for m in range(2):
                        dve.wait_ge(squared, 2 * t + m + 1)
                        nc.vector.tensor_reduce(length[b][:, m, :], square[b][m][:, :].rearrange("p (h d) -> p h d", h=H),
                                                X_AXIS, ALU.add).then_inc(reduced, 1)
                    dve.wait_ge(rooted, t + 1)
                    nc.vector.reciprocal(length[b][:, :, :], length[b][:, :, :]).then_inc(loop_own, 1)
                    dve.wait_ge(loop_own, t + 1)
                    for m in range(2):
                        nc.vector.tensor_tensor(
                            unit[b][m][:, :].rearrange("p (h d) -> p h d", h=H),
                            psP[b][m + 1][:, :].rearrange("p (h d) -> p h d", h=H),
                            length[b][:, m, :].rearrange("p (h o) -> p h o", o=1).broadcast_to([P, H, DH]),
                            ALU.mult).then_inc(scaled, 1)

                def store(t, b):
                    for m, (out, col) in enumerate(((QT, qn_col), (KT, kn_col))):
                        dve.wait_ge(qk_transposed, 2 * t + m + 1)
                        nc.vector.tensor_scalar(out[:, :, bass.ds(t * P, P)], chunks(psX[b][m]), col[:, 0:1], None,
                                                ALU.mult).then_inc(stored, 1)

                def pair(j, first, last):
                    for b in range(2):
                        t = 2 * j + b
                        if not last:
                            prepare(t + 2, b)
                            norm(t + 2, b)
                        if not (first and b == 0):
                            scale(t - 1, 1 - b)
                        if not last:
                            low_part(t + 2, b)
                        if not (first and b == 0):
                            store(t - 1, 1 - b)

                dve.wait_ge(w_hi_ready, 1)
                nc.vector.tensor_tensor(W_lo[0][:, :, :], stage[0][:, :, :], W_hi[0][:, :, :].bitcast(F32),
                                        ALU.subtract).then_inc(first_lo_ready, 1)
                dve.wait_ge(sums_loaded[0], 16)
                invert_sums(0, 2)
                for b in range(2):
                    prepare(b, b)
                    norm(b, b)
                for b in range(2):
                    low_part(b, b)
                dve.wait_ge(sums_loaded[1], 16)
                invert_sums(2, NT)
                dve.wait_ge(cols_loaded, 16 * 6)
                step(nc.vector.tensor_scalar(qn_col[:, :], qn_col[:, :], float(DH) ** 0.5, None, ALU.mult))
                pair(0, True, False)
                with dve.Fori(1, NT // 2 - 1) as j:
                    pair(j, False, False)
                pair(NT // 2 - 1, False, True)
                scale(NT - 1, 1)
                store(NT - 1, 1)

            @block.tensor
            def _(pe):
                def transpose(t, b):
                    pe.wait_ge(normed_ready, t + 1)
                    if not (isinstance(t, int) and t == 0):
                        pe.wait_ge(affine, t)
                    for c in range(KC):
                        last = nc.tensor.transpose(psT[:, c * P:(c + 1) * P], Hn[b][:, c * P:(c + 1) * P], ident[:, :])
                    last.then_inc(transposed, 1)

                def project(t, b, first):
                    pe.wait_ge(lo_ready, t + 1)
                    if not first:
                        pe.wait_ge(v_read, t - 1)
                    for m in range(3):
                        if first and b == 0 and m == 0:
                            pe.wait_ge(first_lo_ready, 1)
                        elif first and b == 0:
                            pe.wait_ge(w_lo_ready, m)
                        if not first and m == 2:
                            pe.wait_ge(stored, 2 * t - 2)
                        for n, (h, w) in enumerate(((HT_hi, W_hi), (HT_hi, W_lo), (HT_lo, W_hi))):
                            for c in range(KC):
                                last = nc.tensor.matmul(psP[b][m][:, :], h[b][:, c, :], w[m][:, c, :],
                                                        start=(n == 0 and c == 0), stop=(n == 2 and c == KC - 1))
                        last.then_inc(projected, 1)

                def transpose_heads(t, b):
                    for m in range(2):
                        pe.wait_ge(scaled, 2 * t + 2 - m)
                        if m == 0 and not (isinstance(t, int) and t == 0):
                            pe.wait_ge(stored, 2 * t - 1)
                        for c in range(KC):
                            last = nc.tensor.transpose(psX[b][m][:, c * P:(c + 1) * P], unit[b][1 - m][:, c * P:(c + 1) * P], ident[:, :])
                        last.then_inc(qk_transposed, 1)

                def pair(j, first, last):
                    for b in range(2):
                        t = 2 * j + b
                        project(t, b, first)
                        if not last:
                            transpose(t + 2, b)
                        if not (first and b == 0):
                            transpose_heads(t - 1, 1 - b)

                for b in range(2):
                    transpose(b, b)
                pair(0, True, False)
                with pe.Fori(1, NT // 2 - 1) as j:
                    pair(j, False, False)
                pair(NT // 2 - 1, False, True)
                transpose_heads(NT - 1, 1)


def attend(nc, sem, psum, ident, QT, KT, V, OT, weight_sums, sums_row, Wo_raw, wo_loaded, Wo):
    ctx = ExitStack()
    with ctx:
        def sb(name, shape, dt=F32):
            return ctx.enter_context(nc.sbuf_tensor(name, shape, dt))

        CQ = 4
        CHUNKS = [range(c, min(c + CQ, NT)) for c in range(0, NT, CQ)]
        REGION = 1024
        PIECES = [(c, i, k0, min(k0 + REGION, (i + 1) * P))
                  for c, tiles in enumerate(CHUNKS) for i in tiles for k0 in range(0, (i + 1) * P, REGION)]
        KEYS = [tiles[-1] + 1 for tiles in CHUNKS]
        NC, NPC, NK = len(CHUNKS), len(PIECES), sum(KEYS)
        assert NPC % 2 == 0 and NK % 2 == 0
        FREE = 2 * NC

        Q = [sb(f"Qs{b}", [P, NP], F32R) for b in range(2)]
        K_hi = [sb(f"K_hi{b}", [P, NP], F32R) for b in range(2)]
        QM = [sb(f"queries_maxima{b}", [P, NP], F32R) for b in range(2)]
        K_lo = [sb(f"K_lo{b}", [P, NP], F32R) for b in range(2)]
        Vs = [sb(f"Vs{b}", [P, NT, P]) for b in range(2)]
        width = [max(len(tiles) for tiles in CHUNKS if k <= tiles[-1]) * P for k in range(NT)]
        PT = [[sb(f"PT{i}_{k}", [P, width[k]]) for k in range(NT)] for i in range(2)]
        sum_rows = sb("sum_rows", [P, NP])
        ident_b = sb("ident_b", [P, P], BF16)
        mask_q = sb("mask_q", [P, P], BF16)
        mask_k = sb("mask_k", [P, P], BF16)
        blocks = sb("blocks", [2 * CQ, CQ, P])
        part = sb("part_max", [P, 2])
        neg_max = sb("neg_max", [P, CQ])
        max_parts = sb("max_parts", [P, 2 * CQ], F32R)

        masks_cleared, masks_ready = sem("masks_cleared"), sem("masks_ready")
        hi_staged, lo_staged, staged = sem("hi_staged"), sem("lo_staged"), sem("staged")
        scores_ready, maxed, max_split, max_transposed, max_ready = (
            sem("scores_ready"), sem("maxed"), sem("max_split"), sem("max_transposed"), sem("max_ready"))
        keyed, weighed, attended, o_read, own = (
            sem("keyed"), sem("exp_done"), sem("attended"), sem("o_read"), sem("attend_vector_own"))
        sums_free, others_cleared = sem("sums_free"), sem("others_cleared")
        v_staged, sums_stored, sums_compact = sem("v_staged"), sem("sums_stored"), sem("sums_compact")

        region = [psum[:, n * REGION:(n + 1) * REGION] for n in range(2)]
        psK = [psum[:, (4 + n) * 512:(5 + n) * 512] for n in range(2)]
        psO = psum[:, 6 * 512:7 * 512]
        psM = psum[:, 7 * 512:8 * 512]

        def head(j, b):
            return 2 * j + b

        def chunk(j, b, c):
            return NC * head(j, b) + c

        def slots(j, last):
            for b in range(2):
                for c in range(NC):
                    if c + 1 < NC:
                        after = (j, b, c + 1)
                    elif b == 0:
                        after = (j, 1, 0)
                    else:
                        after = None if last else (j + 1, 0, 0)
                    yield b, c, after

        def in_turn(eng, slot):
            def pair(j, last):
                for b, c, after in slots(j, last):
                    slot(j, b, c, after, last)

            with eng.Fori(0, H // 2 - 1) as j:
                pair(j, False)
            pair(H // 2 - 1, True)

        def next_head(j, b, c, last, when):
            if c != when or (last and b == 1):
                return None
            return (j, 1) if b == 0 else (j + 1, 0)

        def halves(b):
            own_rows, other_rows = slice(b * DH, (b + 1) * DH), slice((1 - b) * DH, (2 - b) * DH)
            return own_rows, other_rows

        with nc.Block() as block:
            @block.sync
            def _(sp):
                sp.dma_start(Wo_raw[:, :, :], Wo.rearrange("(c p) n -> p c n", p=P)).then_inc(wo_loaded, 16)
                with sp.Fori(0, H // 2) as j:
                    for b in range(2):
                        row = (1 - b) * DH
                        sp.wait_ge(o_read, NC * head(j, b) + NC + 1)
                        sp.dma_start(sums_row[b:b + 1, bass.ds(j * NP, NP)], sum_rows[row:row + 1, :]).then_inc(sums_stored, 16)
                        sp.wait_ge(sums_stored, 16 * (head(j, b) + 1))
                        sp.sem_inc(sums_free, 1)
                sp.dma_start(weight_sums[:, :, :], sums_row.rearrange("b (p k) -> p b k", k=SPREAD)).then_inc(sums_compact, 16)
                sp.wait_ge(sums_compact, 16)
                sp.wait_ge(wo_loaded, 16)

            @block.gpsimd
            def _(pool):
                nc.gpsimd.memset(mask_q[:, :], 0.0)
                nc.gpsimd.memset(mask_k[:, :], 0.0)
                nc.gpsimd.memset(max_parts[:, :].bitcast(F32), 0.0)
                nc.gpsimd.tensor_copy(ident_b[:, :], ident[:, :])
                for b in range(2):
                    nc.gpsimd.memset(Vs[b][:, :, (1 - b) * DH:(2 - b) * DH], 1.0)
                nc.gpsimd.memset(blocks[:, :, :], 0.0).then_inc(masks_cleared, 1)
                pool.wait_ge(masks_cleared, 1)
                nc.gpsimd.affine_select(out=mask_q[:, :], in_=mask_q[:, :], compare_op=ALU.is_ge, fill=MASKED,
                                        base=0, pattern=[[-1, P]], channel_multiplier=1)
                nc.gpsimd.affine_select(out=mask_k[:, :], in_=mask_k[:, :], compare_op=ALU.is_ge, fill=MASKED,
                                        base=0, pattern=[[1, P]], channel_multiplier=-1)
                nc.gpsimd.affine_select(out=blocks[:, :, :], in_=blocks[:, :, :], compare_op=ALU.not_equal, fill=1.0,
                                        base=0, pattern=[[-1, CQ], [0, P]], channel_multiplier=1).then_inc(masks_cleared, 1)
                pool.wait_ge(masks_cleared, 2)
                nc.gpsimd.affine_select(out=blocks[:, :, :], in_=blocks[:, :, :], compare_op=ALU.not_equal, fill=1.0,
                                        base=-CQ, pattern=[[-1, CQ], [0, P]], channel_multiplier=1).then_inc(masks_ready, 1)

                def stage(j, b):
                    rows, _ = halves(b)
                    queries = QT[rows, bass.ds(j, 1), :].rearrange("p o n -> p (o n)")
                    pool.wait_ge(attended, NC * (head(j, b) - 1) + FREE)
                    if not (isinstance(j, int) and head(j, b) == 0):
                        pool.wait_ge(staged, head(j, b))
                    nc.gpsimd.tensor_copy(Vs[b][:, :, b * DH:(b + 1) * DH], V[:, :, bass.ds(head(j, b) * DH, DH)]).then_inc(v_staged, 1)
                    pool.wait_ge(v_staged, head(j, b) + 1)
                    nc.gpsimd.tensor_copy(QM[b][rows, :], queries).then_inc(staged, 1)

                pool.wait_ge(masks_ready, 1)
                stage(0, 0)

                def slot(j, b, c, after, last):
                    if nxt := next_head(j, b, c, last, 0):
                        stage(*nxt)

                in_turn(pool, slot)

            @block.scalar
            def _(act):
                act.sem_inc(weighed, 2)
                act.sem_inc(sums_free, 2)
                act.sem_inc(o_read, 1)

                def stage(j, b):
                    rows, others = halves(b)
                    chunk_j = bass.ds(j, 1)
                    act.wait_ge(attended, NC * (head(j, b) - 1) + FREE)
                    nc.scalar.activation(Q[b][rows, :], QT[rows, chunk_j, :].rearrange("p o n -> p (o n)"), ACT.Copy)
                    nc.scalar.activation(K_hi[b][others, :], KT[rows, chunk_j, :].rearrange("p o n -> p (o n)"), ACT.Copy)
                    nc.scalar.activation(K_hi[b][rows, :], KT[rows, chunk_j, :].rearrange("p o n -> p (o n)"), ACT.Copy).then_inc(hi_staged, 1)

                stage(0, 0)

                def slot(j, b, c, after, last):
                    act.wait_ge(attended, chunk(j, b, c) - 1 + FREE)
                    for kt in range(KEYS[c]):
                        n = NK * head(j, b) + sum(KEYS[:c]) + kt
                        lo = max(kt - CHUNKS[c][0], 0) * P
                        hi = len(CHUNKS[c]) * P
                        act.wait_ge(keyed, n + 1)
                        nc.scalar.activation(PT[(NC * b + c) % 2][kt][:, lo:hi], psK[kt_bank(b, c, kt)][:, lo:hi],
                                             ACT.Exp).then_inc(weighed, 1)
                    if nxt := next_head(j, b, c, last, 0):
                        stage(*nxt)
                    n = len(CHUNKS[c]) * P
                    rows, others = halves(b)
                    q0 = CHUNKS[c][0] * P
                    act.wait_ge(attended, chunk(j, b, c) + 1 + FREE)
                    if c == 0:
                        act.wait_ge(sums_free, head(j, b) + 1)
                    nc.scalar.activation(OT[rows, bass.ds(j, 1), q0:q0 + n].rearrange("p o n -> p (o n)"), psO[rows, 0:n], ACT.Copy)
                    one = slice(others.start, others.start + 1)
                    nc.scalar.activation(sum_rows[one, q0:q0 + n], psO[one, 0:n],
                                         ACT.Copy).then_inc(o_read, 1)

                def kt_bank(b, c, kt):
                    return (sum(KEYS[:c]) + kt) % 2

                in_turn(act, slot)

            @block.vector
            def _(dve):
                def stage(j, b):
                    rows, others = halves(b)
                    c = bass.ds(j, 1)
                    dve.wait_ge(hi_staged, head(j, b) + 1)
                    nc.vector.tensor_tensor(Q[b][others, :], QT[rows, c, :].rearrange("p o n -> p (o n)"),
                                            Q[b][rows, :].bitcast(F32), ALU.subtract)
                    nc.vector.tensor_tensor(K_lo[b][rows, :], KT[rows, c, :].rearrange("p o n -> p (o n)"),
                                            K_hi[b][rows, :].bitcast(F32), ALU.subtract).then_inc(lo_staged, 1)

                def maxima(j, b, c):
                    step = Chain(dve, own, chunk(j, b, c) + head(j, b))
                    for s, (pc, i, k0, k1) in enumerate(PIECES):
                        if pc != c:
                            continue
                        dve.wait_ge(scores_ready, NPC * head(j, b) + s + 1)
                        whole = (i + 1) * P <= REGION
                        to = neg_max[:, i - CHUNKS[c][0]:i - CHUNKS[c][0] + 1] if whole or k0 == 0 else part[:, (i % 2):(i % 2) + 1]
                        nc.vector.tensor_reduce(to, region[s % 2][:, 0:k1 - k0], X_AXIS, ALU.max,
                                                negate=True).then_inc(maxed, 1)
                    dve.wait_ge(maxed, NPC * head(j, b) + sum(x[0] <= c for x in PIECES) + 2)
                    n = len(CHUNKS[c])
                    if c == NC - 1:
                        step(nc.vector.tensor_tensor(neg_max[:, 0:n], neg_max[:, 0:n], part[:, 0:n], ALU.min))
                    step(nc.vector.tensor_copy(max_parts[:, 0:n], neg_max[:, 0:n]))
                    nc.vector.tensor_tensor(max_parts[:, CQ:CQ + n], neg_max[:, 0:n], max_parts[:, 0:n].bitcast(F32),
                                            ALU.subtract).then_inc(max_split, 1)

                def max_row(j, b, c):
                    dve.wait_ge(max_transposed, chunk(j, b, c) + 1)
                    o = (1 - b) * DH
                    first, n = CHUNKS[c][0] * P, len(CHUNKS[c])
                    nc.vector.tensor_tensor(QM[b][o:o + 2 * CQ, first:first + n * P].rearrange("p (t n) -> p t n", n=P), psM[0:2 * CQ, 0:P].rearrange("p (o n) -> p o n", o=1).broadcast_to([2 * CQ, n, P]),
                                            blocks[:, 0:n, :], ALU.mult).then_inc(max_ready, 1)

                dve.sem_inc(maxed, 2)
                for b in range(2):
                    _, others = halves(b)
                    nc.vector.memset(QM[b][others, :].bitcast(F32), 0.0)
                    nc.vector.memset(K_lo[b][others, :].bitcast(F32), 0.0).then_inc(others_cleared, 1)
                dve.wait_ge(others_cleared, 2)
                for b in range(2):
                    o = (1 - b) * DH
                    nc.vector.memset(K_lo[b][o:o + 2 * CQ, :].bitcast(F32), 1.0)
                dve.wait_ge(masks_ready, 1)
                stage(0, 0)
                maxima(0, 0, 0)
                max_row(0, 0, 0)

                def slot(j, b, c, after, last):
                    if nxt := next_head(j, b, c, last, 1):
                        stage(*nxt)
                    if after:
                        maxima(*after)
                        max_row(*after)
                in_turn(dve, slot)

            @block.tensor
            def _(pe):
                pe.sem_inc(attended, FREE)
                pe.wait_ge(masks_ready, 1)

                def score(j, b, s):
                    c, i, k0, k1 = PIECES[s]
                    if s == 0:
                        pe.wait_ge(lo_staged, head(j, b) + 1)
                    pe.wait_ge(maxed, NPC * head(j, b) + s + 1)
                    q = Q[b][:, i * P:(i + 1) * P]
                    rows, _ = halves(b)
                    for a in range(k0, k1, 512):
                        e = min(a + 512, k1)
                        out = region[s % 2][:, a - k0:e - k0]
                        diagonal = e == (i + 1) * P
                        nc.tensor.matmul(out, q, K_hi[b][:, a:e], start=True, stop=False)
                        last = nc.tensor.matmul(out, Q[b][rows, i * P:(i + 1) * P], K_lo[b][rows, a:e], start=False, stop=not diagonal)
                        if diagonal:
                            last = nc.tensor.matmul(region[s % 2][:, e - P - k0:e - k0], ident_b[:, :], mask_q[:, :],
                                                    start=False, stop=True)
                    last.then_inc(scores_ready, 1)

                def pieces(c):
                    return [s for s, piece in enumerate(PIECES) if piece[0] == c]

                def turn_maxima(j, b, c):
                    pe.wait_ge(max_split, chunk(j, b, c) + 1)
                    nc.tensor.transpose(psM[0:2 * CQ, 0:P], max_parts[:, :].bitcast(F32), ident[:, :]).then_inc(max_transposed, 1)

                for s in pieces(0):
                    score(0, 0, s)
                turn_maxima(0, 0, 0)

                def slot(j, b, c, after, last):
                    to_do = pieces(after[2]) if after else []
                    if c == 0:
                        pe.wait_ge(staged, head(j, b) + 1)
                    pe.wait_ge(max_ready, chunk(j, b, c) + 1)
                    first = CHUNKS[c][0]
                    hi = len(CHUNKS[c]) * P
                    for kt in range(KEYS[c]):
                        n = NK * head(j, b) + sum(KEYS[:c]) + kt
                        lo = max(kt - first, 0) * P
                        pe.wait_ge(weighed, n + 1)
                        out = psK[(sum(KEYS[:c]) + kt) % 2]
                        q = Q[b][:, first * P + lo:first * P + hi]
                        nc.tensor.matmul(out[:, lo:hi], K_hi[b][:, kt * P:(kt + 1) * P], q, start=True, stop=False)
                        if kt >= first:
                            nc.tensor.matmul(out[:, lo:lo + P], ident_b[:, :], mask_k[:, :], start=False, stop=False)
                        nc.tensor.matmul(out[:, lo:hi], K_lo[b][:, kt * P:(kt + 1) * P], QM[b][:, first * P + lo:first * P + hi],
                                         start=False, stop=True).then_inc(keyed, 1)
                        for s in to_do[len(to_do) * kt // (KEYS[c] - 1):len(to_do) * (kt + 1) // (KEYS[c] - 1)]:
                            score(after[0], after[1], s)
                    pe.wait_ge(o_read, chunk(j, b, c) + 1)
                    for kt in range(KEYS[c]):
                        if after and kt == KEYS[c] - 3:
                            turn_maxima(*after)
                        lo = max(kt - first, 0) * P
                        pe.wait_ge(weighed, NK * head(j, b) + sum(KEYS[:c]) + kt + 1 + 2)
                        last = nc.tensor.matmul(psO[:, lo:hi], Vs[b][:, kt, :], PT[(NC * b + c) % 2][kt][:, lo:hi],
                                                start=(kt == 0), stop=(kt == KEYS[c] - 1))
                    last.then_inc(attended, 1)

                in_turn(pe, slot)


def combine_heads(nc, sem, carrier, psum, bank, OT, weight_sums, inverse_row, yT, logits, raw, parts, weights_loaded, weights_hi, weights_lo,
                  Wo_raw, wo_loaded, gate_W, gate_b, W1, W2):
    ctx = ExitStack()
    with ctx:
        def sb(name, shape, dt=F32):
            return ctx.enter_context(nc.sbuf_tensor(name, shape, dt))

        STEP = 2 * P
        NS = NP // STEP
        Wo_hi, Wo_lo = sb("Wo_hi", [P, KC, D], F32R), sb("Wo_lo", [P, KC, D], F32R)
        OT_hi, OT_lo = sb("OT_hi", [P, KC, NP], F32R), sb("OT_lo", [P, KC, NP], F32R)
        inverse_rows = sb("inverse_rows", [H, NP])
        select = sb("select_head", [H, KC, P])
        gW = sb("gate_weights", [P, KC, H])
        gW_hi, gW_lo = sb("gate_hi", [P, KC, H], F32R), sb("gate_lo", [P, KC, H], F32R)
        gb_col = sb("gate_bias", [H, 1])

        gate_loaded = sem("gate_loaded")
        wo_hi_ready, wo_lo_ready = sem("wo_hi_ready"), sem("wo_lo_ready")
        gate_hi_ready, gate_lo_ready = sem("gate_hi_ready"), sem("gate_lo_ready")
        inverse_ready, rows_ready = sem("inverse_ready"), sem("inverse_rows_ready")
        selecting, select_ready = sem("selecting"), sem("select_ready")
        inverse_stored = sem("inverse_stored")
        spread, divided = sem("inverse_spread"), sem("o_divided")
        ot_hi_ready, ot_lo_ready = sem("ot_hi_ready"), sem("ot_lo_ready")
        y_made, y_hi_ready, y_lo_ready = sem("y_made"), sem("y_hi_ready"), sem("y_lo_ready")
        logits_made, logits_read = sem("logits_made"), sem("logits_read")

        psI = psum[:, 0:KC * STEP].rearrange("p (c n) -> p c n", c=KC)
        psY, psL = bank[2:6], bank[6]
        yT_hi, yT_lo = yT

        def in_steps(eng, part, product, gate, between=lambda: None):
            part(0)
            part(1)
            product(0)
            between()
            with eng.Fori(1, NS - 1) as n:
                part(n + 1)
                product(n)
                gate(n - 1)
            product(NS - 1)
            gate(NS - 2)
            gate(NS - 1)

        with nc.Block() as block:
            @block.sync
            def _(sp):
                sp.dma_start(gW[:, :, :], gate_W.rearrange("(c p) n -> p c n", p=P)).then_inc(gate_loaded, 16)
                sp.dma_start(gb_col[:, :], gate_b.rearrange("(p o) -> p o", o=1)).then_inc(gate_loaded, 16)
                sp.wait_ge(inverse_ready, 1)
                sp.dma_start(inverse_row.rearrange("b (p k) -> p b k", k=SPREAD), weight_sums[:, :, :]).then_inc(inverse_stored, 16)
                sp.wait_ge(inverse_stored, 16)
                sp.dma_start(inverse_rows[:, :], inverse_row.rearrange("b (j n) -> (b j) n", n=NP)).then_inc(rows_ready, 16)
                for e in range(2):
                    for w, source in enumerate((W1, W2)):
                        sp.dma_start(raw[w][e][:, :, :], source[e].rearrange("(c p) n -> p c n", p=P)).then_inc(weights_loaded[e], 16)

            @block.gpsimd
            def _(pool):
                step = Chain(pool, selecting)
                step(nc.gpsimd.memset(select[:, :, :], 0.0))
                for b in range(2):
                    half = select[:, :, b * DH:(b + 1) * DH]
                    nc.gpsimd.affine_select(out=half, in_=half, compare_op=ALU.not_equal, fill=1.0, base=-b * KC,
                                            pattern=[[-1, KC], [0, DH]], channel_multiplier=1).then_inc(select_ready, 1)
                for w in range(2):
                    pool.wait_ge(weights_hi, w + 1)
                    nc.gpsimd.tensor_tensor(parts[w][0][1][:, :, :], raw[w][0][:, :, :], parts[w][0][0][:, :, :].bitcast(F32),
                                            ALU.subtract).then_inc(weights_lo, 1)

            @block.scalar
            def _(act):
                act.wait_ge(wo_loaded, 16)
                nc.scalar.activation(Wo_hi[:, :, :], Wo_raw[:, :, :], ACT.Copy).then_inc(wo_hi_ready, 1)
                act.wait_ge(gate_loaded, 32)
                nc.scalar.activation(gW_hi[:, :, :], gW[:, :, :], ACT.Copy).then_inc(gate_hi_ready, 1)

                def part(n):
                    cols = bass.ds(n * STEP, STEP)
                    act.wait_ge(divided, n + 1)
                    nc.scalar.activation(OT_hi[:, :, cols], OT[:, :, cols], ACT.Copy).then_inc(ot_hi_ready, 1)

                def product(n):
                    for m in range(KC):
                        act.wait_ge(y_made, KC * n + m + 1)
                        nc.scalar.activation(yT_hi[:, m, bass.ds(n * STEP, STEP)], psY[m][:, 0:STEP], ACT.Copy).then_inc(y_hi_ready, 1)

                def gate(n):
                    act.wait_ge(logits_made, n + 1)
                    act.sem_inc(carrier, 1)
                    nc.scalar.activation(logits[:, bass.ds(n * STEP, STEP)], psL[0:H, 0:STEP], ACT.Identity,
                                         bias=gb_col[:, 0:1]).then_inc(logits_read, 1)

                def first_weights():
                    act.wait_ge(weights_loaded[0], 32)
                    for w in range(2):
                        nc.scalar.activation(parts[w][0][0][:, :, :], raw[w][0][:, :, :], ACT.Copy).then_inc(weights_hi, 1)

                in_steps(act, part, product, gate, first_weights)

            @block.vector
            def _(dve):
                nc.vector.reciprocal(weight_sums[:, :, :], weight_sums[:, :, :]).then_inc(inverse_ready, 1)
                dve.wait_ge(wo_hi_ready, 1)
                nc.vector.tensor_tensor(Wo_lo[:, :, :], Wo_raw[:, :, :], Wo_hi[:, :, :].bitcast(F32),
                                        ALU.subtract).then_inc(wo_lo_ready, 1)
                dve.wait_ge(gate_hi_ready, 1)
                nc.vector.tensor_tensor(gW_lo[:, :, :], gW[:, :, :], gW_hi[:, :, :].bitcast(F32), ALU.subtract).then_inc(gate_lo_ready, 1)

                def part(n):
                    cols = bass.ds(n * STEP, STEP)
                    dve.wait_ge(spread, n + 1)
                    nc.vector.tensor_tensor(OT[:, :, cols], psI, OT[:, :, cols], ALU.mult).then_inc(divided, 1)
                    dve.wait_ge(ot_hi_ready, n + 1)
                    nc.vector.tensor_tensor(OT_lo[:, :, cols], OT[:, :, cols], OT_hi[:, :, cols].bitcast(F32),
                                            ALU.subtract).then_inc(ot_lo_ready, 1)

                def product(n):
                    for m in range(KC):
                        dve.wait_ge(y_hi_ready, KC * n + m + 1)
                        cols = bass.ds(n * STEP, STEP)
                        nc.vector.tensor_tensor(yT_lo[:, m, cols], psY[m][:, 0:STEP], yT_hi[:, m, cols].bitcast(F32),
                                                ALU.subtract).then_inc(y_lo_ready, 1)

                in_steps(dve, part, product, lambda n: None)

            @block.tensor
            def _(pe):
                pe.sem_inc(y_lo_ready, KC)
                pe.sem_inc(logits_read, 1)

                def part(n):
                    if not (isinstance(n, int) and n == 0):
                        pe.wait_ge(divided, n)
                    for c in range(KC):
                        last = nc.tensor.matmul(psI[:, c, :], select[:, c, :], inverse_rows[:, bass.ds(n * STEP, STEP)],
                                                start=True, stop=True)
                    last.then_inc(spread, 1)

                def product(n):
                    if isinstance(n, int) and n == 0:
                        pe.wait_ge(wo_lo_ready, 1)
                    pe.wait_ge(ot_lo_ready, n + 1)
                    cols = bass.ds(n * STEP, STEP)
                    for m in range(KC):
                        pe.wait_ge(y_lo_ready, KC * n + m + 1)
                        for i, (w, o) in enumerate(((Wo_hi, OT_hi), (Wo_lo, OT_hi), (Wo_hi, OT_lo))):
                            for c in range(KC):
                                last = nc.tensor.matmul(psY[m][:, 0:STEP], w[:, c, m * P:(m + 1) * P], o[:, c, cols],
                                                        start=(i == 0 and c == 0), stop=(i == 2 and c == KC - 1))
                        last.then_inc(y_made, 1)

                def gate(n):
                    pe.wait_ge(logits_read, n + 1)
                    pe.wait_ge(y_lo_ready, KC * n + 2 * KC)
                    cols = bass.ds(n * STEP, STEP)
                    for i, (w, y) in enumerate(((gW_hi, yT_hi), (gW_lo, yT_hi), (gW_hi, yT_lo))):
                        for c in range(KC):
                            last = nc.tensor.matmul(psL[0:H, 0:STEP], w[:, c, :], y[:, c, cols],
                                                    start=(i == 0 and c == 0), stop=(i == 2 and c == KC - 1))
                    last.then_inc(logits_made, 1)

                pe.wait_ge(gate_lo_ready, 1)
                pe.wait_ge(select_ready, 2)
                pe.wait_ge(rows_ready, 16)
                in_steps(pe, part, product, gate)


def run_experts(nc, sem, carrier, bank, ident, X, yT, logits, raw, parts, weights_loaded, weights_hi, weights_lo,
                W1, b1, W2, b2, out):
    ctx = ExitStack()
    with ctx:
        def sb(name, shape, dt=F32):
            return ctx.enter_context(nc.sbuf_tensor(name, shape, dt))

        NE, F = W1.shape[0], W1.shape[2]
        FC = F // P
        SPANS = [(a, min(a + 512, NP)) for a in range(0, NP, 512)]
        NSP = len(SPANS)
        NB = 3
        NO = 5
        assert (NSP * FC) % NB == 0 and NT % NO == 0 and NB + NO == 8 and NE == H

        parts = [parts[w] + [[sb(f"expert_hi{w}", [P, c, n], F32R), sb(f"expert_lo{w}", [P, c, n], F32R)]]
                 for w, (c, n) in enumerate(((KC, F), (FC, D)))]
        hid = [sb(f"hid{s}", [P, FC, 512]) for s in range(NSP)]
        hid_hi, hid_lo = sb("hid_hi", [P, FC, NP], F32R), sb("hid_lo", [P, FC, NP], F32R)
        b1_col = sb("b1_col", [P, NE * FC])
        b2_rows = sb("b2_rows", [NE, D])
        gates = sb("gates", [P, NT, NE])
        reduced = sb("gate_reduced", [P, NT])
        gatesT = sb("gatesT", [NE, NP])

        biases_loaded = sem("biases_loaded")
        logits_turned, gates_ready, gates_turned, gatesT_ready = (sem("logits_turned"), sem("gates_ready"),
                                                                  sem("gates_turned"), sem("gatesT_ready"))
        own, shifted, exps_ready = sem("expert_vector_own"), sem("gates_shifted"), sem("gates_exps")
        hid_made, gelu_done, hid_hi_ready, hid_lo_ready = (sem("hid_made"), sem("gelu_done"), sem("hid_hi_ready"),
                                                           sem("hid_lo_ready"))
        out_stored = sem("out_stored")
        expert_made, mixed = sem("expert_made"), sem("mixed")

        psH, psE, psG = bank[0:NB], bank[NB:], bank[7]
        yT_hi, yT_lo = yT

        def in_pairs(eng, step):
            with eng.Fori(0, NE // 2 - 1) as j:
                for b in range(2):
                    step(2 * j + b, b, True, True)
            step(NE - 2, 0, True, False)
            step(NE - 1, 1, False, False)

        with nc.Block() as block:
            @block.sync
            def _(sp):
                sp.dma_start(b1_col[:, :], b1.rearrange("e (f p) -> p (e f)", p=P),
                             allow_slow_non_contiguous=True).then_inc(biases_loaded, 16)
                sp.dma_start(b2_rows[:, :], b2).then_inc(biases_loaded, 16)

                def step(e, b, more_hidden, more_weights):
                    if more_weights:
                        sp.wait_ge(weights_lo, 2 * e + 2)
                        for w, source in enumerate((W1, W2)):
                            sp.dma_start(raw[w][b][:, :, :],
                                         source[bass.ds(e + 2, 1)].rearrange("o (c p) n -> p (o c) n", p=P)).then_inc(weights_loaded[b], 16)

                in_pairs(sp, step)
                for t0 in range(0, NT, 2):
                    sp.wait_ge(mixed, NT * NE + t0 + 2)
                    if (t0 + 2) * P <= N:
                        sp.dma_start(out[t0 * P:(t0 + 2) * P, :].rearrange("(t p) d -> p t d", p=P), X[:, t0:t0 + 2, :]).then_inc(out_stored, 16)
                    else:
                        sp.dma_start(out[t0 * P:(t0 + 1) * P, :], X[:, t0, :]).then_inc(out_stored, 16)
                        sp.dma_start(out[(t0 + 1) * P:N, :], X[0:N - (t0 + 1) * P, t0 + 1, :]).then_inc(out_stored, 16)
                sp.wait_ge(out_stored, 16 * (NT // 2 + 1))

            @block.gpsimd
            def _(pool):
                def weights(e, b):
                    for w in range(2):
                        pool.wait_ge(weights_hi, 2 * e + w + 1)
                        nc.gpsimd.tensor_tensor(parts[w][b][1][:, :, :], raw[w][b][:, :, :], parts[w][b][0][:, :, :].bitcast(F32),
                                                ALU.subtract).then_inc(weights_lo, 1)

                def hidden(e):
                    for s, (n0, n1) in enumerate(SPANS):
                        pool.wait_ge(hid_hi_ready, NSP * e + s + 1)
                        nc.gpsimd.tensor_tensor(hid_lo[:, :, n0:n1], hid[s][:, :, 0:n1 - n0], hid_hi[:, :, n0:n1].bitcast(F32),
                                                ALU.subtract).then_inc(hid_lo_ready, 1)

                weights(1, 1)
                hidden(0)

                def step(e, b, more_hidden, more_weights):
                    if more_hidden:
                        hidden(e + 1)
                    if more_weights:
                        weights(e + 2, b)

                in_pairs(pool, step)

            @block.scalar
            def _(act):
                act.sem_inc(hid_lo_ready, NSP)
                act.sem_inc(gelu_done, NB)

                def weights(e, b, j):
                    act.wait_ge(weights_loaded[b], 32 * (j + 1))
                    for w in range(2):
                        nc.scalar.activation(parts[w][b][0][:, :, :], raw[w][b][:, :, :], ACT.Copy).then_inc(weights_hi, 1)

                def hidden(e):
                    for s, (n0, n1) in enumerate(SPANS):
                        act.wait_ge(hid_lo_ready, NSP * e + s + 1)
                        for f in range(FC):
                            act.wait_ge(hid_made, NSP * FC * e + FC * s + f + 1)
                            act.sem_inc(carrier, 1)
                            nc.scalar.activation(hid[s][:, f, 0:n1 - n0], psH[(FC * s + f) % NB][:, 0:n1 - n0], ACT.Gelu_apprx_tanh,
                                                 bias=b1_col[:, bass.ds(FC * e + f, 1)]).then_inc(gelu_done, 1)
                        act.wait_ge(gelu_done, NSP * FC * e + FC * s + FC + NB)
                        nc.scalar.activation(hid_hi[:, :, n0:n1], hid[s][:, :, 0:n1 - n0], ACT.Copy).then_inc(hid_hi_ready, 1)

                weights(1, 1, 0)
                act.wait_ge(shifted, 1)
                nc.scalar.activation(gates[:, :, :], gates[:, :, :], ACT.Exp).then_inc(exps_ready, 1)
                act.wait_ge(biases_loaded, 32)
                hidden(0)

                with act.Fori(0, NE // 2 - 1) as j:
                    for b in range(2):
                        hidden(2 * j + b + 1)
                        weights(2 * j + b + 2, b, j + 1)
                hidden(NE - 1)

            @block.vector
            def _(dve):
                step = Chain(dve, own)
                wide = lambda a: a[:, :].rearrange("p (t o) -> p t o", o=1).broadcast_to([P, NT, NE])
                turned = psG[:, 0:NT * NE].rearrange("p (t e) -> p t e", e=NE)
                dve.wait_ge(logits_turned, 1)
                step(nc.vector.tensor_reduce(reduced[:, :], turned, X_AXIS, ALU.max))
                nc.vector.tensor_tensor(gates[:, :, :], turned, wide(reduced), ALU.subtract).then_inc(shifted, 1)
                dve.wait_ge(exps_ready, 1)
                step(nc.vector.tensor_reduce(reduced[:, :], gates[:, :, :], X_AXIS, ALU.add))
                step(nc.vector.reciprocal(reduced[:, :], reduced[:, :]))
                nc.vector.tensor_tensor(gates[:, :, :], gates[:, :, :], wide(reduced), ALU.mult).then_inc(gates_ready, 1)
                dve.wait_ge(gates_ready, 1)
                for s, (n0, n1) in enumerate(SPANS):
                    dve.wait_ge(gates_turned, s + 1)
                    nc.vector.tensor_copy(gatesT[:, n0:n1], psE[s][0:NE, 0:n1 - n0]).then_inc(gatesT_ready, 1)
                for t in range(NT):
                    dve.wait_ge(expert_made, t + 1)
                    nc.vector.tensor_tensor(X[:, t, :], psE[t % NO][:, :], X[:, t, :], ALU.add).then_inc(mixed, 1)

                def mix(e, b, more_hidden, more_weights):
                    for t in range(NT):
                        dve.wait_ge(expert_made, NT * (e + 1) + t + 1)
                        dve.wait_ge(mixed, NT * e + t + 1)
                        nc.vector.scalar_tensor_tensor(X[:, t, :], psE[t % NO][:, :], gates[:, t, bass.ds(e, 1)], X[:, t, :],
                                                       ALU.mult, ALU.add).then_inc(mixed, 1)

                in_pairs(dve, mix)

            @block.tensor
            def _(pe):
                for t in range(NT):
                    last = nc.tensor.transpose(psG[:, t * NE:(t + 1) * NE], logits[:, t * P:(t + 1) * P], ident[0:NE, 0:NE])
                last.then_inc(logits_turned, 1)

                def hidden(e, b):
                    pe.wait_ge(weights_lo, 2 * e + 1)
                    for s, (n0, n1) in enumerate(SPANS):
                        for f in range(FC):
                            pe.wait_ge(gelu_done, NSP * FC * e + FC * s + f + 1)
                            w_hi, w_lo = parts[0][b]
                            for i, (w, y) in enumerate(((w_hi, yT_hi), (w_lo, yT_hi), (w_hi, yT_lo))):
                                for c in range(KC):
                                    last = nc.tensor.matmul(psH[(FC * s + f) % NB][:, 0:n1 - n0], w[:, c, f * P:(f + 1) * P],
                                                            y[:, c, n0:n1], start=(i == 0 and c == 0), stop=(i == 2 and c == KC - 1))
                            last.then_inc(hid_made, 1)

                def result(e, b):
                    pe.wait_ge(weights_lo, 2 * e + 2)
                    for t in range(NT):
                        pe.wait_ge(hid_lo_ready, NSP * e + t * P // 512 + 1 + NSP)
                        pe.wait_ge(mixed, NT * (e + 1) + t + 1 - NO)
                        w_hi, w_lo = parts[1][b]
                        rows = slice(t * P, (t + 1) * P)
                        for i, (h, w) in enumerate(((hid_hi, w_hi), (hid_hi, w_lo), (hid_lo, w_hi))):
                            for f in range(FC):
                                last = nc.tensor.matmul(psE[t % NO][:, :], h[:, f, rows], w[:, f, :],
                                                        start=(i == 0 and f == 0), stop=(i == 2 and f == FC - 1))
                        last.then_inc(expert_made, 1)

                hidden(0, 0)
                pe.wait_ge(gates_ready, 1)
                for s, (n0, n1) in enumerate(SPANS):
                    for t in range(n0 // P, n1 // P):
                        last = nc.tensor.transpose(psE[s][0:NE, t * P - n0:(t + 1) * P - n0], gates[:, t, :], ident[:, :])
                    last.then_inc(gates_turned, 1)
                pe.wait_ge(biases_loaded, 32)
                pe.wait_ge(gatesT_ready, NSP)
                for t in range(NT):
                    if t >= NO:
                        pe.wait_ge(mixed, t + 1 - NO)
                    nc.tensor.matmul(psE[t % NO][:, :], gatesT[:, t * P:(t + 1) * P], b2_rows[:, :],
                                     start=True, stop=True).then_inc(expert_made, 1)

                def step(e, b, more_hidden, more_weights):
                    result(e, b)
                    if more_hidden:
                        hidden(e + 1, 1 - b)

                in_pairs(pe, step)


_INS = ['x', 'src', 'dst', 'L0_gnn_Ws', 'L0_gnn_Wb', 'L0_gnn_a_w', 'L0_gnn_a_b', 'L0_ffn_ln_g', 'L0_ffn_ln_b',
        'L0_ffn_Wq', 'L0_ffn_Wk', 'L0_ffn_Wv', 'L0_ffn_Wo', 'L0_ffn_qn_g', 'L0_ffn_kn_g', 'L0_ffn_gate_W',
        'L0_ffn_gate_b', 'L0_ffn_W1', 'L0_ffn_b1', 'L0_ffn_W2', 'L0_ffn_b2']


def kernel(**inputs):
    import numpy as _np
    import concourse.bacc as _bacc
    from concourse import mybir as _mybir
    from concourse.bass_utils import run_bass_kernel_spmd as _run

    nc = _bacc.Bacc("TRN2", target_bir_lowering=False, num_devices=1)
    arrays, args = {}, []
    for name in _INS:
        a = _np.ascontiguousarray(inputs[name])
        arrays[f"in_{name}_dram"] = a
        args.append(nc.dram_tensor(f"in_{name}_dram", a.shape, _mybir.dt.from_np(a.dtype), kind="ExternalInput").ap())
    args.append(nc.dram_tensor("out_0_dram", (1250, 512), _mybir.dt.float32, kind="ExternalOutput").ap())
    build(nc, *args)
    r = _run(nc, [arrays], core_ids=[0])
    return r.results[0]["out_0_dram"]
```
